# Optimizing a Trainium2 kernel written in Bass

```python
import numpy as np
import jax
import jax.numpy as jnp

def _softmax(x, axis=-1):
    return jax.nn.softmax(x, axis=axis)

def _gelu(x):
    return jax.nn.gelu(x, approximate=True)

def _silu(x):
    return jax.nn.silu(x)

def _sigmoid(x):
    return jax.nn.sigmoid(x)

def _layernorm(x, axis=-1, eps=1e-05):
    m = jnp.mean(x, axis=axis, keepdims=True)
    v = jnp.var(x, axis=axis, keepdims=True)
    return (x - m) / jnp.sqrt(v + eps)

def _scatter_add(tgt, idx, src, axis=0):
    return tgt.at[idx].add(src)

def _segment_sum(src, seg, n):
    return jax.ops.segment_sum(src, seg, n)
kernel_name = 'mk_gnn_ffn_d4_gnn_r64_d198d8'

def setup_inputs(seed: int=0):
    np.random.seed(seed)
    _w = jnp.asarray

    def _rec_inputs():
        import jax
        import jax.numpy as jnp
        _gk = jax.random.key(seed)
        x = -0.0001538 + 1 * jax.random.normal(jax.random.fold_in(_gk, 1), (128, 768), jnp.float32)
        _s = jax.random.randint(jax.random.fold_in(_gk, 2), (2048,), 0, 128, jnp.int32)
        _d = jax.random.randint(jax.random.fold_in(_gk, 3), (2048,), 0, 128, jnp.int32)
        _loop = jnp.arange(128, dtype=jnp.int32)
        src = jnp.concatenate([_s, _d, _loop])
        dst = jnp.concatenate([_d, _s, _loop])
        _o = jnp.argsort(dst, stable=True)
        src = src[_o]
        dst = dst[_o]
        edge_weight = jax.random.uniform(jax.random.fold_in(_gk, 12), (4224,), jnp.float32, 0.0, 0.999998)
        return (x, src, dst, edge_weight)
    x, src, dst, edge_weight = _rec_inputs()

    def _L0_gnn_setup():
        import jax, jax.numpy as jnp
        import numpy as np
        NEG_SLOPE = 0.2
        EPS = 1e-16
        N_NODES = 128
        N_EDGES = 1024
        D_IN = 768
        D_HID = 768
        H1 = 8
        H2 = 1

        def gat_layer(x, W, a_s, a_d, b, edge_index, concat):
            n = x.shape[0]
            H, C = a_s.shape
            h = (x @ W).reshape(n, H, C)
            src, dst = (edge_index[0], edge_index[1])
            alpha_s = jnp.einsum('nhc,hc->nh', h, a_s)
            alpha_d = jnp.einsum('nhc,hc->nh', h, a_d)
            e = jax.nn.leaky_relu(alpha_s[src] + alpha_d[dst], NEG_SLOPE)
            m = jax.ops.segment_max(e, dst, num_segments=n)
            e = jnp.exp(e - m[dst])
            denom = jax.ops.segment_sum(e, dst, num_segments=n)
            alpha = e / (denom[dst] + EPS)
            msg = h[src] * alpha[:, :, None]
            out = jax.ops.segment_sum(msg, dst, num_segments=n)
            out = out.reshape(n, H * C) if concat else out.mean(axis=1)
            return out + b
        key = jax.random.key(seed)
        ks = jax.random.split(key, 10)
        x = jax.random.normal(ks[0], (N_NODES, D_IN), dtype=jnp.float32)
        edge_list = jax.random.randint(ks[1], (2, N_EDGES), 0, N_NODES, dtype=jnp.int32)
        s = 0.05
        W1 = jax.random.normal(ks[2], (D_IN, H1 * D_HID), dtype=jnp.float32) * s
        a_src1 = jax.random.normal(ks[3], (H1, D_HID), dtype=jnp.float32) * s
        a_dst1 = jax.random.normal(ks[4], (H1, D_HID), dtype=jnp.float32) * s
        b1 = jnp.zeros((H1 * D_HID,), dtype=jnp.float32)
        W2 = jax.random.normal(ks[5], (H1 * D_HID, H2 * D_HID), dtype=jnp.float32) * s
        a_src2 = jax.random.normal(ks[6], (H2, D_HID), dtype=jnp.float32) * s
        a_dst2 = jax.random.normal(ks[7], (H2, D_HID), dtype=jnp.float32) * s
        b2 = jnp.zeros((H2 * D_HID,), dtype=jnp.float32)
        return {'x': x, 'W1': W1, 'a_src1': a_src1, 'a_dst1': a_dst1, 'b1': b1, 'W2': W2, 'a_src2': a_src2, 'a_dst2': a_dst2, 'b2': b2, 'edge_list': edge_list}
    _L0_gnn_all = _L0_gnn_setup()
    _L0_gnn_in = {k: v for k, v in _L0_gnn_all.items() if k in ('W1', 'a_src1', 'a_dst1', 'b1', 'W2', 'a_src2', 'a_dst2', 'b2')}
    del _L0_gnn_all

    def _L0_ffn_setup():
        import jax, jax.numpy as jnp
        import numpy as np
        B, N, D, E, F, K = (2, 32, 768, 8, 48, 2)
        V_MAX = 3.0
        FEAT_CLAMP = 10.0

        def bk_green_diag(a):
            aT = jnp.swapaxes(a, 0, 1)

            def step(c, ai):
                d = ai - 1.0 / c
                return (d, d)
            d0 = aT[0]
            _, d_rest = jax.lax.scan(step, d0, aT[1:])
            d = jnp.concatenate([d0[None], d_rest], axis=0)
            eN = aT[-1]
            _, e_rest = jax.lax.scan(step, eN, aT[:-1], reverse=True)
            e = jnp.concatenate([e_rest, eN[None]], axis=0)
            G = 1.0 / (d + e - aT)
            return jnp.swapaxes(G, 0, 1)
        key = jax.random.key(seed)
        ks = jax.random.split(key, 8)
        s = lambda k, shape, sc: jax.random.normal(k, shape, jnp.float32) * sc
        return {'x': s(ks[0], (B, N, D), 1.0), 'v_w': s(ks[1], (D,), 0.02), 'v_b': jnp.zeros((), jnp.float32), 'gate_w': s(ks[2], (D, E), 0.02), 'gate_b': jnp.zeros((E,), jnp.float32), 'w1': s(ks[3], (E, D, F), 0.02), 'b1': jnp.zeros((E, F), jnp.float32), 'w2': s(ks[4], (E, F, D), 0.02), 'b2': jnp.zeros((E, D), jnp.float32), 'out_w': s(ks[5], (2, D), 0.02), 'out_b': jnp.zeros((D,), jnp.float32), 'bk_scale': jnp.ones((D,), jnp.float32)}
    _L0_ffn_all = _L0_ffn_setup()
    _L0_ffn_in = {k: v for k, v in _L0_ffn_all.items() if k in ('v_w', 'v_b', 'gate_w', 'gate_b', 'w1', 'b1', 'w2', 'b2', 'out_w', 'out_b', 'bk_scale')}
    del _L0_ffn_all

    def _L1_gnn_setup():
        import jax, jax.numpy as jnp
        import numpy as np
        N_NODES = 10000
        key = jax.random.key(seed)
        k1, k2, k3 = jax.random.split(key, 3)
        x = jax.random.normal(k1, (N_NODES, 768), dtype=jnp.float32)
        edge_index = jax.random.randint(k2, (2, 100000), 0, N_NODES, dtype=jnp.int32)
        W = jax.random.normal(k3, (768, 768), dtype=jnp.float32) * (1.0 / np.sqrt(768))
        b = jnp.zeros((768,), dtype=jnp.float32)
        return {'x': x, 'edge_index': edge_index, 'W': W, 'b': b}
    _L1_gnn_all = _L1_gnn_setup()
    _L1_gnn_in = {k: v for k, v in _L1_gnn_all.items() if k in ('W', 'b')}
    del _L1_gnn_all

    def _L1_ffn_setup():
        import jax, jax.numpy as jnp
        import numpy as np
        G, E = (4, 8)
        KG, KE = (2, 2)
        D, M = (768, 48)
        SCALE = 0.02

        def _combine_weights(xf, Wg, bg, Wge, bge):
            N = xf.shape[0]
            glog = xf @ Wg + bg
            gtop, gidx = jax.lax.top_k(glog, KG)
            ggate = jax.nn.softmax(gtop, axis=-1)
            elog_all = jnp.einsum('nd,gde->nge', xf, Wge) + bge
            elog = jnp.take_along_axis(elog_all, gidx[:, :, None], axis=1)
            etop, eidx = jax.lax.top_k(elog, KE)
            egate = jax.nn.softmax(etop, axis=-1)
            w = ggate[:, :, None] * egate
            flat = gidx[:, :, None] * E + eidx
            comb = jnp.zeros((N, G * E), xf.dtype).at[jnp.arange(N)[:, None, None], flat].add(w)
            return comb
        key = jax.random.key(seed)
        ks = jax.random.split(key, 8)
        x = jax.random.normal(ks[0], (1, 512, D), jnp.float32)
        Wg = jax.random.normal(ks[1], (D, G), jnp.float32) * SCALE
        bg = jnp.zeros((G,), jnp.float32)
        Wge = jax.random.normal(ks[2], (G, D, E), jnp.float32) * SCALE
        bge = jnp.zeros((G, E), jnp.float32)
        W1 = jax.random.normal(ks[3], (G * E, D, M), jnp.float32) * SCALE
        b1 = jnp.zeros((G * E, M), jnp.float32)
        W2 = jax.random.normal(ks[4], (G * E, M, D), jnp.float32) * SCALE
        b2 = jnp.zeros((G * E, D), jnp.float32)
        return {'x': x, 'Wg': Wg, 'bg': bg, 'Wge': Wge, 'bge': bge, 'W1': W1, 'b1': b1, 'W2': W2, 'b2': b2}
    _L1_ffn_all = _L1_ffn_setup()
    _L1_ffn_in = {k: v for k, v in _L1_ffn_all.items() if k in ('Wg', 'bg', 'Wge', 'bge', 'W1', 'b1', 'W2', 'b2')}
    del _L1_ffn_all

    def _L2_gnn_setup():
        import jax, jax.numpy as jnp
        import numpy as np
        N = 50000
        E = 500000
        D = 768
        H = 256
        R = 32

        def _gcn(x, W, b, row, col, ew):
            x = x @ W
            n = x.shape[0]
            deg = jax.ops.segment_sum(ew, col, num_segments=n) + 1.0
            dinv = jax.lax.rsqrt(deg)
            norm = dinv[row] * ew * dinv[col]
            agg = jax.ops.segment_sum(norm[:, None] * x[row], col, num_segments=n)
            return agg + (dinv * dinv)[:, None] * x + b
        key = jax.random.key(seed)
        ks = jax.random.split(key, 8)
        d = D // R
        w = lambda k, sh: jax.random.normal(k, sh, jnp.float32) * 0.05
        return {'x': jax.random.normal(ks[0], (N, D), jnp.float32), 'edge_index': jax.random.randint(ks[1], (2, E), 0, N), 'edge_weight': jax.random.uniform(ks[2], (E,), jnp.float32), 'Wd': w(ks[3], (D, d)), 'bd': jnp.zeros((d,), jnp.float32), 'Wu': w(ks[4], (d, D)), 'bu': jnp.zeros((D,), jnp.float32), 'W1': w(ks[5], (D, H)), 'b1': jnp.zeros((H,), jnp.float32), 'W2': w(ks[6], (H, D)), 'b2': jnp.zeros((D,), jnp.float32)}
    _L2_gnn_all = _L2_gnn_setup()
    _L2_gnn_in = {k: v for k, v in _L2_gnn_all.items() if k in ('Wd', 'bd', 'Wu', 'bu', 'W1', 'b1', 'W2', 'b2')}
    del _L2_gnn_all

    def _L2_ffn_setup():
        import jax, jax.numpy as jnp
        import numpy as np
        EPS_NORM = 1e-06
        EPS_Q = 1e-05

        def rmsnorm(x, g):
            return x * jax.lax.rsqrt(jnp.mean(x * x, axis=-1, keepdims=True) + EPS_NORM) * g

        def activation_quant(x):
            scale = 127.0 / jnp.maximum(jnp.max(jnp.abs(x), axis=-1, keepdims=True), EPS_Q)
            return jnp.clip(jnp.round(x * scale), -128, 127) / scale

        def weight_quant(w):
            scale = 1.0 / jnp.maximum(jnp.mean(jnp.abs(w)), EPS_Q)
            return jnp.clip(jnp.round(w * scale), -1, 1) / scale

        def bitlinear(x, w, g):
            x_norm = rmsnorm(x, g)
            x_q = x_norm + jax.lax.stop_gradient(activation_quant(x_norm) - x_norm)
            w_q = w + jax.lax.stop_gradient(weight_quant(w) - w)
            return jnp.einsum('bsd,od->bso', x_q, w_q)
        key = jax.random.key(seed)
        k1, k2, k3 = jax.random.split(key, 3)
        B, S, D, H = (8, 64, 768, 32)
        x = jax.random.normal(k1, (B, S, D), dtype=jnp.float32)
        w_in = jax.random.normal(k2, (2 * H, D), dtype=jnp.float32) * 0.002
        w_out = jax.random.normal(k3, (D, H), dtype=jnp.float32) * 0.002
        g_in = jnp.ones((D,), dtype=jnp.float32)
        g_out = jnp.ones((H,), dtype=jnp.float32)
        return {'x': x, 'w_in': w_in, 'g_in': g_in, 'w_out': w_out, 'g_out': g_out}
    _L2_ffn_all = _L2_ffn_setup()
    _L2_ffn_in = {k: v for k, v in _L2_ffn_all.items() if k in ('w_in', 'g_in', 'w_out', 'g_out')}
    del _L2_ffn_all

    def _L3_gnn_setup():
        import jax, jax.numpy as jnp
        import numpy as np
        N_NODES = 10000
        D = 768
        N_EDGES = 2500

        def gcn_conv(x, W, b, src, dst, n_nodes):
            h = x @ W
            deg = jax.ops.segment_sum(jnp.ones_like(dst, dtype=h.dtype), dst, num_segments=n_nodes)
            dinv = jnp.where(deg > 0, jax.lax.rsqrt(deg), 0.0)
            norm = dinv[src] * dinv[dst]
            msgs = h[src] * norm[:, None]
            out = jax.ops.segment_sum(msgs, dst, num_segments=n_nodes)
            return out + b

        def add_self_loops(edge_index, n_nodes):
            loop = jnp.arange(n_nodes, dtype=edge_index.dtype)
            src = jnp.concatenate([edge_index[0], loop])
            dst = jnp.concatenate([edge_index[1], loop])
            return (src, dst)
        key = jax.random.key(seed)
        k1, k2, k3, k4 = jax.random.split(key, 4)
        x = jax.random.normal(k1, (N_NODES, D), dtype=jnp.float32)
        edge_index = jax.random.randint(k2, (2, N_EDGES), 0, N_NODES, dtype=jnp.int32)
        glorot = float(np.sqrt(6.0 / (D + D)))
        W1 = jax.random.uniform(k3, (D, D), jnp.float32, -glorot, glorot)
        W2 = jax.random.uniform(k4, (D, D), jnp.float32, -glorot, glorot)
        b1 = jnp.zeros((D,), jnp.float32)
        b2 = jnp.zeros((D,), jnp.float32)
        return {'x': x, 'W1': W1, 'b1': b1, 'W2': W2, 'b2': b2, 'edge_index': edge_index}
    _L3_gnn_all = _L3_gnn_setup()
    _L3_gnn_in = {k: v for k, v in _L3_gnn_all.items() if k in ('W1', 'b1', 'W2', 'b2')}
    del _L3_gnn_all

    def _L3_ffn_setup():
        import jax, jax.numpy as jnp
        import numpy as np
        DIM = 768
        HEADS = 12
        HD = DIM // HEADS
        MLP = 48
        RHD = 512
        RANK = 256
        BS = 2
        RESERVE = 1
        EPS = 1e-05

        def _ln(x, g, b):
            m = jnp.mean(x, axis=-1, keepdims=True)
            v = jnp.var(x, axis=-1, keepdims=True)
            return (x - m) / jnp.sqrt(v + EPS) * g + b

        def _gelu(t):
            return jax.nn.gelu(t, approximate=False)

        def _forward(x, wq, bq, wk, bk, wv, bv, wo, bo, ln1_g, ln1_b, ln2_g, ln2_b, fc1_w, fc1_b, fc2_w, fc2_b, r_ln_g, r_ln_b, r_in_w, r_in_b, r_o1_w, r_o1_b, r_o2_w, r_o2_b, r_o3_w, r_o3_b, lra_down, lra_up):
            B, N, _ = x.shape
            e = _gelu(_ln(x, r_ln_g, r_ln_b) @ r_in_w.T + r_in_b)
            g = jnp.mean(e[:, RESERVE:, :], axis=1, keepdims=True)
            f = jnp.concatenate([e, jnp.broadcast_to(g, e.shape)], axis=-1)
            h1 = _gelu(f @ r_o1_w.T + r_o1_b)
            h2 = _gelu(h1 @ r_o2_w.T + r_o2_b)
            logits = (h2 @ r_o3_w.T + r_o3_b).reshape(B, N, BS, 2)
            hard = jax.nn.one_hot(jnp.argmax(logits, axis=-1), 2, dtype=x.dtype)
            keep = jnp.broadcast_to(jnp.array([0.0, 1.0], dtype=x.dtype), hard[:, :RESERVE].shape)
            hard = hard.at[:, :RESERVE].set(keep)
            hard = jax.lax.stop_gradient(hard)
            bits = hard[..., 1]
            indices = (bits * jnp.array([2.0, 1.0], dtype=x.dtype)).sum(-1).astype(jnp.int32)
            indices = jax.lax.stop_gradient(indices)
            xa = _ln(x, ln1_g, ln1_b)
            q = (xa @ wq.T + bq).reshape(B, N, HEADS, HD).transpose(0, 2, 1, 3)
            k = (xa @ wk.T + bk).reshape(B, N, HEADS, HD).transpose(0, 2, 1, 3)
            v = (xa @ wv.T + bv).reshape(B, N, HEADS, HD).transpose(0, 2, 1, 3)
            s = jax.nn.softmax(jnp.einsum('bhqd,bhkd->bhqk', q, k) / np.float32(np.sqrt(HD)), axis=-1)
            o = jnp.einsum('bhqk,bhkd->bhqd', s, v).transpose(0, 2, 1, 3).reshape(B, N, DIM)
            o = o @ wo.T + bo
            h = x + bits[:, :, 0:1] * o
            xf = _ln(h, ln2_g, ln2_b)
            ff = _gelu(xf @ fc1_w.T + fc1_b) @ fc2_w.T + fc2_b
            out = h + bits[:, :, 1:2] * ff
            down = jnp.einsum('bnd,krd->bknr', out, lra_down)
            up = jnp.einsum('bknr,kdr->bknd', down, lra_up)
            sel = jax.nn.one_hot(indices, 3, dtype=x.dtype)
            out = out + jnp.einsum('bknd,bnk->bnd', up, sel)
            return out
        key = jax.random.key(seed)
        ks = iter(jax.random.split(key, 40))

        def w(shape, std=0.02):
            return (jax.random.normal(next(ks), shape) * std).astype(jnp.float32)
        B, N = (128, 197)
        inp = {'x': jax.random.normal(next(ks), (B, N, DIM), dtype=jnp.float32)}
        inp.update(wq=w((DIM, DIM)), bq=jnp.zeros((DIM,), jnp.float32), wk=w((DIM, DIM)), bk=jnp.zeros((DIM,), jnp.float32), wv=w((DIM, DIM)), bv=jnp.zeros((DIM,), jnp.float32), wo=w((DIM, DIM)), bo=jnp.zeros((DIM,), jnp.float32), ln1_g=jnp.ones((DIM,), jnp.float32), ln1_b=jnp.zeros((DIM,), jnp.float32), ln2_g=jnp.ones((DIM,), jnp.float32), ln2_b=jnp.zeros((DIM,), jnp.float32), fc1_w=w((MLP, DIM)), fc1_b=jnp.zeros((MLP,), jnp.float32), fc2_w=w((DIM, MLP)), fc2_b=jnp.zeros((DIM,), jnp.float32), r_ln_g=jnp.ones((DIM,), jnp.float32), r_ln_b=jnp.zeros((DIM,), jnp.float32), r_in_w=w((RHD, DIM)), r_in_b=jnp.zeros((RHD,), jnp.float32), r_o1_w=w((RHD, 2 * RHD)), r_o1_b=jnp.zeros((RHD,), jnp.float32), r_o2_w=w((RHD // 2, RHD)), r_o2_b=jnp.zeros((RHD // 2,), jnp.float32), r_o3_w=w((2 * BS, RHD // 2), 0.01), r_o3_b=jnp.array([0.0, 5.0, 0.0, 5.0], dtype=jnp.float32), lra_down=w((3, RANK, DIM), 0.01), lra_up=w((3, DIM, RANK), 0.01))
        return inp
    _L3_ffn_all = _L3_ffn_setup()
    _L3_ffn_in = {k: v for k, v in _L3_ffn_all.items() if k in ('wq', 'bq', 'wk', 'bk', 'wv', 'bv', 'wo', 'bo', 'ln1_g', 'ln1_b', 'ln2_g', 'ln2_b', 'fc1_w', 'fc1_b', 'fc2_w', 'fc2_b', 'r_ln_g', 'r_ln_b', 'r_in_w', 'r_in_b', 'r_o1_w', 'r_o1_b', 'r_o2_w', 'r_o2_b', 'r_o3_w', 'r_o3_b', 'lra_down', 'lra_up')}
    del _L3_ffn_all
    return {'x': x, 'src': src, 'dst': dst, 'edge_weight': edge_weight, 'L0_gnn_W1': _L0_gnn_in['W1'], 'L0_gnn_a_src1': _L0_gnn_in['a_src1'], 'L0_gnn_a_dst1': _L0_gnn_in['a_dst1'], 'L0_gnn_b1': _L0_gnn_in['b1'], 'L0_gnn_W2': _L0_gnn_in['W2'], 'L0_gnn_a_src2': _L0_gnn_in['a_src2'], 'L0_gnn_a_dst2': _L0_gnn_in['a_dst2'], 'L0_gnn_b2': _L0_gnn_in['b2'], 'L0_ffn_v_w': _L0_ffn_in['v_w'], 'L0_ffn_v_b': _L0_ffn_in['v_b'], 'L0_ffn_gate_w': _L0_ffn_in['gate_w'], 'L0_ffn_gate_b': _L0_ffn_in['gate_b'], 'L0_ffn_w1': _L0_ffn_in['w1'], 'L0_ffn_b1': _L0_ffn_in['b1'], 'L0_ffn_w2': _L0_ffn_in['w2'], 'L0_ffn_b2': _L0_ffn_in['b2'], 'L0_ffn_out_w': _L0_ffn_in['out_w'], 'L0_ffn_out_b': _L0_ffn_in['out_b'], 'L0_ffn_bk_scale': _L0_ffn_in['bk_scale'], 'L1_gnn_W': _L1_gnn_in['W'], 'L1_gnn_b': _L1_gnn_in['b'], 'L1_ffn_Wg': _L1_ffn_in['Wg'], 'L1_ffn_bg': _L1_ffn_in['bg'], 'L1_ffn_Wge': _L1_ffn_in['Wge'], 'L1_ffn_bge': _L1_ffn_in['bge'], 'L1_ffn_W1': _L1_ffn_in['W1'], 'L1_ffn_b1': _L1_ffn_in['b1'], 'L1_ffn_W2': _L1_ffn_in['W2'], 'L1_ffn_b2': _L1_ffn_in['b2'], 'L2_gnn_Wd': _L2_gnn_in['Wd'], 'L2_gnn_bd': _L2_gnn_in['bd'], 'L2_gnn_Wu': _L2_gnn_in['Wu'], 'L2_gnn_bu': _L2_gnn_in['bu'], 'L2_gnn_W1': _L2_gnn_in['W1'], 'L2_gnn_b1': _L2_gnn_in['b1'], 'L2_gnn_W2': _L2_gnn_in['W2'], 'L2_gnn_b2': _L2_gnn_in['b2'], 'L2_ffn_w_in': _L2_ffn_in['w_in'], 'L2_ffn_g_in': _L2_ffn_in['g_in'], 'L2_ffn_w_out': _L2_ffn_in['w_out'], 'L2_ffn_g_out': _L2_ffn_in['g_out'], 'L3_gnn_W1': _L3_gnn_in['W1'], 'L3_gnn_b1': _L3_gnn_in['b1'], 'L3_gnn_W2': _L3_gnn_in['W2'], 'L3_gnn_b2': _L3_gnn_in['b2'], 'L3_ffn_wq': _L3_ffn_in['wq'], 'L3_ffn_bq': _L3_ffn_in['bq'], 'L3_ffn_wk': _L3_ffn_in['wk'], 'L3_ffn_bk': _L3_ffn_in['bk'], 'L3_ffn_wv': _L3_ffn_in['wv'], 'L3_ffn_bv': _L3_ffn_in['bv'], 'L3_ffn_wo': _L3_ffn_in['wo'], 'L3_ffn_bo': _L3_ffn_in['bo'], 'L3_ffn_ln1_g': _L3_ffn_in['ln1_g'], 'L3_ffn_ln1_b': _L3_ffn_in['ln1_b'], 'L3_ffn_ln2_g': _L3_ffn_in['ln2_g'], 'L3_ffn_ln2_b': _L3_ffn_in['ln2_b'], 'L3_ffn_fc1_w': _L3_ffn_in['fc1_w'], 'L3_ffn_fc1_b': _L3_ffn_in['fc1_b'], 'L3_ffn_fc2_w': _L3_ffn_in['fc2_w'], 'L3_ffn_fc2_b': _L3_ffn_in['fc2_b'], 'L3_ffn_r_ln_g': _L3_ffn_in['r_ln_g'], 'L3_ffn_r_ln_b': _L3_ffn_in['r_ln_b'], 'L3_ffn_r_in_w': _L3_ffn_in['r_in_w'], 'L3_ffn_r_in_b': _L3_ffn_in['r_in_b'], 'L3_ffn_r_o1_w': _L3_ffn_in['r_o1_w'], 'L3_ffn_r_o1_b': _L3_ffn_in['r_o1_b'], 'L3_ffn_r_o2_w': _L3_ffn_in['r_o2_w'], 'L3_ffn_r_o2_b': _L3_ffn_in['r_o2_b'], 'L3_ffn_r_o3_w': _L3_ffn_in['r_o3_w'], 'L3_ffn_r_o3_b': _L3_ffn_in['r_o3_b'], 'L3_ffn_lra_down': _L3_ffn_in['lra_down'], 'L3_ffn_lra_up': _L3_ffn_in['lra_up']}

def reference(x, src, dst, edge_weight, L0_gnn_W1, L0_gnn_a_src1, L0_gnn_a_dst1, L0_gnn_b1, L0_gnn_W2, L0_gnn_a_src2, L0_gnn_a_dst2, L0_gnn_b2, L0_ffn_v_w, L0_ffn_v_b, L0_ffn_gate_w, L0_ffn_gate_b, L0_ffn_w1, L0_ffn_b1, L0_ffn_w2, L0_ffn_b2, L0_ffn_out_w, L0_ffn_out_b, L0_ffn_bk_scale, L1_gnn_W, L1_gnn_b, L1_ffn_Wg, L1_ffn_bg, L1_ffn_Wge, L1_ffn_bge, L1_ffn_W1, L1_ffn_b1, L1_ffn_W2, L1_ffn_b2, L2_gnn_Wd, L2_gnn_bd, L2_gnn_Wu, L2_gnn_bu, L2_gnn_W1, L2_gnn_b1, L2_gnn_W2, L2_gnn_b2, L2_ffn_w_in, L2_ffn_g_in, L2_ffn_w_out, L2_ffn_g_out, L3_gnn_W1, L3_gnn_b1, L3_gnn_W2, L3_gnn_b2, L3_ffn_wq, L3_ffn_bq, L3_ffn_wk, L3_ffn_bk, L3_ffn_wv, L3_ffn_bv, L3_ffn_wo, L3_ffn_bo, L3_ffn_ln1_g, L3_ffn_ln1_b, L3_ffn_ln2_g, L3_ffn_ln2_b, L3_ffn_fc1_w, L3_ffn_fc1_b, L3_ffn_fc2_w, L3_ffn_fc2_b, L3_ffn_r_ln_g, L3_ffn_r_ln_b, L3_ffn_r_in_w, L3_ffn_r_in_b, L3_ffn_r_o1_w, L3_ffn_r_o1_b, L3_ffn_r_o2_w, L3_ffn_r_o2_b, L3_ffn_r_o3_w, L3_ffn_r_o3_b, L3_ffn_lra_down, L3_ffn_lra_up):
    import jax
    import jax.numpy as jnp

    def _L0_gnn_ref(x, W1, a_src1, a_dst1, b1, W2, a_src2, a_dst2, b2, edge_list):
        import jax, jax.numpy as jnp
        import numpy as np
        NEG_SLOPE = 0.2
        EPS = 1e-16
        N_NODES = 128
        N_EDGES = 1024
        D_IN = 768
        D_HID = 768
        H1 = 8
        H2 = 1

        def gat_layer(x, W, a_s, a_d, b, edge_index, concat):
            n = x.shape[0]
            H, C = a_s.shape
            h = (x @ W).reshape(n, H, C)
            src, dst = (edge_index[0], edge_index[1])
            alpha_s = jnp.einsum('nhc,hc->nh', h, a_s)
            alpha_d = jnp.einsum('nhc,hc->nh', h, a_d)
            e = jax.nn.leaky_relu(alpha_s[src] + alpha_d[dst], NEG_SLOPE)
            m = jax.ops.segment_max(e, dst, num_segments=n)
            e = jnp.exp(e - m[dst])
            denom = jax.ops.segment_sum(e, dst, num_segments=n)
            alpha = e / (denom[dst] + EPS)
            msg = h[src] * alpha[:, :, None]
            out = jax.ops.segment_sum(msg, dst, num_segments=n)
            out = out.reshape(n, H * C) if concat else out.mean(axis=1)
            return out + b
        h = gat_layer(x, W1, a_src1, a_dst1, b1, edge_list, concat=True)
        h = jax.nn.elu(h)
        out = gat_layer(h, W2, a_src2, a_dst2, b2, edge_list, concat=True)
        return out

    def _L0_ffn_ref(x, v_w, v_b, gate_w, gate_b, w1, b1, w2, b2, out_w, out_b, bk_scale):
        import jax, jax.numpy as jnp
        import numpy as np
        B, N, D, E, F, K = (2, 32, 768, 8, 48, 2)
        V_MAX = 3.0
        FEAT_CLAMP = 10.0

        def bk_green_diag(a):
            aT = jnp.swapaxes(a, 0, 1)

            def step(c, ai):
                d = ai - 1.0 / c
                return (d, d)
            d0 = aT[0]
            _, d_rest = jax.lax.scan(step, d0, aT[1:])
            d = jnp.concatenate([d0[None], d_rest], axis=0)
            eN = aT[-1]
            _, e_rest = jax.lax.scan(step, eN, aT[:-1], reverse=True)
            e = jnp.concatenate([e_rest, eN[None]], axis=0)
            G = 1.0 / (d + e - aT)
            return jnp.swapaxes(G, 0, 1)
        v = jnp.clip(x @ v_w + v_b, -V_MAX, V_MAX)
        a = (-2.0 + v).astype(jnp.complex64) - 1j
        G = bk_green_diag(a)
        feats = jnp.stack([G.real, G.imag], axis=-1)
        logits = x @ gate_w + gate_b
        probs = jax.nn.softmax(logits, axis=-1)
        topv, topi = jax.lax.top_k(probs, K)
        topv = topv / jnp.sum(topv, axis=-1, keepdims=True)
        comb = jnp.sum(topv[..., None] * jax.nn.one_hot(topi, E, dtype=x.dtype), axis=2)
        h = jax.nn.gelu(jnp.einsum('bnd,edf->bnef', x, w1) + b1)
        y = jnp.einsum('bnef,efd->bned', h, w2) + b2
        ffn_out = jnp.einsum('bne,bned->bnd', comb, y)
        feats_c = jnp.clip(feats, -FEAT_CLAMP, FEAT_CLAMP)
        spec_out = feats_c @ out_w + out_b
        return ffn_out + bk_scale * spec_out

    def _L1_gnn_ref(x, edge_index, W, b):
        import jax, jax.numpy as jnp
        import numpy as np
        N_NODES = 10000
        n = x.shape[0]
        loops = jnp.arange(n, dtype=edge_index.dtype)
        row = jnp.concatenate([edge_index[0], loops])
        col = jnp.concatenate([edge_index[1], loops])
        ones = jnp.ones(row.shape[0], dtype=x.dtype)
        deg = jax.ops.segment_sum(ones, col, num_segments=n)
        dinv = jnp.where(deg > 0, jax.lax.rsqrt(deg), 0.0)
        norm = dinv[row] * dinv[col]
        h = x @ W
        msg = h[row] * norm[:, None]
        out = jax.ops.segment_sum(msg, col, num_segments=n) + b
        return out

    def _L1_ffn_ref(x, Wg, bg, Wge, bge, W1, b1, W2, b2):
        import jax, jax.numpy as jnp
        import numpy as np
        G, E = (4, 8)
        KG, KE = (2, 2)
        D, M = (768, 48)
        SCALE = 0.02

        def _combine_weights(xf, Wg, bg, Wge, bge):
            N = xf.shape[0]
            glog = xf @ Wg + bg
            gtop, gidx = jax.lax.top_k(glog, KG)
            ggate = jax.nn.softmax(gtop, axis=-1)
            elog_all = jnp.einsum('nd,gde->nge', xf, Wge) + bge
            elog = jnp.take_along_axis(elog_all, gidx[:, :, None], axis=1)
            etop, eidx = jax.lax.top_k(elog, KE)
            egate = jax.nn.softmax(etop, axis=-1)
            w = ggate[:, :, None] * egate
            flat = gidx[:, :, None] * E + eidx
            comb = jnp.zeros((N, G * E), xf.dtype).at[jnp.arange(N)[:, None, None], flat].add(w)
            return comb
        shp = x.shape
        xf = x.reshape(-1, D)
        comb = _combine_weights(xf, Wg, bg, Wge, bge)
        h = jax.nn.gelu(jnp.einsum('nd,edm->nem', xf, W1) + b1, approximate=False)
        y = jnp.einsum('nem,emd->ned', h, W2) + b2
        out = jnp.einsum('ne,ned->nd', comb, y)
        return out.reshape(shp)

    def _L2_gnn_ref(x, edge_index, edge_weight, Wd, bd, Wu, bu, W1, b1, W2, b2):
        import jax, jax.numpy as jnp
        import numpy as np
        N = 50000
        E = 500000
        D = 768
        H = 256
        R = 32

        def _gcn(x, W, b, row, col, ew):
            x = x @ W
            n = x.shape[0]
            deg = jax.ops.segment_sum(ew, col, num_segments=n) + 1.0
            dinv = jax.lax.rsqrt(deg)
            norm = dinv[row] * ew * dinv[col]
            agg = jax.ops.segment_sum(norm[:, None] * x[row], col, num_segments=n)
            return agg + (dinv * dinv)[:, None] * x + b
        h = jax.nn.relu(x @ Wd + bd) @ Wu + bu + x
        row, col = (edge_index[0], edge_index[1])
        h = jax.nn.relu(_gcn(h, W1, b1, row, col, edge_weight))
        h = _gcn(h, W2, b2, row, col, edge_weight)
        return h

    def _L2_ffn_ref(x, w_in, g_in, w_out, g_out):
        import jax, jax.numpy as jnp
        import numpy as np
        EPS_NORM = 1e-06
        EPS_Q = 1e-05

        def rmsnorm(x, g):
            return x * jax.lax.rsqrt(jnp.mean(x * x, axis=-1, keepdims=True) + EPS_NORM) * g

        def activation_quant(x):
            scale = 127.0 / jnp.maximum(jnp.max(jnp.abs(x), axis=-1, keepdims=True), EPS_Q)
            return jnp.clip(jnp.round(x * scale), -128, 127) / scale

        def weight_quant(w):
            scale = 1.0 / jnp.maximum(jnp.mean(jnp.abs(w)), EPS_Q)
            return jnp.clip(jnp.round(w * scale), -1, 1) / scale

        def bitlinear(x, w, g):
            x_norm = rmsnorm(x, g)
            x_q = x_norm + jax.lax.stop_gradient(activation_quant(x_norm) - x_norm)
            w_q = w + jax.lax.stop_gradient(weight_quant(w) - w)
            return jnp.einsum('bsd,od->bso', x_q, w_q)
        h = bitlinear(x, w_in, g_in)
        up, gate = jnp.split(h, 2, axis=-1)
        y = jax.nn.silu(gate) * up
        return bitlinear(y, w_out, g_out)

    def _L3_gnn_ref(x, W1, b1, W2, b2, edge_index):
        import jax, jax.numpy as jnp
        import numpy as np
        N_NODES = 10000
        D = 768
        N_EDGES = 2500

        def gcn_conv(x, W, b, src, dst, n_nodes):
            h = x @ W
            deg = jax.ops.segment_sum(jnp.ones_like(dst, dtype=h.dtype), dst, num_segments=n_nodes)
            dinv = jnp.where(deg > 0, jax.lax.rsqrt(deg), 0.0)
            norm = dinv[src] * dinv[dst]
            msgs = h[src] * norm[:, None]
            out = jax.ops.segment_sum(msgs, dst, num_segments=n_nodes)
            return out + b

        def add_self_loops(edge_index, n_nodes):
            loop = jnp.arange(n_nodes, dtype=edge_index.dtype)
            src = jnp.concatenate([edge_index[0], loop])
            dst = jnp.concatenate([edge_index[1], loop])
            return (src, dst)
        n = x.shape[0]
        src, dst = add_self_loops(edge_index, n)
        h = gcn_conv(x, W1, b1, src, dst, n)
        h = jax.nn.relu(h)
        out = gcn_conv(h, W2, b2, src, dst, n)
        return out

    def _L3_ffn_ref(x, wq, bq, wk, bk, wv, bv, wo, bo, ln1_g, ln1_b, ln2_g, ln2_b, fc1_w, fc1_b, fc2_w, fc2_b, r_ln_g, r_ln_b, r_in_w, r_in_b, r_o1_w, r_o1_b, r_o2_w, r_o2_b, r_o3_w, r_o3_b, lra_down, lra_up):
        import jax, jax.numpy as jnp
        import numpy as np
        DIM = 768
        HEADS = 12
        HD = DIM // HEADS
        MLP = 48
        RHD = 512
        RANK = 256
        BS = 2
        RESERVE = 1
        EPS = 1e-05

        def _ln(x, g, b):
            m = jnp.mean(x, axis=-1, keepdims=True)
            v = jnp.var(x, axis=-1, keepdims=True)
            return (x - m) / jnp.sqrt(v + EPS) * g + b

        def _gelu(t):
            return jax.nn.gelu(t, approximate=False)

        def _forward(x, wq, bq, wk, bk, wv, bv, wo, bo, ln1_g, ln1_b, ln2_g, ln2_b, fc1_w, fc1_b, fc2_w, fc2_b, r_ln_g, r_ln_b, r_in_w, r_in_b, r_o1_w, r_o1_b, r_o2_w, r_o2_b, r_o3_w, r_o3_b, lra_down, lra_up):
            B, N, _ = x.shape
            e = _gelu(_ln(x, r_ln_g, r_ln_b) @ r_in_w.T + r_in_b)
            g = jnp.mean(e[:, RESERVE:, :], axis=1, keepdims=True)
            f = jnp.concatenate([e, jnp.broadcast_to(g, e.shape)], axis=-1)
            h1 = _gelu(f @ r_o1_w.T + r_o1_b)
            h2 = _gelu(h1 @ r_o2_w.T + r_o2_b)
            logits = (h2 @ r_o3_w.T + r_o3_b).reshape(B, N, BS, 2)
            hard = jax.nn.one_hot(jnp.argmax(logits, axis=-1), 2, dtype=x.dtype)
            keep = jnp.broadcast_to(jnp.array([0.0, 1.0], dtype=x.dtype), hard[:, :RESERVE].shape)
            hard = hard.at[:, :RESERVE].set(keep)
            hard = jax.lax.stop_gradient(hard)
            bits = hard[..., 1]
            indices = (bits * jnp.array([2.0, 1.0], dtype=x.dtype)).sum(-1).astype(jnp.int32)
            indices = jax.lax.stop_gradient(indices)
            xa = _ln(x, ln1_g, ln1_b)
            q = (xa @ wq.T + bq).reshape(B, N, HEADS, HD).transpose(0, 2, 1, 3)
            k = (xa @ wk.T + bk).reshape(B, N, HEADS, HD).transpose(0, 2, 1, 3)
            v = (xa @ wv.T + bv).reshape(B, N, HEADS, HD).transpose(0, 2, 1, 3)
            s = jax.nn.softmax(jnp.einsum('bhqd,bhkd->bhqk', q, k) / np.float32(np.sqrt(HD)), axis=-1)
            o = jnp.einsum('bhqk,bhkd->bhqd', s, v).transpose(0, 2, 1, 3).reshape(B, N, DIM)
            o = o @ wo.T + bo
            h = x + bits[:, :, 0:1] * o
            xf = _ln(h, ln2_g, ln2_b)
            ff = _gelu(xf @ fc1_w.T + fc1_b) @ fc2_w.T + fc2_b
            out = h + bits[:, :, 1:2] * ff
            down = jnp.einsum('bnd,krd->bknr', out, lra_down)
            up = jnp.einsum('bknr,kdr->bknd', down, lra_up)
            sel = jax.nn.one_hot(indices, 3, dtype=x.dtype)
            out = out + jnp.einsum('bknd,bnk->bnd', up, sel)
            return out
        return _forward(x, wq, bq, wk, bk, wv, bv, wo, bo, ln1_g, ln1_b, ln2_g, ln2_b, fc1_w, fc1_b, fc2_w, fc2_b, r_ln_g, r_ln_b, r_in_w, r_in_b, r_o1_w, r_o1_b, r_o2_w, r_o2_b, r_o3_w, r_o3_b, lra_down, lra_up)
    edge_index = jnp.stack([src, dst])
    x = x + _L0_gnn_ref(_layernorm(x, axis=-1), L0_gnn_W1, L0_gnn_a_src1, L0_gnn_a_dst1, L0_gnn_b1, L0_gnn_W2, L0_gnn_a_src2, L0_gnn_a_dst2, L0_gnn_b2, edge_index)
    x = x + _L0_ffn_ref(_layernorm(x, axis=-1)[None], L0_ffn_v_w, L0_ffn_v_b, L0_ffn_gate_w, L0_ffn_gate_b, L0_ffn_w1, L0_ffn_b1, L0_ffn_w2, L0_ffn_b2, L0_ffn_out_w, L0_ffn_out_b, L0_ffn_bk_scale)[0]
    x = x + _L1_gnn_ref(_layernorm(x, axis=-1), edge_index, L1_gnn_W, L1_gnn_b)
    x = x + _L1_ffn_ref(_layernorm(x, axis=-1)[None], L1_ffn_Wg, L1_ffn_bg, L1_ffn_Wge, L1_ffn_bge, L1_ffn_W1, L1_ffn_b1, L1_ffn_W2, L1_ffn_b2)[0]
    x = x + _L2_gnn_ref(_layernorm(x, axis=-1), edge_index, edge_weight, L2_gnn_Wd, L2_gnn_bd, L2_gnn_Wu, L2_gnn_bu, L2_gnn_W1, L2_gnn_b1, L2_gnn_W2, L2_gnn_b2)
    x = x + _L2_ffn_ref(_layernorm(x, axis=-1)[None], L2_ffn_w_in, L2_ffn_g_in, L2_ffn_w_out, L2_ffn_g_out)[0]
    x = x + _L3_gnn_ref(_layernorm(x, axis=-1), L3_gnn_W1, L3_gnn_b1, L3_gnn_W2, L3_gnn_b2, edge_index)
    x = x + _L3_ffn_ref(_layernorm(x, axis=-1)[None], L3_ffn_wq, L3_ffn_bq, L3_ffn_wk, L3_ffn_bk, L3_ffn_wv, L3_ffn_bv, L3_ffn_wo, L3_ffn_bo, L3_ffn_ln1_g, L3_ffn_ln1_b, L3_ffn_ln2_g, L3_ffn_ln2_b, L3_ffn_fc1_w, L3_ffn_fc1_b, L3_ffn_fc2_w, L3_ffn_fc2_b, L3_ffn_r_ln_g, L3_ffn_r_ln_b, L3_ffn_r_in_w, L3_ffn_r_in_b, L3_ffn_r_o1_w, L3_ffn_r_o1_b, L3_ffn_r_o2_w, L3_ffn_r_o2_b, L3_ffn_r_o3_w, L3_ffn_r_o3_b, L3_ffn_lra_down, L3_ffn_lra_up)[0]
    return x

_drawn_inputs = setup_inputs


def setup_inputs(seed=0):
    import zlib

    import numpy as np

    out = dict(_drawn_inputs(seed))
    spreads = {'L0_gnn_b1': (0.0, 0.1),
     'L0_gnn_b2': (0.0, 0.1),
     'L0_ffn_gate_b': (0.0, 0.472),
     'L0_ffn_b1': (0.0, 0.8),
     'L0_ffn_b2': (0.0, 0.1),
     'L0_ffn_out_b': (0.0, 0.1),
     'L0_ffn_bk_scale': (1.0, 0.6),
     'L1_gnn_b': (0.0, 0.1),
     'L1_ffn_bg': (0.0, 0.8),
     'L1_ffn_bge': (0.0, 0.627),
     'L1_ffn_b1': (0.0, 0.8),
     'L1_ffn_b2': (0.0, 0.3),
     'L2_gnn_bd': (0.0, 0.8),
     'L2_gnn_bu': (0.0, 0.1),
     'L2_gnn_b1': (0.0, 0.324),
     'L2_gnn_b2': (0.0, 0.1),
     'L2_ffn_g_in': (1.0, 0.6),
     'L2_ffn_g_out': (1.0, 0.6),
     'L3_gnn_b1': (0.0, 0.1),
     'L3_gnn_b2': (0.0, 0.1),
     'L3_ffn_bq': (0.0, 0.8),
     'L3_ffn_bk': (0.0, 2.0),
     'L3_ffn_bv': (0.0, 0.445),
     'L3_ffn_bo': (0.0, 0.1),
     'L3_ffn_ln1_g': (1.0, 0.6),
     'L3_ffn_ln1_b': (0.0, 0.8),
     'L3_ffn_ln2_g': (1.0, 0.6),
     'L3_ffn_ln2_b': (0.0, 0.8),
     'L3_ffn_fc1_b': (0.0, 0.8),
     'L3_ffn_fc2_b': (0.0, 0.307),
     'L3_ffn_r_ln_g': (1.0, 0.2),
     'L3_ffn_r_ln_b': (0.0, 0.1),
     'L3_ffn_r_in_b': (0.0, 0.1),
     'L3_ffn_r_o1_b': (0.0, 0.1),
     'L3_ffn_r_o2_b': (0.0, 0.1)}
    factors = {'edge_weight': 3.625,
     'L0_ffn_v_w': 8.0,
     'L0_ffn_w1': 3.739,
     'L0_ffn_w2': 3.393,
     'L0_ffn_out_w': 8.0,
     'L1_ffn_Wg': 3.567,
     'L1_ffn_W1': 5.531,
     'L1_ffn_W2': 5.199,
     'L2_ffn_w_in': 8.0,
     'L2_ffn_w_out': 8.0,
     'L3_ffn_wq': 8.0,
     'L3_ffn_wk': 8.0,
     'L3_ffn_fc1_w': 4.209,
     'L3_ffn_fc2_w': 4.298}
    for name, (base, spread) in spreads.items():
        noise = np.random.default_rng([zlib.crc32(name.encode()), seed]).standard_normal(out[name].shape)
        drawn = base * np.exp(spread * noise) if base else spread * noise
        out[name] = jnp.asarray(drawn.astype(out[name].dtype))
    for name, factor in factors.items():
        out[name] = (out[name] * factor).astype(out[name].dtype)
    return out
```

```python
import concourse.bass as bass
from concourse import mybir
from contextlib import ExitStack

F32 = mybir.dt.float32
BF16 = mybir.dt.bfloat16
I32 = mybir.dt.int32
ALU = mybir.AluOpType
ACT = mybir.ActivationFunctionType
AX = mybir.AxisListType

P = 128
D = 768
C = D // P
UNIT = C * D
SLOTS = 8
EDGES = 4224
EC = EDGES // P
HEADS1 = 8
WIN = 512
BIG = 1.0e30
LEAK = 0.2
SEG_EPS = 1e-16
LN_EPS = 1e-5
RMS_EPS = 1e-6
QUANT_EPS = 1e-5
ROUND = 12582912.0
E0, F0 = 8, 48
G1N, E1N = 4, 8
H0 = E0 * F0
H1N = G1N * E1N * F0
DOWN = 24
HID2 = 256
BIT = 32
RHD = 512
AH, AD = 12, 64
MLP = 48

HALVES = ((0, WIN), (WIN, D))

POSITION = [0, 4, 1, 5, 2, 6, 3, 7, 8, 10, 9, 11]

COLS = {}
_at = 0
for _name, _n in (("gat_b1", 48), ("bq", 6), ("bk", 6), ("ln1_g", 6), ("ln1_b", 6), ("r_ln_g", 6),
                  ("r_ln_b", 6), ("ln2_g", 6), ("ln2_b", 6), ("r_in_b", 4), ("r_o1_b", 4), ("r_o2_b", 2)):
    COLS[_name] = (_at, _at + _n)
    _at += _n
NCOLS = _at

ROWS = {}
_at = 0
for _name, _n in (("l0_b1", H0), ("l2_b1", HID2), ("l0_gate", E0 + 1), ("l1_gate", G1N + G1N * E1N),
                  ("g_out", BIT), ("r_o3_b", 4)):
    ROWS[_name] = (_at, _at + _n)
    _at += _n
NROWS = _at

UNITS = [
    [("l0_w1", 0, P, C * H0), ("l0_w2", C * H0, P, 3 * D)],
    [("l1_w", 0, P, UNIT)],
    [("l1f_w1a", 0, P, UNIT)],
    [("l1f_w1b", 0, P, UNIT)],
    [("l1f_w2a", 0, P, UNIT)],
    [("l1f_w2b", 0, P, UNIT)],
    [("l2_w1", 0, P, C * HID2), ("l2_w2", 1536, P, 2 * D), ("l2_win", 3072, P, C * 2 * BIT),
     ("l2_wd", 3456, P, C * DOWN), ("l2_wu", 3600, DOWN + 1, D)],
    [("l3_w1", 0, P, UNIT)],
    [("l3_w2", 0, P, UNIT)],
    [("r_in", 0, P, C * RHD), ("r_o2", 3072, P, 4 * RHD // 2), ("r_o3", 4096, P, 8)],
    [("wq", 0, P, UNIT)],
    [("r_o1", 0, P, 8 * RHD), ("fc1", 8 * RHD, P, C * MLP)],
    [("wk", 0, P, UNIT)],
    [("wv", 0, P, UNIT)],
    [("wo", 0, P, UNIT)],
    [("down", 0, P, UNIT)],
    [("up", 0, P, UNIT)],
]
FIRST_SLOT = 4
(U_L0, U_L1, U_L1W1A, U_L1W1B, U_L1W2A, U_L1W2B, U_L2, U_L3A, U_L3B, U_RIN, U_Q, U_RO1, U_K, U_V,
 U_O, U_DOWN, U_UP) = range(len(UNITS))


def build(nc, a, out):
    ctx = ExitStack()
    with ctx:
        def sb(name, shape, dt=F32):
            return ctx.enter_context(nc.sbuf_tensor(name, shape, dt))

        def sem(name):
            return ctx.enter_context(nc.semaphore(name))

        ring = sb("ring", [P, SLOTS, UNIT])
        x = sb("x", [P, D])
        xb = sb("xb", [P, D])
        xn = sb("xn", [P, D])
        xT = sb("xT", [P, C, P])
        g1 = sb("g1", [P, D])
        g2 = sb("g2", [P, D])
        g3 = sb("g3", [P, D])
        g4 = sb("g4", [P, D])
        h1 = sb("h1", [P, 2 * D])
        h2 = sb("h2", [P, 2 * D])
        avec = sb("avec", [P, 2 * D])
        row0 = sb("row0", [P, D])
        row1 = sb("row1", [P, D])
        rows = sb("rows", [P, NROWS])
        cols = sb("cols", [P, NCOLS])
        shiftm = sb("shiftm", [P, 3 * P])
        count = sb("count", [P, P])
        absent = sb("absent", [P, P])
        adj1T = sb("adj1T", [P, P])
        adj2T = sb("adj2T", [P, P])
        att = sb("att", [P, 2, P])
        attnT = sb("attnT", [P, 2, P])
        alpha = sb("alpha", [P, 2, 2])
        soft = sb("soft", [P, 4])
        stats = sb("stats", [P, 2, 6])
        mv = sb("mv", [P, 2])
        var = sb("var", [P, 1])
        rstd = sb("rstd", [P, 1])
        mhalf = sb("mhalf", [P, 1])
        ones = sb("ones", [P, P])
        zrow = sb("zrow", [1, P])
        gatew = sb("gatew", [P, C * (E0 + 1)])
        gatew1 = sb("gatew1", [P, C * (G1N + G1N * E1N)])
        lin = sb("lin", [P, 40])
        tk = sb("tk", [P, 5, 32])
        tks = sb("tks", [P, 2, 4])
        desc = sb("desc", [P, E1N])
        comb = sb("comb", [P, 44])
        identb = sb("identb", [P, P], BF16)
        combT = sb("combT", [32, P])
        cells = sb("cells", [P, 128])
        bias1 = sb("bias1", [P, 2])
        zT = sb("zT", [64, P])
        idx = sb("idx", [P, 2, EC], I32)
        idxb = sb("idxb", [P, 2, EC], BF16)
        ew = sb("ew", [P, 2, EC])
        ewb = sb("ewb", [P, 3, EC], BF16)

        ps = ctx.enter_context(nc.psum_tensor("ps", [P, 8 * WIN], F32))

        def bank(n, w=WIN, off=0, rows_=P):
            return ps[0:rows_, n * WIN + off:n * WIN + off + w]

        def head_psum(par):
            return ps[:, 0:D] if par == 0 else ps[:, WIN + 256:WIN + 256 + D]

        def score_ps(at):
            return ps[:, at * P:(at + 1) * P] if at < 10 else ps[:, (at + 2) * P:(at + 3) * P]

        ident = shiftm[:, P:2 * P]

        scratch = ring[:, 4:8, :].rearrange("p s n -> p (s n)").bitcast(BF16)
        n1h = EC * P
        oh_dst = scratch[:, 0:n1h].rearrange("p (e n) -> p e n", n=P)
        oh_src = scratch[:, n1h:5 * n1h].rearrange("p (k e n) -> p k e n", k=4, n=P)
        iotab = scratch[:, 5 * n1h:5 * n1h + P]
        iotai = ring[:, 7, UNIT - P:UNIT].bitcast(I32)

        masks = h2[0:1, 0:3 * P]
        state = h2[:, 384:416]
        ident4 = h2[0:1, 416:432]
        prod = h2[:, 512:640]
        w_in_q = g2[:, 256:448].bitcast(BF16)
        w_out_q = g3[0:BIT, 256:640].bitcast(BF16)
        bits = h2[:, 0:384].bitcast(BF16)
        bitsT = h2[:, 384:768].bitcast(BF16)
        SMALL = 16 * 8

        S = {}

        def s(name):
            if name not in S:
                S[name] = sem(name)
            return S[name]

        for name in ("x_in graph_in small_in avec_in w1_in0 w1_in1 w2_in0 w2_in1 w2_used hprod "
                     "h_rows alpha_ready alpha_rows score_sum score_leaky negmax exped weighed "
                     "denom_ready attn_ready attnT_ps attnT_ready agg_ready z_ready z_neg z_exp elu_ready "
                     "acc_zeroed dve_step pool_step act_step out_done").split():
            s(name)
        for n in range(SLOTS):
            s(f"slot{n}_in")

        landed, filled = [], [0] * SLOTS
        for u, parts in enumerate(UNITS):
            slot = (FIRST_SLOT + u) % SLOTS
            filled[slot] += 16 * len(parts)
            landed.append((slot, filled[slot]))

        released = [("l0_weights_used", 1), ("rows_ps", 3), ("hid1_mm", 2), ("hid1_mm", 4), ("w2a_used", 1),
                    ("rows_ps", 4), ("rows_ps", 5), ("mid_ps", 1), ("rows_ps", 7)]

        def unit(u, name, rearr=None, **kw):
            slot = landed[u][0]
            for part, c0, parts, n in UNITS[u]:
                if part == name:
                    v = ring[0:parts, slot, c0:c0 + n]
                    return v.rearrange(rearr, **kw) if rearr else v
            raise KeyError(name)

        def wait_unit(eng, u):
            slot, value = landed[u]
            eng.wait_ge(S[f"slot{slot}_in"], value)

        cell_at = {}

        def cell(name, n=1):
            if name not in cell_at:
                cell_at[name] = sum(w for _, w in cell_at.values()), n
            lo, w = cell_at[name]
            assert w == n and lo + n <= 128
            return cells[:, lo:lo + n]

        def col(name, i=None, n=1):
            lo, hi = COLS[name]
            return cols[:, lo:hi] if i is None else cols[:, lo + i:lo + i + n]

        def row(name):
            lo, hi = ROWS[name]
            return rows[:, lo:hi]

        def wait(eng, name, value):
            if not isinstance(value, int) or value >= 1:
                eng.wait_ge(s(name), value)

        used = {name: 0 for name in ("dve_step", "pool_step", "act_step")}

        def chained(eng, name, ins):
            used[name] += 1
            ins.then_inc(S[name], 1)
            eng.wait_ge(S[name], used[name])

        block = ctx.enter_context(nc.Block())

        def broadcast_row(src, n):
            return src.rearrange("(o n) -> o n", o=1).broadcast_to([P, n])

        @block.sync
        def _(sp):
            def load_avec(h):
                wait(sp, "alpha_ready", h)
                sp.dma_start(avec[:], a["gat_a"][bass.ds(h, 1), :].broadcast_to([P, 2 * D])).then_inc(S["avec_in"], 16)

            def load_w1(h, par):
                if not isinstance(h, int) or h >= 2:
                    sp.wait_ge(S["hprod"], h - 1)
                sp.dma_start(ring[:, par, :], a["gat_w1"][bass.ds(h, 1)].rearrange("o p n -> (o p) n")) \
                    .then_inc(S[f"w1_in{par}"], 16)

            def load_w2(h, par):
                if not isinstance(h, int) or h >= 2:
                    sp.wait_ge(S["w2_used"], h - 1)
                sp.dma_start(ring[:, 2 + par, :], a["gat_w2"][bass.ds(h, 1)].rearrange("o p n -> (o p) n")) \
                    .then_inc(S[f"w2_in{par}"], 16)

            def load_step(h, par):
                load_avec(h)
                load_w1(h + 1, 1 - par)
                load_w2(h, par)

            def load_unit(u):
                slot = landed[u][0]
                for name, c0, parts, n in UNITS[u]:
                    sp.dma_start(ring[0:parts, slot, c0:c0 + n], a[name]).then_inc(S[f"slot{slot}_in"], 16)

            sp.dma_start(x[:], a["x"]).then_inc(S["x_in"], 16)
            load_w1(0, 0)
            load_avec(0)
            load_w1(1, 1)
            load_w2(0, 0)
            load_step(1, 1)
            load_step(2, 0)
            with sp.Fori(1, 3) as i:
                load_step(2 * i + 1, 1)
                load_step(2 * i + 2, 0)
            load_avec(7)
            load_w2(7, 1)
            load_avec(8)

            sp.wait_ge(s("edges_summed"), 1)
            for u in range(len(UNITS)):
                if u == 4:
                    sp.wait_ge(S["hprod"], 7)
                if u == 5:
                    sp.wait_ge(S["hprod"], 8)
                if u == 6:
                    sp.wait_ge(S["w2_used"], 7)
                if u == 7:
                    sp.wait_ge(S["hprod"], 9)
                if u >= SLOTS:
                    sp.wait_ge(s(released[u - SLOTS][0]), released[u - SLOTS][1])
                if u - SLOTS == U_L2:
                    sp.wait_ge(s("w_quantised"), 1)
                load_unit(u)
            sp.wait_ge(s("result_ready"), 1)
            sp.dma_start(out, xb[:]).then_inc(S["out_done"], 16)
            sp.wait_ge(S["out_done"], 16)

        @block.gpsimd
        def _(pool):
            def link(ins):
                chained(pool, "pool_step", ins)

            def inverse_root(k):
                pool.wait_ge(s("var_ready"), k)
                pool.tensor_tensor(rstd[:], var[:], mhalf[:], ALU.pow).then_inc(s("rstd_ready"), 1)

            link(pool.memset(mhalf[:], -0.5))
            pool.memset(shiftm[:], 0.0).then_inc(S["pool_step"], 1)
            used["pool_step"] += 1
            pool.wait_ge(S["pool_step"], used["pool_step"])
            pool.affine_select(out=shiftm[:], in_=shiftm[:], compare_op=ALU.not_equal, fill=1.0, base=P,
                               pattern=[[-1, 3 * P]], channel_multiplier=1).then_inc(s("constants"), 1)
            inverse_root(1)
            pool.wait_ge(s("constants"), 1)
            pool.tensor_copy(identb[:], ident).then_inc(s("constants"), 1)
            link(pool.iota(iotai, [[1, P]], base=0, channel_multiplier=0))
            pool.tensor_copy(iotab, iotai).then_inc(s("constants"), 1)
            pool.memset(ones[:], 1.0).then_inc(s("constants"), 1)
            pool.memset(zrow[:], 0.0).then_inc(s("constants"), 1)
            pool.memset(zT[:], 1.0).then_inc(s("constants"), 1)
            steps8 = tk[:, 0, 0:E1N].bitcast(I32)
            link(pool.iota(steps8, [[-1, E1N]], base=E1N, channel_multiplier=0))
            pool.tensor_copy(desc[:], steps8).then_inc(s("constants"), 1)
            pool.wait_ge(S["graph_in"], 48)
            link(pool.tensor_copy(ewb[:, 0, :], ew[:, 0, :]))
            link(pool.tensor_tensor(ew[:, 1, :], ew[:, 0, :], ewb[:, 0, :], ALU.subtract))
            link(pool.tensor_copy(ewb[:, 1, :], ew[:, 1, :]))
            link(pool.tensor_tensor(ew[:, 0, :], ew[:, 1, :], ewb[:, 1, :], ALU.subtract))
            pool.tensor_copy(ewb[:, 2, :], ew[:, 0, :]).then_inc(s("ew_parts"), 1)
            pool.wait_ge(s("ew_parts"), 1)
            pool.wait_ge(s("onehots"), 2)
            pool.tensor_tensor(oh_src[:, 3], oh_src[:, 0], ewb[:, 2, :].unsqueeze(2).broadcast_to([P, EC, P]),
                               ALU.mult).then_inc(s("ew_rows"), 1)

            def residual_bias(k, bias):
                pool.wait_ge(s("residual"), k)
                pool.tensor_tensor(xb[:], x[:], bias, ALU.add).then_inc(s("xb_ready"), 1)

            def load_row(dst, name, n=D):
                pool.dma_start(dst, broadcast_row(a[name], n)).then_inc(s("in_" + name), 16)

            pool.wait_ge(S["small_in"], SMALL)
            pool.wait_ge(S["x_in"], 16)
            pool.tensor_tensor(xb[:], x[:], row0[:], ALU.add).then_inc(s("xb_ready"), 1)
            for n in range(2):
                pool.wait_ge(s("degree"), n + 1)
                pool.tensor_tensor(cell("deg_root", 2)[:, n:n + 1], cell("degree", 2)[:, n:n + 1], mhalf[:], ALU.pow) \
                    .then_inc(s("deg_root"), 1)

            pool.wait_ge(s("residual"), 1)
            pool.memset(masks, 0.0).then_inc(S["pool_step"], 1)
            pool.memset(state, 0.0).then_inc(S["pool_step"], 1)
            pool.memset(ident4, 0.0).then_inc(S["pool_step"], 1)
            pool.memset(g4[0:11, :], 1.0).then_inc(S["pool_step"], 1)
            used["pool_step"] += 4
            pool.wait_ge(S["pool_step"], used["pool_step"])
            pool.dma_start(g4[8:11, :], a["bk_scale"].rearrange("(o n) -> o n", o=1).broadcast_to([3, D])) \
                .then_inc(s("spec_in"), 16)
            pool.dma_start(g3[0:11, :], a["l0_tail"]).then_inc(s("spec_in"), 16)
            pool.memset(masks[:, 0:P], 1.0).then_inc(s("bk_const"), 1)
            pool.memset(masks[:, 2 * P:3 * P], 1.0).then_inc(s("bk_const"), 1)
            pool.memset(ident4[:, 0:16:5], 1.0).then_inc(s("bk_const"), 1)
            for d in range(2):
                m = state[:, 16 * d:16 * d + 16]
                pool.memset(m[:, 1:3], -1.0).then_inc(s("bk_const"), 1)
                pool.memset(m[:, 7:8], -1.0).then_inc(s("bk_const"), 1)
                pool.memset(m[:, 4:5], 1.0).then_inc(s("bk_const"), 1)
                pool.memset(m[:, 8:14:5], 1.0).then_inc(s("bk_const"), 1)
            pool.memset(comb[:, 10:11], 1.0).then_inc(s("bk_const"), 1)
            inverse_root(2)
            pool.wait_ge(S["alpha_ready"], 9)
            load_row(avec[:], "l1_b1", 2 * D)

            pool.dma_start(g1[0:G1N * E1N, :], a["l1_b2"]).then_inc(s("in_b2"), 16)

            residual_bias(2, row1[:])
            load_row(row0[:], "g_in")
            pool.wait_ge(s("tail_ready"), 1)
            pool.dma_start(g4[0:BIT, :], a["l2_wout"]).then_inc(s("in_wout"), 16)
            inverse_root(3)
            pool.wait_ge(s("residual"), 3)
            pool.wait_ge(S["xb_ready"], 2)
            load_row(row1[:], "l2_b2")
            inverse_root(4)

            pool.wait_ge(s("in_l2_b2"), 16)
            residual_bias(4, row1[:])
            load_row(avec[:, 0:D], "l3_b1")
            load_row(avec[:, D:2 * D], "bv")
            inverse_root(5)
            pool.wait_ge(S["xb_ready"], 3)
            load_row(row1[:], "l3_b2")
            for k in (6, 7, 8):
                inverse_root(k)

            pool.wait_ge(s("in_l3_b2"), 16)
            residual_bias(6, row1[:])
            pool.dma_start(row0[0:MLP + 1, :], a["fc2"]).then_inc(s("in_fc2"), 16)
            inverse_root(9)
            pool.wait_ge(s("residual"), 7)
            load_row(avec[:, 0:D], "bo")
            for k in (10, 11, 12):
                inverse_root(k)
            pool.wait_ge(s("out_rows"), 1)
            pool.tensor_tensor(xb[:], x[:], g3[:], ALU.add).then_inc(s("xb_ready"), 1)

        @block.scalar
        def _(act):
            def copy(dst, src):
                return nc.scalar.activation(dst, src, ACT.Copy)

            def link(ins):
                chained(act, "act_step", ins)

            for n, name in enumerate(("dst", "src")):
                act.dma_start(idx[:, n, :], a[name]).then_inc(S["graph_in"], 16)
            act.dma_start(ew[:, 0, :], a["edge_weight"]).then_inc(S["graph_in"], 16)
            act.dma_start(cols[:], a["cols"]).then_inc(S["small_in"], 16)
            act.dma_start(row0[:], broadcast_row(a["gat_b2"], D)).then_inc(S["small_in"], 16)
            act.dma_start(row1[:], broadcast_row(a["l1_b"], D)).then_inc(S["small_in"], 16)
            act.dma_start(rows[:], broadcast_row(a["rows"], NROWS)).then_inc(S["small_in"], 16)
            act.dma_start(gatew[:], a["gatew"]).then_inc(S["small_in"], 16)
            act.dma_start(gatew1[:], a["gatew1"]).then_inc(S["small_in"], 16)
            act.dma_start(bias1[0:DOWN, 0:1], a["bd"]).then_inc(S["small_in"], 16)
            act.dma_start(bias1[0:MLP, 1:2], a["fc1_b"]).then_inc(S["small_in"], 16)

            def half_T(k):
                act.wait_ge(s("T_ps"), k)
                copy(xT[:, 0:4, :], bank(4).rearrange("p (c n) -> p c n", n=P)) \
                    .then_inc(s("T_ready"), 1)

            def head_rows(h, par):
                wait(act, "hprod", h + 1)
                if not isinstance(h, int) or h >= 2:
                    wait(act, "agg_ready", h - 1)
                    wait(act, "alpha_ready", h - 1)
                copy(h1[:, par * D:(par + 1) * D], head_psum(par)).then_inc(S["h_rows"], 1)

            def head_exp(h):
                wait(act, "negmax", h + 1)
                nc.scalar.activation(att[:, 0, :], att[:, 1, :], ACT.Exp, bias=soft[:, 1:2]) \
                    .then_inc(S["exped"], 1)

            def head_attnT(h, par):
                wait(act, "attnT_ps", h + 1)
                copy(attnT[:, par, :], bank(7, P, 384)).then_inc(S["attnT_ready"], 1)

            def head_elu(h):
                wait(act, "z_neg", h + 1)
                nc.scalar.activation(g2[:], g2[:], ACT.Exp).then_inc(S["z_exp"], 1)

            def step(h, par, last=False):
                head_exp(h)
                head_attnT(h, par)
                if not last:
                    head_rows(h + 1, 1 - par)
                head_elu(h)

            half_T(1)
            head_rows(0, 0)
            step(0, 0)
            step(1, 1)
            step(2, 0)
            with act.Fori(1, 3) as i:
                step(2 * i + 1, 1)
                step(2 * i + 2, 0)
            step(7, 1, last=True)
            act.wait_ge(S["hprod"], 9)
            copy(h1[:, 0:D], ps[:, 4 * WIN:4 * WIN + D]).then_inc(S["h_rows"], 1)
            head_exp(8)
            head_attnT(8, 0)

            half_T(2)
            act.wait_ge(s("top_shifted"), 1)
            nc.scalar.activation(tk[:, 3, 0:E0], tk[:, 3, 0:E0], ACT.Exp).then_inc(s("top_exped"), 1)
            act.wait_ge(s("hid0_ready"), 1)
            nc.scalar.activation(h1[:, 0:H0], h1[:, 0:H0], ACT.Gelu_apprx_tanh).then_inc(s("gelu0"), 1)
            act.wait_ge(s("hid0_ps"), 1)
            copy(h1[:, H0:2 * H0], ps[:, 4 * WIN:4 * WIN + H0]).then_inc(s("hid0T"), 1)

            half_T(3)
            half_T(4)
            act.wait_ge(s("top_shifted"), 2)
            nc.scalar.activation(tk[:, 3, :], tk[:, 3, :], ACT.Exp).then_inc(s("top_exped"), 1)
            act.wait_ge(s("top_shifted"), 3)
            nc.scalar.activation(tk[:, 3, 0:G1N], tk[:, 3, 0:G1N], ACT.Exp).then_inc(s("top_exped"), 1)
            for g in range(4):
                act.wait_ge(s("hid1_ready"), g + 1)
                nc.scalar.activation(h1[:, g * H0:(g + 1) * H0], h1[:, g * H0:(g + 1) * H0], ACT.Gelu) \
                    .then_inc(s("gelu1"), 1)
            for g in range(4):
                act.wait_ge(s("hid1_ps"), g + 1)
                copy(h2[:, g * H0:(g + 1) * H0], bank(4 + g % 2, H0)).then_inc(s("hid1T"), 1)

            half_T(5)
            act.wait_ge(s("down_ps"), 1)
            act.wait_ge(s("constants"), 6)
            nc.scalar.activation(zT[0:DOWN, :], bank(6, P, 0, DOWN), ACT.Relu, bias=bias1[0:DOWN, 0:1]) \
                .then_inc(s("down_ready"), 1)
            half_T(6)
            act.wait_ge(s("rel_ps"), 1)
            copy(g3[:, 0:HID2], bank(2, HID2)).then_inc(s("relT"), 1)
            act.wait_ge(s("bits_ps"), 1)
            copy(bitsT, ps[:, 4 * WIN:4 * WIN + D // 2].bitcast(BF16)).then_inc(s("bitsT_ready"), 1)
            act.wait_ge(s("gated"), 1)
            nc.scalar.activation(g1[:, 2 * BIT:3 * BIT], g1[:, BIT:2 * BIT], ACT.Exp, scale=-1.0).then_inc(s("gate_exp"), 1)

            half_T(7)
            half_T(8)

            act.wait_ge(s("xrT_ready"), 1)
            for c in range(C):
                last = nc.scalar.activation(g1[:, c * P:(c + 1) * P], ps[:, 4 * WIN + c * P:4 * WIN + (c + 1) * P],
                                            ACT.Identity, bias=col("ln1_b", c), scale=col("ln1_g", c))
            last.then_inc(s("xaT_ready"), 1)
            for f in range(4):
                act.wait_ge(s("rin_ps"), f + 1)
                nc.scalar.activation(h1[:, f * P:(f + 1) * P], bank(f % 2, P), ACT.Gelu, bias=col("r_in_b", f)) \
                    .then_inc(s("eT_ready"), 1)
            act.wait_ge(s("ro1_bias"), 1)
            for f in range(4):
                act.wait_ge(s("ro1_ps"), f + 1)
                nc.scalar.activation(h1[:, 512 + f * P:512 + (f + 1) * P], bank(6 + f % 2, P), ACT.Gelu,
                                     bias=cell("ro1_bias", 4)[:, f:f + 1]).then_inc(s("h1T_ready"), 1)
            for f in range(2):
                act.wait_ge(s("ro2_ps"), f + 1)
                nc.scalar.activation(h1[:, 1024 + f * P:1024 + (f + 1) * P], bank(f % 2, P), ACT.Gelu,
                                     bias=col("r_o2_b", f)).then_inc(s("h2T_ready"), 1)
            for h in range(AH):
                if h % 4 == 0:
                    act.wait_ge(s("smax"), h // 4 + 1)
                if h == 0:
                    act.wait_ge(s("ro3_ps"), 1)
                nc.scalar.activation(h1[:, h * P:(h + 1) * P], score_ps(h), ACT.Exp,
                                     bias=cell("s_negmax", AH)[:, h:h + 1], scale=AD ** -0.5,
                                     accum_out=cell("s_sum", AH)[:, h:h + 1]).then_inc(s("sexp"), 1)
            for g in range(3):
                act.wait_ge(s("pT_ps"), g + 1)
                copy(h2[:, g * 512:(g + 1) * 512], bank(4 + g % 2)).then_inc(s("pT_ready"), 1)
            act.wait_ge(s("oT_ps"), 1)
            o_ps = ps[:, 0:AH * P].rearrange("p (c b n) -> p c b n", b=2, n=P)
            copy(xT[0:AD, :, :], o_ps[0:AD, :, 0, :]).then_inc(s("oT_ready"), 1)
            act.wait_ge(s("hhatT_ps"), 1)
            for c in range(4):
                last = nc.scalar.activation(g2[:, c * P:(c + 1) * P], ps[:, 4 * WIN + c * P:4 * WIN + (c + 1) * P],
                                            ACT.Identity, bias=col("ln2_b", c), scale=col("ln2_g", c))
            last.then_inc(s("xfT_ready"), 1)
            act.wait_ge(s("fc1_ps"), 1)
            nc.scalar.activation(zT[0:MLP, :], bank(6, P, 0, MLP), ACT.Gelu, bias=bias1[0:MLP, 1:2]) \
                .then_inc(s("fc1_ready"), 1)
            half_T(9)
            half_T(10)

        @block.vector
        def _(dve):
            def link(ins):
                chained(dve, "dve_step", ins)

            def normalise(k, dst, src):
                for n in range(2):
                    nc.vector.bn_stats(stats[:, n, :], src[:, n * 384:(n + 1) * 384]).then_inc(S["dve_step"], 1)
                used["dve_step"] += 2
                dve.wait_ge(S["dve_step"], used["dve_step"])
                link(nc.vector.bn_aggr(mv[:], stats[:].rearrange("p a b -> p (a b)")))
                nc.vector.tensor_scalar(var[:], mv[:, 1:2], LN_EPS, None, ALU.add).then_inc(s("var_ready"), 1)
                dve.wait_ge(s("rstd_ready"), k)
                return nc.vector.tensor_scalar(dst, src, mv[:, 0:1], rstd[:], ALU.subtract, ALU.mult)

            def half_T(k):
                dve.wait_ge(s("T_ps"), k)
                nc.vector.tensor_copy(xT[:, 4:6, :], bank(5, 2 * P).rearrange("p (c n) -> p c n", n=P)) \
                    .then_inc(s("T_ready"), 1)

            dve.wait_ge(S["x_in"], 16)
            normalise(1, xn[:], x[:]).then_inc(s("xn_ready"), 1)
            dve.wait_ge(S["graph_in"], 48)
            link(nc.vector.tensor_copy(idxb[:], idx[:]))
            dve.wait_ge(s("constants"), 3)
            iota_rows = iotab.unsqueeze(1).broadcast_to([P, EC, P])
            half_T(1)
            for n, dst in ((0, oh_dst), (1, oh_src[:, 0])):
                nc.vector.tensor_tensor(dst, iota_rows, idxb[:, n, :].unsqueeze(2).broadcast_to([P, EC, P]),
                                        ALU.is_equal).then_inc(s("onehots"), 1)
            dve.wait_ge(s("onehots"), 2)
            dve.wait_ge(s("ew_parts"), 1)
            for k in range(2):
                nc.vector.tensor_tensor(oh_src[:, 1 + k], oh_src[:, 0],
                                        ewb[:, k, :].unsqueeze(2).broadcast_to([P, EC, P]), ALU.mult) \
                    .then_inc(s("ew_rows"), 1)
            dve.wait_ge(s("counted"), 1)
            link(nc.vector.tensor_copy(count[:], bank(3, P)))
            link(nc.vector.tensor_scalar(absent[:], count[:], 1.0, None, ALU.min))
            nc.vector.tensor_scalar(absent[:], absent[:], BIG, -BIG, ALU.mult, ALU.add).then_inc(s("absent_ready"), 1)

            def head_alphas(h, par):
                wait(dve, "h_rows", h + 1)
                dve.wait_ge(S["avec_in"], 16 * h + 16)
                wait(dve, "alpha_ready", h)
                hp = h1[:, par * D:(par + 1) * D]
                nc.vector.tensor_tensor_reduce(g3[:], hp, avec[:, 0:D], 1.0, 0.0, ALU.mult, ALU.add,
                                               alpha[:, par, 0:1]).then_inc(S["alpha_rows"], 1)
                wait(dve, "alpha_rows", h + 1)
                nc.vector.tensor_tensor_reduce(g4[:], hp, avec[:, D:2 * D], 1.0, 0.0, ALU.mult, ALU.add,
                                               alpha[:, par, 1:2]).then_inc(S["alpha_ready"], 1)

            def head_softmax(h, par):
                wait(dve, "score_row_ps", h + 1)
                wait(dve, "attn_ready", h)
                if not isinstance(h, int) or h >= 1:
                    wait(dve, "attnT_ps", h)
                nc.vector.scalar_tensor_tensor(out=att[:, 0, :], in0=bank(7, P, 256), scalar=alpha[:, par, 1:2],
                                               in1=absent[:], op0=ALU.add, op1=ALU.add).then_inc(S["score_sum"], 1)
                wait(dve, "score_sum", h + 1)
                nc.vector.scalar_tensor_tensor(out=att[:, 1, :], in0=att[:, 0, :], scalar=LEAK, in1=att[:, 0, :],
                                               op0=ALU.mult, op1=ALU.max).then_inc(S["score_leaky"], 1)
                wait(dve, "score_leaky", h + 1)
                nc.vector.tensor_reduce(soft[:, 1:2], att[:, 1, :], AX.X, ALU.max, negate=True).then_inc(S["negmax"], 1)
                wait(dve, "exped", h + 1)
                nc.vector.tensor_tensor_reduce(att[:, 1, :], att[:, 0, :], count[:], 1.0, SEG_EPS, ALU.mult, ALU.add,
                                               soft[:, 2:3]).then_inc(S["weighed"], 1)
                wait(dve, "weighed", h + 1)
                nc.vector.reciprocal(soft[:, 3:4], soft[:, 2:3]).then_inc(S["denom_ready"], 1)
                wait(dve, "denom_ready", h + 1)
                nc.vector.tensor_scalar(att[:, 1, :], att[:, 1, :], soft[:, 3:4], None, ALU.mult) \
                    .then_inc(S["attn_ready"], 1)

            def head_elu(h, par):
                wait(dve, "agg_ready", h + 1)
                wait(dve, "elu_ready", h)
                if isinstance(h, int):
                    b1 = cols[:, C * h:C * h + C]
                else:
                    b1 = cols[:, bass.ds(h * C, C)]
                nc.vector.tensor_tensor(g1[:].rearrange("p (c n) -> p c n", n=P),
                                        ps[:, 6 * WIN:6 * WIN + D].rearrange("p (c n) -> p c n", n=P),
                                        b1.unsqueeze(2).broadcast_to([P, C, P]), ALU.add).then_inc(S["z_ready"], 1)
                wait(dve, "z_ready", h + 1)
                nc.vector.tensor_scalar(g2[:], g1[:], 0.0, None, ALU.min).then_inc(S["z_neg"], 1)
                wait(dve, "z_exp", h + 1)
                if not isinstance(h, int) or h >= 2:
                    wait(dve, "w2_used", h - 1)
                nc.vector.scalar_tensor_tensor(out=h2[:, par * D:(par + 1) * D], in0=g2[:], scalar=-1.0, in1=g1[:],
                                               op0=ALU.add, op1=ALU.max).then_inc(S["elu_ready"], 1)

            def step(h, par, last=False):
                head_softmax(h, par)
                if not last:
                    head_alphas(h + 1, 1 - par)
                head_elu(h, par)

            dve.wait_ge(s("absent_ready"), 1)
            head_alphas(0, 0)
            dve.wait_ge(S["small_in"], SMALL)
            step(0, 0)
            step(1, 1)
            step(2, 0)
            with dve.Fori(1, 3) as i:
                step(2 * i + 1, 1)
                step(2 * i + 2, 0)
            step(7, 1, last=True)

            deg, root = cell("degree", 2), cell("deg_root", 2)
            for n, adjT in enumerate((adj1T, adj2T)):
                if n == 0:
                    link(nc.vector.tensor_tensor(att[:, 0, :], count[:], ident, ALU.add))
                else:
                    dve.wait_ge(s("edges_summed"), 1)
                    link(nc.vector.tensor_tensor(att[:, 0, :], bank(3, P, P), ident, ALU.add))
                    link(nc.vector.tensor_tensor(att[:, 0, :], att[:, 0, :], bank(3, P, 2 * P), ALU.add))
                    link(nc.vector.tensor_tensor(att[:, 0, :], att[:, 0, :], bank(3, P, 3 * P), ALU.add))
                nc.vector.tensor_reduce(deg[:, n:n + 1], att[:, 0, :], AX.X, ALU.add).then_inc(s("degree"), 1)
                dve.wait_ge(s("deg_root"), n + 1)
                nc.vector.tensor_scalar(att[:, 1, :], att[:, 0, :], root[:, n:n + 1], None, ALU.mult) \
                    .then_inc(s("adj_half"), 1)
                dve.wait_ge(s("adj_ps"), n + 1)
                nc.vector.tensor_scalar(adjT[:], bank(3, P), root[:, n:n + 1], None, ALU.mult).then_inc(s("adj_ready"), 1)

            head_alphas(8, 0)
            head_softmax(8, 0)

            def add_residual(k, product, base):
                dve.wait_ge(s("rows_ps"), k)
                nc.vector.tensor_tensor(x[:], product, base, ALU.add).then_inc(s("residual"), 1)
                dve.wait_ge(s("residual"), k)

            dve.wait_ge(S["xb_ready"], 1)
            add_residual(1, ps[:, 0:D], xb[:])

            normalise(2, xn[:], x[:]).then_inc(s("xn_ready"), 1)
            half_T(2)

            def grouped(v, groups, n):
                return v.rearrange("p (g n) -> p g n", n=n)

            def wide(v, groups, n):
                return v.unsqueeze(2).broadcast_to([P, groups, n])

            def pick(src, dst, groups, n, shifted=None):
                top, order = tks[:, 1, 0:groups], desc[:, 0:n].unsqueeze(1).broadcast_to([P, groups, n])
                t = grouped(tk[:, 0, 0:groups * n], groups, n)
                link(nc.vector.tensor_reduce(top, src, AX.X, ALU.max))
                if shifted is not None:
                    link(nc.vector.tensor_tensor(shifted, src, wide(top, groups, n), ALU.subtract))
                link(nc.vector.tensor_tensor(t, src, wide(top, groups, n), ALU.is_equal))
                link(nc.vector.tensor_tensor(t, t, order, ALU.mult))
                link(nc.vector.tensor_reduce(top, t, AX.X, ALU.max))
                return nc.vector.tensor_tensor(dst, t, wide(top, groups, n), ALU.is_equal)

            def pick_first(k, logits, groups, n):
                w = groups * n
                pick(grouped(logits, groups, n), grouped(tk[:, 2, 0:w], groups, n), groups, n,
                     grouped(tk[:, 3, 0:w], groups, n)).then_inc(s("top_shifted"), 1)
                dve.wait_ge(s("top_shifted"), k)

            def pick_second(logits, groups, n):
                w = groups * n
                link(nc.vector.scalar_tensor_tensor(out=tk[:, 1, 0:w], in0=tk[:, 2, 0:w], scalar=-BIG, in1=logits,
                                                    op0=ALU.mult, op1=ALU.add))
                link(pick(grouped(tk[:, 1, 0:w], groups, n), grouped(tk[:, 4, 0:w], groups, n), groups, n))
                link(nc.vector.tensor_tensor(tk[:, 2, 0:w], tk[:, 2, 0:w], tk[:, 4, 0:w], ALU.add))

            def top_shares(k, dst, groups, n):
                w = groups * n
                e, top = tk[:, 3, 0:w], tks[:, 1, 0:groups]
                dve.wait_ge(s("top_exped"), k)
                link(nc.vector.tensor_tensor(e, e, tk[:, 2, 0:w], ALU.mult))
                link(nc.vector.tensor_reduce(top, grouped(e, groups, n), AX.X, ALU.add))
                link(nc.vector.reciprocal(top, top))
                link(nc.vector.tensor_tensor(grouped(dst, groups, n), grouped(e, groups, n), wide(top, groups, n), ALU.mult))

            directions = state.rearrange("p (d m) -> p d m", m=16)

            def green_level(lv):
                dve.wait_ge(s("shifted"), lv + 1)
                for d in range(2):
                    own = state[:, 16 * d:16 * d + 16].rearrange("p (a k) -> p a k", k=4)
                    far = bank(7, 16, 16 * d).rearrange("p (k b) -> p b k", b=4)
                    nc.vector.tensor_tensor(prod[:, 64 * d:64 * d + 64].rearrange("p (a b k) -> p a b k", a=4, b=4),
                                            own.unsqueeze(2).broadcast_to([P, 4, 4, 4]),
                                            far.unsqueeze(1).broadcast_to([P, 4, 4, 4]), ALU.mult) \
                        .then_inc(S["dve_step"], 1)
                used["dve_step"] += 2
                dve.wait_ge(S["dve_step"], used["dve_step"])
                last = nc.vector.tensor_reduce(state, prod.rearrange("p (m k) -> p m k", k=4), AX.X, ALU.add)
                if lv == 4:
                    largest = cell("largest", 2)
                    link(last)
                    link(nc.vector.tensor_reduce(largest, directions, AX.X, ALU.max, apply_absolute_value=True))
                    link(nc.vector.reciprocal(largest, largest))
                    last = nc.vector.tensor_tensor(directions, directions, largest.unsqueeze(2).broadcast_to([P, 2, 16]),
                                                   ALU.mult)
                last.then_inc(s("green_state"), 1)

            dve.wait_ge(s("gate_ps"), 1)
            level = cell("level")
            link(nc.vector.tensor_tensor(lin[:, 0:E0 + 1], bank(6, E0 + 1), row("l0_gate"), ALU.add))
            link(nc.vector.tensor_scalar(level, lin[:, E0:E0 + 1], 3.0, -3.0, ALU.min, ALU.max))
            link(nc.vector.tensor_scalar(level, level, -2.0, None, ALU.add))
            dve.wait_ge(s("bk_const"), 12)
            nc.vector.tensor_copy(directions[:, :, 0:6:5], level.unsqueeze(2).broadcast_to([P, 2, 2])) \
                .then_inc(s("green_state"), 1)
            dve.wait_ge(s("constants"), 7)
            pick_first(1, lin[:, 0:E0], 1, E0)
            green_level(0)
            pick_second(lin[:, 0:E0], 1, E0)
            green_level(1)
            top_shares(1, comb[:, 0:E0], 1, E0)
            green_level(2)
            green_level(3)
            dve.wait_ge(s("hid0_mm"), 1)
            nc.vector.tensor_tensor(h1[:, 0:H0], bank(0, H0), row("l0_b1"), ALU.add).then_inc(s("hid0_ready"), 1)
            green_level(4)
            dve.wait_ge(s("spec_in"), 32)
            nc.vector.tensor_tensor(g3[0:11, :], g3[0:11, :], g4[0:11, :], ALU.mult).then_inc(s("tail_ready"), 1)
            green_level(5)
            dve.wait_ge(s("gelu0"), 1)
            nc.vector.tensor_tensor(grouped(h1[:, 0:H0], E0, F0), grouped(h1[:, 0:H0], E0, F0),
                                    wide(comb[:, 0:E0], E0, F0), ALU.mult).then_inc(s("hid0_scaled"), 1)
            green_level(6)
            dve.wait_ge(s("green_state"), 8)
            pq = state[:, 0:16].rearrange("p (m r) -> p m r", r=8)[:, :, 0:2]
            w_blk = state[:, 24:32].rearrange("p (r c) -> p c r", c=4)[:, 0:2, :]
            q_blk = state[:, 8:16].rearrange("p (r c) -> p c r", c=4)[:, 0:2, :]
            r_vec = state[:, 16:18]
            terms, sums, half = cell("terms", 12), cell("sums", 6), cell("half", 2)
            for m in range(2):
                nc.vector.tensor_tensor(terms[:, 4 * m:4 * m + 4].rearrange("p (c r) -> p c r", c=2),
                                        pq[:, m, :].unsqueeze(1).broadcast_to([P, 2, 2]), w_blk, ALU.mult) \
                    .then_inc(S["dve_step"], 1)
            used["dve_step"] += 2
            link(nc.vector.tensor_tensor(terms[:, 8:12].rearrange("p (c r) -> p c r", c=2),
                                         r_vec.unsqueeze(1).broadcast_to([P, 2, 2]), q_blk, ALU.mult))
            link(nc.vector.tensor_reduce(sums, terms.rearrange("p (m r) -> p m r", r=2), AX.X, ALU.add))
            qw, den = sums[:, 2:4], cell("den", 2)
            link(nc.vector.tensor_tensor(half, sums[:, 0:2], sums[:, 4:6], ALU.add))
            link(nc.vector.scalar_tensor_tensor(out=den, in0=qw, scalar=level, in1=half, op0=ALU.mult, op1=ALU.subtract))
            link(nc.vector.tensor_tensor(den[:, 0:1], den[:, 0:1], qw[:, 1:2], ALU.add))
            link(nc.vector.tensor_tensor(den[:, 1:2], den[:, 1:2], qw[:, 0:1], ALU.subtract))
            norm, dot, cross, gre = cell("norm"), cell("dot"), cell("cross"), cell("green", 2)
            link(nc.vector.tensor_tensor_reduce(terms[:, 0:2], den, den, 1.0, 0.0, ALU.mult, ALU.add, norm))
            link(nc.vector.tensor_tensor_reduce(terms[:, 2:4], qw, den, 1.0, 0.0, ALU.mult, ALU.add, dot))
            link(nc.vector.reciprocal(norm, norm))
            link(nc.vector.tensor_tensor(cross, qw[:, 1:2], den[:, 0:1], ALU.mult))
            link(nc.vector.tensor_scalar(gre[:, 0:1], dot, -1.0, None, ALU.mult))
            link(nc.vector.scalar_tensor_tensor(out=gre[:, 1:2], in0=qw[:, 0:1], scalar=den[:, 1:2], in1=cross,
                                                op0=ALU.mult, op1=ALU.subtract))
            link(nc.vector.tensor_scalar(gre, gre, norm, 10.0, ALU.mult, ALU.min))
            nc.vector.tensor_scalar(comb[:, 8:10], gre, -10.0, None, ALU.max).then_inc(s("comb_ready"), 1)
            dve.wait_ge(s("combT_ps"), 1)
            nc.vector.tensor_copy(combT[0:11, :], bank(7, P, 0, 11)).then_inc(s("combT_ready"), 1)
            add_residual(2, ps[:, 2 * WIN:2 * WIN + D], x[:])

            normalise(3, xn[:], x[:]).then_inc(s("xn_ready"), 1)
            half_T(3)
            dve.wait_ge(S["xb_ready"], 2)
            add_residual(3, ps[:, 0:D], xb[:])

            normalise(4, xn[:], x[:]).then_inc(s("xn_ready"), 1)
            half_T(4)
            NG = G1N * E1N
            dve.wait_ge(s("gate_ps"), 2)
            link(nc.vector.tensor_tensor(lin[:, 0:G1N + NG], bank(6, G1N + NG), row("l1_gate"), ALU.add))
            pick_first(2, lin[:, G1N:G1N + NG], G1N, E1N)
            pick_second(lin[:, G1N:G1N + NG], G1N, E1N)
            top_shares(2, comb[:, 0:NG], G1N, E1N)
            pick_first(3, lin[:, 0:G1N], 1, G1N)
            pick_second(lin[:, 0:G1N], 1, G1N)
            top_shares(3, comb[:, 32:36], 1, G1N)
            nc.vector.tensor_tensor(grouped(comb[:, 0:NG], G1N, E1N), grouped(comb[:, 0:NG], G1N, E1N),
                                    wide(comb[:, 32:36], G1N, E1N), ALU.mult).then_inc(s("comb_ready"), 1)
            dve.wait_ge(s("comb_ready"), 2)
            dve.wait_ge(s("in_l1_b1"), 16)

            def hidden_bias(g):
                dve.wait_ge(s("hid1_mm"), g + 1)
                nc.vector.tensor_tensor(h1[:, g * H0:(g + 1) * H0], bank(g, H0), avec[:, g * H0:(g + 1) * H0], ALU.add) \
                    .then_inc(s("hid1_ready"), 1)

            def hidden_scale(g):
                dve.wait_ge(s("gelu1"), g + 1)
                v = grouped(h1[:, g * H0:(g + 1) * H0], E0, F0)
                nc.vector.tensor_tensor(v, v, wide(comb[:, E0 * g:E0 * g + E0], E0, F0), ALU.mult) \
                    .then_inc(s("hid1_scaled"), 1)

            hidden_bias(0)
            dve.wait_ge(s("combT_ps"), 2)
            nc.vector.tensor_copy(combT[:], bank(7, P, 0, 32)).then_inc(s("combT_ready"), 1)
            hidden_bias(1)
            hidden_scale(0)
            hidden_bias(2)
            hidden_scale(1)
            hidden_bias(3)
            hidden_scale(2)
            hidden_scale(3)

            dve.wait_ge(s("in_wout"), 16)
            wait_unit(dve, U_L2)
            w_in = unit(U_L2, "l2_win")
            wabs, worth, winv = cell("w_abs", 2), cell("w_worth", 2), cell("w_inverse", 2)
            nc.vector.tensor_reduce(wabs[:, 0:1], w_in, AX.X, ALU.add, apply_absolute_value=True).then_inc(s("wsum_ready"), 1)
            nc.vector.tensor_reduce(wabs[0:BIT, 1:2], g4[0:BIT, :], AX.X, ALU.add, apply_absolute_value=True) \
                .then_inc(s("wsum_ready"), 1)
            dve.wait_ge(s("wsum_ps"), 1)
            for n, size in enumerate((2 * BIT * D, BIT * D)):
                link(nc.vector.tensor_scalar(worth[:, n:n + 1], bank(7, 1, P + n), 1.0 / size, QUANT_EPS, ALU.mult, ALU.max))
            link(nc.vector.reciprocal(winv, worth))
            link(nc.vector.tensor_scalar(g1[:, 0:384], w_in, winv[:, 0:1], ROUND, ALU.mult, ALU.add))
            link(nc.vector.tensor_scalar(g1[:, 0:384], g1[:, 0:384], ROUND, 1.0, ALU.subtract, ALU.min))
            nc.vector.tensor_scalar(w_in_q, g1[:, 0:384], -1.0, None, ALU.max).then_inc(s("w_quantised"), 1)
            dve.wait_ge(s("w_quantised"), 1)
            link(nc.vector.tensor_scalar(g1[0:BIT, :], g4[0:BIT, :], winv[0:BIT, 1:2], ROUND, ALU.mult, ALU.add))
            link(nc.vector.tensor_scalar(g1[0:BIT, :], g1[0:BIT, :], ROUND, 1.0, ALU.subtract, ALU.min))
            nc.vector.tensor_scalar(w_out_q, g1[0:BIT, :], -1.0, None, ALU.max).then_inc(s("w_quantised"), 1)
            dve.wait_ge(s("w_quantised"), 2)
            add_residual(4, ps[:, 2 * WIN:2 * WIN + D], x[:])

            normalise(5, xn[:], x[:]).then_inc(s("xn_ready"), 1)
            half_T(5)
            dve.wait_ge(s("up_ps"), 1)
            nc.vector.tensor_tensor(g1[:], ps[:, 0:D], xn[:], ALU.add).then_inc(s("node_rows"), 1)
            half_T(6)
            dve.wait_ge(s("gcn_ps"), 1)
            link(nc.vector.tensor_tensor(g2[:, 0:HID2], bank(6, HID2), row("l2_b1"), ALU.add))
            nc.vector.tensor_scalar(g2[:, 0:HID2], g2[:, 0:HID2], 0.0, None, ALU.max).then_inc(s("node_rows"), 1)
            dve.wait_ge(S["xb_ready"], 3)
            add_residual(5, ps[:, 0:D], xb[:])

            normalise(6, xn[:], x[:]).then_inc(s("xn_ready"), 1)
            dve.wait_ge(s("xn_ready"), 6)
            largest, scale, square = cell("act_max"), cell("act_scale"), cell("square")

            def quantise(k, dst, src, gain, n, tmp):
                link(nc.vector.tensor_tensor_reduce(tmp, src, src, 1.0, 0.0, ALU.mult, ALU.add, square))
                nc.vector.tensor_scalar(var[:], square, 1.0 / n, RMS_EPS, ALU.mult, ALU.add).then_inc(s("var_ready"), 1)
                dve.wait_ge(s("rstd_ready"), k)
                link(nc.vector.scalar_tensor_tensor(out=tmp, in0=src, scalar=rstd[:], in1=gain, op0=ALU.mult, op1=ALU.mult))
                link(nc.vector.tensor_reduce(largest, tmp, AX.X, ALU.max, apply_absolute_value=True))
                link(nc.vector.tensor_scalar(largest, largest, QUANT_EPS, None, ALU.max))
                link(nc.vector.reciprocal(scale, largest))
                link(nc.vector.tensor_scalar(scale, scale, 127.0, None, ALU.mult))
                link(nc.vector.tensor_scalar(tmp, tmp, scale, ROUND, ALU.mult, ALU.add))
                link(nc.vector.tensor_scalar(tmp, tmp, ROUND, 127.0, ALU.subtract, ALU.min))
                nc.vector.tensor_scalar(dst, tmp, -128.0, None, ALU.max).then_inc(s("bits_ready"), 1)

            def worth_of(n, dst):
                link(nc.vector.scalar_tensor_tensor(out=dst, in0=largest, scalar=1.0 / 127.0, in1=worth[:, n:n + 1],
                                                    op0=ALU.mult, op1=ALU.mult))

            dve.wait_ge(s("in_g_in"), 16)
            quantise(7, bits, xn[:], row0[:], D, g1[:])
            worth_of(0, cell("unit_in"))
            dve.wait_ge(s("bit_ps"), 1)
            nc.vector.tensor_scalar(g1[:, 0:2 * BIT], bank(6, 2 * BIT), cell("unit_in"), None, ALU.mult).then_inc(s("gated"), 1)
            dve.wait_ge(s("gate_exp"), 1)
            expd, y = g1[:, 2 * BIT:3 * BIT], g1[:, 3 * BIT:4 * BIT]
            link(nc.vector.tensor_scalar(expd, expd, 1.0, None, ALU.add))
            link(nc.vector.reciprocal(expd, expd))
            link(nc.vector.tensor_tensor(y, g1[:, 0:BIT], g1[:, BIT:2 * BIT], ALU.mult))
            link(nc.vector.tensor_tensor(y, y, expd, ALU.mult))
            bits_y = h2[:, 0:BIT // 2].bitcast(BF16)
            quantise(8, bits_y, y, row("g_out"), BIT, g1[:, 4 * BIT:5 * BIT])
            worth_of(1, cell("unit_out"))
            dve.wait_ge(s("bits_ps"), 2)
            nc.vector.tensor_copy(bitsT[0:BIT, 0:P], ps[0:BIT, 4 * WIN:4 * WIN + P // 2].bitcast(BF16)) \
                .then_inc(s("bitsT_ready"), 1)
            dve.wait_ge(s("rows_ps"), 6)
            nc.vector.scalar_tensor_tensor(out=x[:], in0=ps[:, 0:D], scalar=cell("unit_out"), in1=x[:], op0=ALU.mult,
                                           op1=ALU.add).then_inc(s("residual"), 1)
            dve.wait_ge(s("residual"), 6)

            normalise(9, xn[:], x[:]).then_inc(s("xn_ready"), 1)
            half_T(7)
            dve.wait_ge(s("mid_ps"), 1)
            dve.wait_ge(s("in_l3_b1"), 16)
            link(nc.vector.tensor_tensor(g1[:], ps[:, 0:D], avec[:, 0:D], ALU.add))
            nc.vector.tensor_scalar(g1[:], g1[:], 0.0, None, ALU.max).then_inc(s("node_rows"), 1)
            half_T(8)
            dve.wait_ge(S["xb_ready"], 4)
            add_residual(7, ps[:, 2 * WIN:2 * WIN + D], xb[:])

            normalise(10, xn[:], x[:]).then_inc(s("xn_ready"), 1)
            dve.wait_ge(s("xn_ready"), 8)
            normalise(11, g1[:], xn[:]).then_inc(s("zhat_ready"), 1)
            dve.wait_ge(s("zhatT_ps"), 1)
            for c in range(C):
                last = nc.vector.tensor_scalar(xT[:, c, :], ps[:, 4 * WIN + c * P:4 * WIN + (c + 1) * P],
                                               col("r_ln_g", c), col("r_ln_b", c), ALU.mult, ALU.add)
            last.then_inc(s("xrT_ready"), 1)

            def biased_T(dst, ps_at, bias):
                return nc.vector.tensor_tensor(dst.rearrange("p (c n) -> p c n", n=P),
                                               ps[:, ps_at:ps_at + D].rearrange("p (c n) -> p c n", n=P),
                                               bias.unsqueeze(2).broadcast_to([P, C, P]), ALU.add)

            dve.wait_ge(s("eT_ready"), 4)
            gmean = cell("router_mean", 4)
            link(nc.vector.tensor_reduce(gmean, h1[:, 0:512].rearrange("p (f n) -> p f n", n=P)[:, :, 1:P], AX.X, ALU.add))
            nc.vector.tensor_scalar(gmean, gmean, 1.0 / (P - 1), None, ALU.mult).then_inc(s("gmean_ready"), 1)
            dve.wait_ge(s("q_ps"), 1)
            biased_T(g2[:], 2 * WIN, col("bq")).then_inc(s("q_ready"), 1)
            dve.wait_ge(s("ro1g_ps"), 1)
            nc.vector.tensor_tensor(cell("ro1_bias", 4), bank(6, 4), col("r_o1_b"), ALU.add).then_inc(s("ro1_bias"), 1)
            dve.wait_ge(s("k_ps"), 1)
            biased_T(g3[:], 4 * WIN, col("bk")).then_inc(s("k_ready"), 1)
            dve.wait_ge(s("v_ps"), 1)
            dve.wait_ge(s("in_bv"), 16)
            nc.vector.tensor_tensor(g4[:], ps[:, 2 * WIN:2 * WIN + D], avec[:, D:2 * D], ALU.add).then_inc(s("v_ready"), 1)
            dve.wait_ge(s("ro3_ps"), 1)
            lg, bit, nbit, sel = cell("router_logits", 4), cell("bits", 2), cell("not_bits", 2), cell("selected", 3)
            link(nc.vector.tensor_tensor(lg, bank(7, 4), row("r_o3_b"), ALU.add))
            link(nc.vector.tensor_tensor(bit, lg[:, 1:4:2], lg[:, 0:4:2], ALU.is_gt))
            link(nc.vector.memset(bit[0:1, :], 1.0))
            link(nc.vector.tensor_scalar(nbit, bit, -1.0, 1.0, ALU.mult, ALU.add))
            link(nc.vector.tensor_tensor(sel[:, 0:1], nbit[:, 0:1], nbit[:, 1:2], ALU.mult))
            link(nc.vector.tensor_tensor(sel[:, 1:2], nbit[:, 0:1], bit[:, 1:2], ALU.mult))
            nc.vector.tensor_tensor(sel[:, 2:3], bit[:, 0:1], nbit[:, 1:2], ALU.mult).then_inc(s("router_done"), 1)
            negmax, total = cell("s_negmax", AH), cell("s_sum", AH)
            for g in range(3):
                dve.wait_ge(s("s_ps"), g + 1)
                m = negmax[:, 4 * g:4 * g + 4]
                sc = bank(g).rearrange("p (h n) -> p h n", n=P)
                if g == 2:
                    sc = ps[:, 2 * WIN:4 * WIN].rearrange("p (b h n) -> p b h n", b=2, n=P)[:, :, 0:2, :]
                link(nc.vector.tensor_reduce(m, sc, AX.X, ALU.max, negate=True))
                nc.vector.tensor_scalar(m, m, AD ** -0.5, None, ALU.mult).then_inc(s("smax"), 1)
            for g in range(3):
                dve.wait_ge(s("sexp"), 4 * g + 4)
                link(nc.vector.reciprocal(total[:, 4 * g:4 * g + 4], total[:, 4 * g:4 * g + 4]))
                v = h1[:, 512 * g:512 * g + 512].rearrange("p (h n) -> p h n", n=P)
                nc.vector.tensor_tensor(v, v, total[:, 4 * g:4 * g + 4].unsqueeze(2).broadcast_to([P, 4, P]), ALU.mult) \
                    .then_inc(s("p_ready"), 1)
            dve.wait_ge(s("oT_ps"), 1)
            o_ps = ps[:, 0:AH * P].rearrange("p (c b n) -> p c b n", b=2, n=P)
            nc.vector.tensor_copy(xT[AD:P, :, :], o_ps[AD:P, :, 1, :]).then_inc(s("oT_ready"), 1)
            dve.wait_ge(s("wo_ps"), 1)
            dve.wait_ge(s("in_bo"), 16)
            link(nc.vector.tensor_tensor(g3[:], ps[:, 4 * WIN:4 * WIN + D], avec[:, 0:D], ALU.add))
            link(nc.vector.scalar_tensor_tensor(out=g1[:], in0=g3[:], scalar=bit[:, 0:1], in1=xn[:], op0=ALU.mult,
                                                op1=ALU.add))
            normalise(12, g4[:], g1[:]).then_inc(s("hhat_ready"), 1)
            dve.wait_ge(s("hhatT_ps"), 1)
            for c in range(4, C):
                last = nc.vector.tensor_scalar(g2[:, c * P:(c + 1) * P], ps[:, 4 * WIN + c * P:4 * WIN + (c + 1) * P],
                                               col("ln2_g", c), col("ln2_b", c), ALU.mult, ALU.add)
            last.then_inc(s("xfT_ready"), 1)
            dve.wait_ge(s("fc2_ps"), 1)
            nc.vector.scalar_tensor_tensor(out=g3[:], in0=ps[:, 0:D], scalar=bit[:, 1:2], in1=g1[:], op0=ALU.mult,
                                           op1=ALU.add).then_inc(s("out_rows"), 1)
            half_T(9)
            dve.wait_ge(s("rank_ps"), 1)
            for k in range(3):
                last = nc.vector.tensor_scalar(g4[:, 256 * k:256 * k + 256], ps[:, 2 * WIN + 256 * k:2 * WIN + 256 * k + 256],
                                               sel[:, k:k + 1], None, ALU.mult)
            last.then_inc(s("rank_rows"), 1)
            half_T(10)
            dve.wait_ge(s("final_ps"), 1)
            dve.wait_ge(S["xb_ready"], 5)
            nc.vector.tensor_tensor(xb[:], ps[:, 0:D], xb[:], ALU.add).then_inc(s("result_ready"), 1)

        @block.tensor
        def _(pe):
            mm, tr = nc.tensor.matmul, nc.tensor.transpose

            def transpose_rows(k, src):
                for c in range(C):
                    last = tr(ps[:, 4 * WIN + c * P:4 * WIN + (c + 1) * P], src[:, c * P:(c + 1) * P], ident)
                last.then_inc(s("T_ps"), 1)

            def aggregate(k, src, adjT):
                for c in range(C):
                    last = mm(ps[:, 4 * WIN + c * P:4 * WIN + (c + 1) * P], src[:, c * P:(c + 1) * P], adjT[:],
                              start=True, stop=True)
                last.then_inc(s("T_ps"), 1)

            def product(u, name, at, signal):
                pe.wait_ge(s("T_ready"), 2 * used_T[0])
                wait_unit(pe, u)
                w = unit(u, name, "p (c n) -> p c n", c=C)
                for lo, hi in HALVES:
                    for c in range(C):
                        last = mm(ps[:, at + lo:at + hi], xT[:, c, :], w[:, c, lo:hi], start=(c == 0), stop=(c == C - 1))
                last.then_inc(s(signal), 1)

            used_T = [0]

            def head_product(n, par, in_value, after_first=None):
                pe.wait_ge(S[f"w1_in{par}"], in_value)
                if not isinstance(n, int) or n >= 2:
                    pe.wait_ge(S["h_rows"], n - 1)
                w = ring[:, par, :].rearrange("p (c n) -> p c n", c=C)
                at = 0 if par == 0 else WIN + 256
                parts = ((0, WIN), (WIN, D)) if par == 0 else ((256, D), (0, 256))
                for lo, hi in parts:
                    if lo != parts[0][0]:
                        if after_first is not None:
                            after_first()
                        wait(pe, "h_rows", n)
                    for c in range(C):
                        last = mm(ps[:, at + lo:at + hi], xT[:, c, :], w[:, c, lo:hi], start=(c == 0), stop=(c == C - 1))
                return last

            def score_row(h, par):
                wait(pe, "alpha_ready", h + 1)
                wait(pe, "score_sum", h)
                wait(pe, "z_ready", h)
                mm(bank(7, P, 256), alpha[:, par, 0:1].broadcast_to([P, P]), ident, start=True, stop=True) \
                    .then_inc(s("score_row_ps"), 1)

            def turn_attention(h):
                wait(pe, "attn_ready", h + 1)
                wait(pe, "attnT_ready", h)
                tr(bank(7, P, 384), att[:, 1, :], ident).then_inc(S["attnT_ps"], 1)

            def aggregate_head(h, par):
                wait(pe, "attnT_ready", h + 1)
                wait(pe, "h_rows", h + 1)
                wait(pe, "z_ready", h)
                for c in range(C):
                    last = mm(ps[:, 6 * WIN + c * P:6 * WIN + (c + 1) * P], h1[:, par * D + c * P:par * D + (c + 1) * P],
                              attnT[:, par, :], start=True, stop=True)
                last.then_inc(S["agg_ready"], 1)

            def head_second(n, par, in_value, final=False):
                pe.wait_ge(S[f"w2_in{par}"], in_value)
                wait(pe, "elu_ready", n + 1)
                w = ring[:, 2 + par, :].rearrange("p (c n) -> p c n", c=C)
                for c in range(C):
                    for lo, hi in HALVES:
                        last = mm(ps[:, 4 * WIN + lo:4 * WIN + hi], h2[:, par * D + c * P:par * D + (c + 1) * P],
                                  w[:, c, lo:hi], start=False, stop=(final and c == C - 1))
                return last

            def step(h, par, w1_value, w2_value):
                score_row(h, par)
                head_product(h + 1, 1 - par, w1_value, lambda: turn_attention(h)).then_inc(S["hprod"], 1)
                aggregate_head(h, par)
                head_second(h - 1, 1 - par, w2_value).then_inc(S["w2_used"], 1)

            pe.wait_ge(s("constants"), 1)
            pe.wait_ge(s("xn_ready"), 1)
            transpose_rows(1, xn)
            pe.wait_ge(s("T_ready"), 2)
            head_product(0, 0, 16).then_inc(S["hprod"], 1)
            pe.wait_ge(s("constants"), 5)
            for lo, hi in HALVES:
                mm(ps[:, 4 * WIN + lo:4 * WIN + hi], zrow[:], zrow[:, 0:1].broadcast_to([1, hi - lo]), start=True, stop=False)
            pe.wait_ge(s("onehots"), 2)
            for e in range(EC):
                last = mm(bank(3, P), oh_dst[:, e, :], oh_src[:, 0, e, :], start=(e == 0), stop=(e == EC - 1))
            last.then_inc(s("counted"), 1)
            score_row(0, 0)
            head_product(1, 1, 16, lambda: turn_attention(0)).then_inc(S["hprod"], 1)
            aggregate_head(0, 0)
            pe.wait_ge(s("ew_rows"), 3)
            pe.wait_ge(s("absent_ready"), 1)
            for e in range(EC):
                last = mm(bank(3, 3 * P, P), oh_dst[:, e, :], oh_src[:, 1:4, e, :], start=(e == 0), stop=(e == EC - 1))
            last.then_inc(s("edges_summed"), 1)
            step(1, 1, 32, 16)
            step(2, 0, 32, 16)
            with pe.Fori(1, 3) as i:
                step(2 * i + 1, 1, 16 * i + 32, 16 * i + 16)
                step(2 * i + 2, 0, 16 * i + 32, 16 * i + 16)
            score_row(7, 1)
            turn_attention(7)
            head_second(6, 0, 64).then_inc(S["w2_used"], 1)
            aggregate_head(7, 1)
            head_second(7, 1, 64, final=True).then_inc(S["hprod"], 1)
            for n in range(2):
                pe.wait_ge(s("adj_half"), n + 1)
                if n:
                    pe.wait_ge(s("adj_ready"), n)
                tr(bank(3, P), att[:, 1, :], ident).then_inc(s("adj_ps"), 1)
            score_row(8, 0)
            turn_attention(8)
            wait(pe, "attnT_ready", 9)
            wait(pe, "h_rows", 9)
            for lo, hi in HALVES:
                last = mm(ps[:, lo:hi], attnT[:, 0, :], h1[:, lo:hi], start=True, stop=True)
            last.then_inc(s("rows_ps"), 1)

            pe.wait_ge(s("xn_ready"), 2)
            transpose_rows(2, xn)
            pe.wait_ge(s("T_ready"), 4)
            for c in range(C):
                last = mm(bank(6, E0 + 1), xT[:, c, :], gatew[:, c * (E0 + 1):(c + 1) * (E0 + 1)],
                          start=(c == 0), stop=(c == C - 1))
            last.then_inc(s("gate_ps"), 1)

            def shift_green(lv):
                pe.wait_ge(s("green_state"), lv + 1)
                for d, off in enumerate((P - 2 ** lv, P + 2 ** lv)):
                    far = bank(7, 16, 16 * d)
                    mm(far, shiftm[:, off:off + P], state[:, 16 * d:16 * d + 16], start=True, stop=False)
                    last = mm(far, masks[:, off:off + P], ident4, start=False, stop=True)
                last.then_inc(s("shifted"), 1)

            wait_unit(pe, U_L0)
            w = unit(U_L0, "l0_w1", "p (c n) -> p c n", c=C)
            for c in range(C):
                last = mm(bank(0, H0), xT[:, c, :], w[:, c, :], start=(c == 0), stop=(c == C - 1))
                if c == C - 1:
                    last.then_inc(s("hid0_mm"), 1)
                if c == 1:
                    shift_green(0)
                if c == 3:
                    shift_green(1)
            for lv in range(2, 6):
                shift_green(lv)
            pe.wait_ge(s("hid0_scaled"), 1)
            for c in range(3):
                last = tr(ps[:, 4 * WIN + c * P:4 * WIN + (c + 1) * P], h1[:, c * P:(c + 1) * P], ident)
            last.then_inc(s("hid0_ps"), 1)
            shift_green(6)
            pe.wait_ge(s("hid0T"), 1)
            w = unit(U_L0, "l0_w2", "p (c n) -> p c n", c=3)
            for c in range(3):
                for lo, hi in HALVES:
                    last = mm(ps[:, 2 * WIN + lo:2 * WIN + hi], h1[:, H0 + c * P:H0 + (c + 1) * P], w[:, c, lo:hi],
                              start=(c == 0), stop=False)
            last.then_inc(s("l0_weights_used"), 1)
            pe.wait_ge(s("comb_ready"), 1)
            tr(bank(7, P, 0, 11), comb[:, 0:11], ident).then_inc(s("combT_ps"), 1)
            pe.wait_ge(s("combT_ready"), 1)
            pe.wait_ge(s("tail_ready"), 1)
            for lo, hi in HALVES:
                last = mm(ps[:, 2 * WIN + lo:2 * WIN + hi], combT[0:11, :], g3[0:11, lo:hi], start=False, stop=True)
            last.then_inc(s("rows_ps"), 1)

            def graph_product(k, xn_value, adjT, src, u, name, at, signal):
                aggregate(k, src, adjT)
                used_T[0] = k
                product(u, name, at, signal)

            pe.wait_ge(s("adj_ready"), 2)
            pe.wait_ge(s("xn_ready"), 3)
            graph_product(3, 3, adj1T, xn, U_L1, "l1_w", 0, "rows_ps")

            pe.wait_ge(s("xn_ready"), 4)
            transpose_rows(4, xn)
            pe.wait_ge(s("T_ready"), 8)
            n36 = G1N + G1N * E1N
            for c in range(C):
                last = mm(bank(6, n36), xT[:, c, :], gatew1[:, c * n36:(c + 1) * n36], start=(c == 0), stop=(c == C - 1))
            last.then_inc(s("gate_ps"), 1)

            def hidden(g):
                u, name = ((U_L1W1A, "l1f_w1a"), (U_L1W1B, "l1f_w1b"))[g // 2]
                wait_unit(pe, u)
                weights = unit(u, name, "p (c n) -> p c n", c=C)
                lo = (g % 2) * H0
                for c in range(C):
                    last_ = mm(bank(g, H0), xT[:, c, :], weights[:, c, lo:lo + H0], start=(c == 0), stop=(c == C - 1))
                last_.then_inc(s("hid1_mm"), 1)

            def turn_hidden(g):
                pe.wait_ge(s("hid1_scaled"), g + 1)
                if g >= 2:
                    pe.wait_ge(s("hid1T"), g - 1)
                for c in range(3):
                    last_ = tr(bank(4 + g % 2, P, c * P), h1[:, g * H0 + c * P:g * H0 + (c + 1) * P], ident)
                last_.then_inc(s("hid1_ps"), 1)

            def hidden_out(g):
                u, name = ((U_L1W2A, "l1f_w2a"), (U_L1W2B, "l1f_w2b"))[g // 2]
                wait_unit(pe, u)
                pe.wait_ge(s("hid1T"), g + 1)
                weights = unit(u, name, "p (c n) -> p c n", c=C)
                for c in range(3):
                    for lo, hi in HALVES:
                        last_ = mm(ps[:, 2 * WIN + lo:2 * WIN + hi], h2[:, g * H0 + c * P:g * H0 + (c + 1) * P],
                                   weights[:, 3 * (g % 2) + c, lo:hi], start=False, stop=(g == 3 and c == 2))
                return last_

            hidden(0)
            hidden(1)
            pe.wait_ge(s("comb_ready"), 2)
            tr(bank(7, P, 0, 32), comb[:, 0:32], ident).then_inc(s("combT_ps"), 1)
            hidden(2)
            turn_hidden(0)
            hidden(3)
            turn_hidden(1)
            turn_hidden(2)
            pe.wait_ge(s("combT_ready"), 2)
            pe.wait_ge(s("in_b2"), 16)
            for lo, hi in HALVES:
                mm(ps[:, 2 * WIN + lo:2 * WIN + hi], combT[:], g1[0:32, lo:hi], start=True, stop=False)
            hidden_out(0)
            hidden_out(1).then_inc(s("w2a_used"), 1)
            turn_hidden(3)
            hidden_out(2)
            pe.wait_ge(s("wsum_ready"), 2)
            pe.wait_ge(s("constants"), 4)
            mm(bank(7, 1, P), ones[:], cell("w_abs", 2)[:, 0:1], start=True, stop=True)
            mm(bank(7, 1, P + 1), ones[0:BIT, :], cell("w_abs", 2)[0:BIT, 1:2], start=True, stop=True) \
                .then_inc(s("wsum_ps"), 1)
            hidden_out(3).then_inc(s("rows_ps"), 1)

            pe.wait_ge(s("xn_ready"), 5)
            transpose_rows(5, xn)
            pe.wait_ge(s("T_ready"), 10)
            wait_unit(pe, U_L2)
            w = unit(U_L2, "l2_wd", "p (c n) -> p c n", c=C)
            for c in range(C):
                last = mm(bank(6, P, 0, DOWN), w[:, c, :], xT[:, c, :], start=(c == 0), stop=(c == C - 1))
            last.then_inc(s("down_ps"), 1)
            pe.wait_ge(s("down_ready"), 1)
            w = unit(U_L2, "l2_wu")
            for lo, hi in HALVES:
                last = mm(ps[:, lo:hi], zT[0:DOWN + 1, :], w[:, lo:hi], start=True, stop=True)
            last.then_inc(s("up_ps"), 1)
            pe.wait_ge(s("node_rows"), 1)
            aggregate(6, g1, adj2T)
            pe.wait_ge(s("T_ready"), 12)
            w = unit(U_L2, "l2_w1", "p (c n) -> p c n", c=C)
            for c in range(C):
                last = mm(bank(6, HID2), xT[:, c, :], w[:, c, :], start=(c == 0), stop=(c == C - 1))
            last.then_inc(s("gcn_ps"), 1)
            pe.wait_ge(s("node_rows"), 2)
            for c in range(2):
                last = mm(bank(2, P, c * P), g2[:, c * P:(c + 1) * P], adj2T[:], start=True, stop=True)
            last.then_inc(s("rel_ps"), 1)
            pe.wait_ge(s("relT"), 1)
            w = unit(U_L2, "l2_w2", "p (c n) -> p c n", c=2)
            for lo, hi in HALVES:
                for c in range(2):
                    last = mm(ps[:, lo:hi], g3[:, c * P:(c + 1) * P], w[:, c, lo:hi], start=(c == 0), stop=(c == 1))
            last.then_inc(s("rows_ps"), 1)

            pe.wait_ge(s("constants"), 2)
            pe.wait_ge(s("bits_ready"), 1)
            for c in range(C):
                last = tr(ps[:, 4 * WIN + c * P // 2:4 * WIN + (c + 1) * P // 2].bitcast(BF16), bits[:, c * P:(c + 1) * P],
                          identb[:])
            last.then_inc(s("bits_ps"), 1)
            pe.wait_ge(s("bitsT_ready"), 1)
            for c in range(C):
                last = mm(bank(6, 2 * BIT), bitsT[:, c * P:(c + 1) * P], w_in_q[:, c * 2 * BIT:(c + 1) * 2 * BIT],
                          start=(c == 0), stop=(c == C - 1))
            last.then_inc(s("bit_ps"), 1)
            pe.wait_ge(s("bits_ready"), 2)
            tr(ps[0:BIT, 4 * WIN:4 * WIN + P // 2].bitcast(BF16), h2[:, 0:BIT // 2].bitcast(BF16), identb[:]) \
                .then_inc(s("bits_ps"), 1)
            pe.wait_ge(s("bitsT_ready"), 2)
            for lo, hi in HALVES:
                last = mm(ps[:, lo:hi], bitsT[0:BIT, 0:P], w_out_q[:, lo:hi], start=True, stop=True)
            last.then_inc(s("rows_ps"), 1)

            pe.wait_ge(s("xn_ready"), 7)
            graph_product(7, 7, adj1T, xn, U_L3A, "l3_w1", 0, "mid_ps")
            pe.wait_ge(s("node_rows"), 3)
            graph_product(8, 8, adj1T, g1, U_L3B, "l3_w2", 2 * WIN, "rows_ps")

            def product_T(weights, first_bank, outs, operand, signal, emptied=None):
                chunks = weights.shape[1]
                for o in range(outs):
                    if emptied is not None and o >= 2:
                        pe.wait_ge(s(emptied), o - 1)
                    to = ps[:, first_bank * WIN + o * P:first_bank * WIN + (o + 1) * P]
                    if emptied is not None:
                        to = bank(first_bank + o % 2, P)
                    for c in range(chunks):
                        last_ = mm(to, weights[:, c, o * P:(o + 1) * P], operand(c), start=(c == 0), stop=(c == chunks - 1))
                    if emptied is not None or o == outs - 1:
                        last_.then_inc(s(signal), 1)

            pe.wait_ge(s("zhat_ready"), 1)
            for c in range(C):
                last = tr(ps[:, 4 * WIN + c * P:4 * WIN + (c + 1) * P], g1[:, c * P:(c + 1) * P], ident)
            last.then_inc(s("zhatT_ps"), 1)
            wait_unit(pe, U_RIN)
            pe.wait_ge(s("xrT_ready"), 1)
            product_T(unit(U_RIN, "r_in", "p (c n) -> p c n", c=C), 0, 4, lambda c: xT[:, c, :], "rin_ps", emptied="eT_ready")
            wait_unit(pe, U_Q)
            pe.wait_ge(s("xaT_ready"), 1)
            product_T(unit(U_Q, "wq", "p (c n) -> p c n", c=C), 2, C, lambda c: g1[:, c * P:(c + 1) * P], "q_ps")
            wait_unit(pe, U_RO1)
            pe.wait_ge(s("gmean_ready"), 1)
            w = unit(U_RO1, "r_o1", "p (c n) -> p c n", c=8)
            for f in range(4):
                for c in range(4):
                    last = mm(bank(6, 1, f), w[:, 4 + c, f * P:(f + 1) * P], cell("router_mean", 4)[:, c:c + 1],
                              start=(c == 0), stop=(c == 3))
            last.then_inc(s("ro1g_ps"), 1)
            pe.wait_ge(s("ro1_bias"), 1)
            product_T(w[:, 0:4, :], 6, 4, lambda c: h1[:, c * P:(c + 1) * P], "ro1_ps", emptied="h1T_ready")
            wait_unit(pe, U_K)
            product_T(unit(U_K, "wk", "p (c n) -> p c n", c=C), 4, C, lambda c: g1[:, c * P:(c + 1) * P], "k_ps")
            pe.wait_ge(s("h1T_ready"), 4)
            product_T(unit(U_RIN, "r_o2", "p (c n) -> p c n", c=4), 0, 2,
                      lambda c: h1[:, 512 + c * P:512 + (c + 1) * P], "ro2_ps", emptied="h2T_ready")
            wait_unit(pe, U_V)
            pe.wait_ge(s("q_ready"), 1)
            w = unit(U_V, "wv", "p (c n) -> p c n", c=C)
            for lo, hi in HALVES:
                for c in range(C):
                    last = mm(ps[:, 2 * WIN + lo:2 * WIN + hi], g1[:, c * P:(c + 1) * P], w[:, c, lo:hi],
                              start=(c == 0), stop=(c == C - 1))
            last.then_inc(s("v_ps"), 1)
            pe.wait_ge(s("h2T_ready"), 2)
            w = unit(U_RIN, "r_o3", "p (c n) -> p c n", c=2)
            for c in range(2):
                last = mm(bank(7, 4), h1[:, 1024 + c * P:1024 + (c + 1) * P], w[:, c, :], start=(c == 0), stop=(c == 1))
            last.then_inc(s("ro3_ps"), 1)
            pe.wait_ge(s("k_ready"), 1)
            pe.wait_ge(s("v_ready"), 1)
            for h in range(AH):
                r0, c = (h % 2) * AD, h // 2
                last = mm(score_ps(POSITION[h]), g2[r0:r0 + AD, c * P:(c + 1) * P], g3[r0:r0 + AD, c * P:(c + 1) * P],
                          start=True, stop=True)
                if h in (6, 7, 11):
                    last.then_inc(s("s_ps"), 1)
            for g in range(3):
                pe.wait_ge(s("p_ready"), g + 1)
                if g == 2:
                    pe.wait_ge(s("pT_ready"), 1)
                for h in range(4):
                    last = tr(bank(4 + g % 2, P, h * P), h1[:, (4 * g + h) * P:(4 * g + h + 1) * P], ident)
                last.then_inc(s("pT_ps"), 1)
            for at in range(AH):
                h = POSITION.index(at)
                if at % 4 == 0:
                    pe.wait_ge(s("pT_ready"), at // 4 + 1)
                last = mm(ps[:, h * P:(h + 1) * P], g4[:, (h // 2) * P:(h // 2 + 1) * P], h2[:, at * P:(at + 1) * P],
                          start=True, stop=True)
            last.then_inc(s("oT_ps"), 1)
            wait_unit(pe, U_O)
            pe.wait_ge(s("oT_ready"), 2)
            w = unit(U_O, "wo", "p (c n) -> p c n", c=C)
            for lo, hi in HALVES:
                for c in range(C):
                    last = mm(ps[:, 4 * WIN + lo:4 * WIN + hi], xT[:, c, :], w[:, c, lo:hi], start=(c == 0), stop=(c == C - 1))
            last.then_inc(s("wo_ps"), 1)
            pe.wait_ge(s("hhat_ready"), 1)
            for c in range(C):
                last = tr(ps[:, 4 * WIN + c * P:4 * WIN + (c + 1) * P], g4[:, c * P:(c + 1) * P], ident)
            last.then_inc(s("hhatT_ps"), 1)
            pe.wait_ge(s("xfT_ready"), 2)
            w = unit(U_RO1, "fc1", "p (c n) -> p c n", c=C)
            for c in range(C):
                last = mm(bank(6, P, 0, MLP), w[:, c, :], g2[:, c * P:(c + 1) * P], start=(c == 0), stop=(c == C - 1))
            last.then_inc(s("fc1_ps"), 1)
            pe.wait_ge(s("fc1_ready"), 1)
            pe.wait_ge(s("in_fc2"), 16)
            for lo, hi in HALVES:
                last = mm(ps[:, lo:hi], zT[0:MLP + 1, :], row0[0:MLP + 1, lo:hi], start=True, stop=True)
            last.then_inc(s("fc2_ps"), 1)
            pe.wait_ge(s("out_rows"), 1)
            transpose_rows(9, g3)
            used_T[0] = 9
            product(U_DOWN, "down", 2 * WIN, "rank_ps")
            pe.wait_ge(s("rank_rows"), 1)
            transpose_rows(10, g4)
            used_T[0] = 10
            product(U_UP, "up", 0, "final_ps")


def chunked(np, w):
    k, n = w.shape
    return np.ascontiguousarray(w.reshape(k // P, P, n).transpose(1, 0, 2).reshape(P, k // P * n))


def lay_out(np, i):
    a = {"x": i["x"], "edge_weight": i["edge_weight"].reshape(P, EC)}
    a["src"], a["dst"] = i["src"].reshape(P, EC), i["dst"].reshape(P, EC)
    a["gat_w1"] = i["L0_gnn_W1"].reshape(C, P, HEADS1, D).transpose(2, 1, 0, 3).reshape(HEADS1, P, UNIT)
    a["gat_w2"] = i["L0_gnn_W2"].reshape(HEADS1, C, P, D).transpose(0, 2, 1, 3).reshape(HEADS1, P, UNIT)
    a["gat_a"] = np.concatenate([np.concatenate([i["L0_gnn_a_src1"], i["L0_gnn_a_src2"]]),
                                 np.concatenate([i["L0_gnn_a_dst1"], i["L0_gnn_a_dst2"]])], axis=1)
    a["gat_b2"] = i["L0_gnn_b2"]
    a["gatew"] = chunked(np, np.concatenate([i["L0_ffn_gate_w"], i["L0_ffn_v_w"][:, None]], axis=1))
    a["l0_w1"] = chunked(np, i["L0_ffn_w1"].transpose(1, 0, 2).reshape(D, H0))
    a["l0_w2"] = chunked(np, i["L0_ffn_w2"].reshape(H0, D))
    a["l0_tail"] = np.concatenate([i["L0_ffn_b2"], i["L0_ffn_out_w"], i["L0_ffn_out_b"][None]])
    a["bk_scale"] = i["L0_ffn_bk_scale"]
    a["l1_w"] = chunked(np, i["L1_gnn_W"])
    a["l1_b"] = i["L1_gnn_b"]
    a["gatew1"] = chunked(np, np.concatenate([i["L1_ffn_Wg"], i["L1_ffn_Wge"].transpose(1, 0, 2).reshape(D, G1N * E1N)],
                                             axis=1))
    w1 = i["L1_ffn_W1"].transpose(1, 0, 2).reshape(D, H1N)
    a["l1f_w1a"], a["l1f_w1b"] = chunked(np, w1[:, :D]), chunked(np, w1[:, D:])
    w2 = i["L1_ffn_W2"].reshape(H1N, D)
    a["l1f_w2a"], a["l1f_w2b"] = chunked(np, w2[:D]), chunked(np, w2[D:])
    a["l1_b1"] = i["L1_ffn_b1"].reshape(H1N)
    a["l1_b2"] = i["L1_ffn_b2"]
    a["l2_w1"], a["l2_w2"] = chunked(np, i["L2_gnn_W1"]), chunked(np, i["L2_gnn_W2"])
    a["l2_wd"] = chunked(np, i["L2_gnn_Wd"])
    a["l2_wu"] = np.concatenate([i["L2_gnn_Wu"], i["L2_gnn_bu"][None]])
    a["l2_b2"] = i["L2_gnn_b2"]
    a["l2_win"] = chunked(np, i["L2_ffn_w_in"].T)
    a["l2_wout"] = i["L2_ffn_w_out"].T
    a["g_in"] = i["L2_ffn_g_in"]
    a["l3_w1"], a["l3_w2"] = chunked(np, i["L3_gnn_W1"]), chunked(np, i["L3_gnn_W2"])
    a["l3_b1"], a["l3_b2"] = i["L3_gnn_b1"], i["L3_gnn_b2"]
    for name in ("wq", "wk", "wv", "wo"):
        a[name] = chunked(np, i["L3_ffn_" + name].T)
    a["bv"], a["bo"] = i["L3_ffn_bv"], i["L3_ffn_bo"]
    a["r_in"], a["r_o1"] = chunked(np, i["L3_ffn_r_in_w"].T), chunked(np, i["L3_ffn_r_o1_w"].T)
    a["r_o2"], a["r_o3"] = chunked(np, i["L3_ffn_r_o2_w"].T), chunked(np, i["L3_ffn_r_o3_w"].T)
    a["fc1"] = chunked(np, i["L3_ffn_fc1_w"].T)
    a["fc2"] = np.concatenate([i["L3_ffn_fc2_w"].T, i["L3_ffn_fc2_b"][None]])
    a["down"] = chunked(np, i["L3_ffn_lra_down"].reshape(D, D).T)
    a["up"] = chunked(np, i["L3_ffn_lra_up"].transpose(0, 2, 1).reshape(D, D))
    a["bd"], a["fc1_b"] = i["L2_gnn_bd"].reshape(DOWN, 1), i["L3_ffn_fc1_b"].reshape(MLP, 1)
    vectors = [i["L0_gnn_b1"]] + [i["L3_ffn_" + n] for n in ("bq", "bk", "ln1_g", "ln1_b", "r_ln_g", "r_ln_b", "ln2_g",
                                                           "ln2_b", "r_in_b", "r_o1_b", "r_o2_b")]
    a["cols"] = np.concatenate(vectors).reshape(NCOLS, P).T
    a["rows"] = np.concatenate([i["L0_ffn_b1"].reshape(-1), i["L2_gnn_b1"], i["L0_ffn_gate_b"], i["L0_ffn_v_b"].reshape(1),
                                i["L1_ffn_bg"], i["L1_ffn_bge"].reshape(-1), i["L2_ffn_g_out"], i["L3_ffn_r_o3_b"]])
    return {n: np.ascontiguousarray(v) for n, v in a.items()}


def kernel(**inputs):
    import numpy as np
    import concourse.bacc as bacc
    from concourse.bass_utils import run_bass_kernel_spmd

    arrays = lay_out(np, {n: np.asarray(v) for n, v in inputs.items()})
    nc = bacc.Bacc("TRN2", target_bir_lowering=False, num_devices=1)
    a = {n: nc.dram_tensor("in_" + n, v.shape, mybir.dt.from_np(v.dtype), kind="ExternalInput").ap()
         for n, v in arrays.items()}
    out = nc.dram_tensor("out_x", (P, D), F32, kind="ExternalOutput").ap()
    build(nc, a, out)
    r = run_bass_kernel_spmd(nc, [{"in_" + n: v for n, v in arrays.items()}], core_ids=[0])
    return r.results[0]["out_x"]
```

```python
import concourse.bass as bass
from concourse import mybir
from contextlib import ExitStack

F32 = mybir.dt.float32
BF16 = mybir.dt.bfloat16
I32 = mybir.dt.int32
ALU = mybir.AluOpType
ACT = mybir.ActivationFunctionType
AX = mybir.AxisListType

P = 128
D = 768
C = D // P
UNIT = C * D
SLOTS = 8
EDGES = 4224
EC = EDGES // P
HEADS1 = 8
WIN = 512
BIG = 1.0e30
LEAK = 0.2
SEG_EPS = 1e-16
LN_EPS = 1e-5
RMS_EPS = 1e-6
QUANT_EPS = 1e-5
ROUND = 12582912.0
E0, F0 = 8, 48
G1N, E1N = 4, 8
H0 = E0 * F0
H1N = G1N * E1N * F0
DOWN = 24
HID2 = 256
BIT = 32
RHD = 512
AH, AD = 12, 64
MLP = 48

HALVES = ((0, WIN), (WIN, D))

POSITION = [0, 4, 1, 5, 2, 6, 3, 7, 8, 10, 9, 11]

COLS = {}
_at = 0
for _name, _n in (("gat_b1", 48), ("bq", 6), ("bk", 6), ("ln1_g", 6), ("ln1_b", 6), ("r_ln_g", 6),
                  ("r_ln_b", 6), ("ln2_g", 6), ("ln2_b", 6), ("r_in_b", 4), ("r_o1_b", 4), ("r_o2_b", 2)):
    COLS[_name] = (_at, _at + _n)
    _at += _n
NCOLS = _at

ROWS = {}
_at = 0
for _name, _n in (("l0_b1", H0), ("l2_b1", HID2), ("l0_gate", E0 + 1), ("l1_gate", G1N + G1N * E1N),
                  ("g_out", BIT), ("r_o3_b", 4)):
    ROWS[_name] = (_at, _at + _n)
    _at += _n
NROWS = _at

UNITS = [
    [("l0_w1", 0, P, C * H0), ("l0_w2", C * H0, P, 3 * D)],
    [("l1_w", 0, P, UNIT)],
    [("l1f_w1a", 0, P, UNIT)],
    [("l1f_w1b", 0, P, UNIT)],
    [("l1f_w2a", 0, P, UNIT)],
    [("l1f_w2b", 0, P, UNIT)],
    [("l2_w1", 0, P, C * HID2), ("l2_w2", 1536, P, 2 * D), ("l2_win", 3072, P, C * 2 * BIT),
     ("l2_wd", 3456, P, C * DOWN), ("l2_wu", 3600, DOWN + 1, D)],
    [("l3_w1", 0, P, UNIT)],
    [("l3_w2", 0, P, UNIT)],
    [("r_in", 0, P, C * RHD), ("r_o2", 3072, P, 4 * RHD // 2), ("r_o3", 4096, P, 8)],
    [("wq", 0, P, UNIT)],
    [("r_o1", 0, P, 8 * RHD), ("fc1", 8 * RHD, P, C * MLP)],
    [("wk", 0, P, UNIT)],
    [("wv", 0, P, UNIT)],
    [("wo", 0, P, UNIT)],
    [("down", 0, P, UNIT)],
    [("up", 0, P, UNIT)],
]
FIRST_SLOT = 4
(U_L0, U_L1, U_L1W1A, U_L1W1B, U_L1W2A, U_L1W2B, U_L2, U_L3A, U_L3B, U_RIN, U_Q, U_RO1, U_K, U_V,
 U_O, U_DOWN, U_UP) = range(len(UNITS))


def build(nc, a, out):
    ctx = ExitStack()
    with ctx:
        def sb(name, shape, dt=F32):
            return ctx.enter_context(nc.sbuf_tensor(name, shape, dt))

        def sem(name):
            return ctx.enter_context(nc.semaphore(name))

        ring = sb("ring", [P, SLOTS, UNIT])
        x = sb("x", [P, D])
        xb = sb("xb", [P, D])
        xn = sb("xn", [P, D])
        xT = sb("xT", [P, C, P])
        g1 = sb("g1", [P, D])
        g2 = sb("g2", [P, D])
        g3 = sb("g3", [P, D])
        g4 = sb("g4", [P, D])
        h1 = sb("h1", [P, 2 * D])
        h2 = sb("h2", [P, 2 * D])
        avec = sb("avec", [P, 2 * D])
        row0 = sb("row0", [P, D])
        row1 = sb("row1", [P, D])
        rows = sb("rows", [P, NROWS])
        cols = sb("cols", [P, NCOLS])
        shiftm = sb("shiftm", [P, 3 * P])
        count = sb("count", [P, P])
        absent = sb("absent", [P, P])
        adj1T = sb("adj1T", [P, P])
        adj2T = sb("adj2T", [P, P])
        att = sb("att", [P, 2, P])
        attnT = sb("attnT", [P, 2, P])
        alpha = sb("alpha", [P, 2, 2])
        soft = sb("soft", [P, 4])
        stats = sb("stats", [P, 2, 6])
        mv = sb("mv", [P, 2])
        var = sb("var", [P, 1])
        rstd = sb("rstd", [P, 1])
        mhalf = sb("mhalf", [P, 1])
        ones = sb("ones", [P, P])
        zrow = sb("zrow", [1, P])
        gatew = sb("gatew", [P, C * (E0 + 1)])
        gatew1 = sb("gatew1", [P, C * (G1N + G1N * E1N)])
        lin = sb("lin", [P, 40])
        tk = sb("tk", [P, 5, 32])
        tks = sb("tks", [P, 2, 4])
        desc = sb("desc", [P, E1N])
        comb = sb("comb", [P, 44])
        identb = sb("identb", [P, P], BF16)
        combT = sb("combT", [32, P])
        cells = sb("cells", [P, 128])
        bias1 = sb("bias1", [P, 2])
        zT = sb("zT", [64, P])
        idx = sb("idx", [P, 2, EC], I32)
        idxb = sb("idxb", [P, 2, EC], BF16)
        ew = sb("ew", [P, 2, EC])
        ewb = sb("ewb", [P, 3, EC], BF16)

        ps = ctx.enter_context(nc.psum_tensor("ps", [P, 8 * WIN], F32))

        def bank(n, w=WIN, off=0, rows_=P):
            return ps[0:rows_, n * WIN + off:n * WIN + off + w]

        def head_psum(par):
            return ps[:, 0:D] if par == 0 else ps[:, WIN + 256:WIN + 256 + D]

        def score_ps(at):
            return ps[:, at * P:(at + 1) * P] if at < 10 else ps[:, (at + 2) * P:(at + 3) * P]

        ident = shiftm[:, P:2 * P]

        scratch = ring[:, 4:8, :].rearrange("p s n -> p (s n)").bitcast(BF16)
        n1h = EC * P
        oh_dst = scratch[:, 0:n1h].rearrange("p (e n) -> p e n", n=P)
        oh_src = scratch[:, n1h:5 * n1h].rearrange("p (k e n) -> p k e n", k=4, n=P)
        iotab = scratch[:, 5 * n1h:5 * n1h + P]
        iotai = ring[:, 7, UNIT - P:UNIT].bitcast(I32)

        state = h2[:, 384:416]
        prod = h2[:, 512:672]
        w_in_q = g2[:, 256:448].bitcast(BF16)
        w_out_q = g3[0:BIT, 256:640].bitcast(BF16)
        bits = h2[:, 0:384].bitcast(BF16)
        bitsT = h2[:, 384:768].bitcast(BF16)
        SMALL = 16 * 7

        S = {}

        def s(name):
            if name not in S:
                S[name] = sem(name)
            return S[name]

        for name in ("x_in w1_first_in cols_in graph_in small_in avec_in w1_in0 w1_in1 w2_in0 w2_in1 w2_used hprod "
                     "h_rows alpha_ready alpha_rows score_sum score_leaky negmax exped weighed "
                     "denom_ready attn_ready attnT_ps attnT_ready agg_ready z_ready z_neg z_exp elu_ready "
                     "dve_step pool_step act_step out_done").split():
            s(name)
        for n in range(SLOTS):
            s(f"slot{n}_in")

        landed, filled = [], [0] * SLOTS
        for u, parts in enumerate(UNITS):
            slot = (FIRST_SLOT + u) % SLOTS
            filled[slot] += 16 * len(parts)
            landed.append((slot, filled[slot]))

        released = [("l0_weights_used", 1), ("rows_ps", 6), ("hid1_mm", 2), ("hid1_mm", 4), ("w2a_used", 1),
                    ("rows_ps", 8), ("rows_ps", 10), ("mid_ps", 2), ("rows_ps", 14)]

        def unit(u, name, rearr=None, **kw):
            slot = landed[u][0]
            for part, c0, parts, n in UNITS[u]:
                if part == name:
                    v = ring[0:parts, slot, c0:c0 + n]
                    return v.rearrange(rearr, **kw) if rearr else v
            raise KeyError(name)

        def wait_unit(eng, u):
            slot, value = landed[u]
            eng.wait_ge(S[f"slot{slot}_in"], value)

        cell_at = {}

        def cell(name, n=1):
            if name not in cell_at:
                cell_at[name] = sum(w for _, w in cell_at.values()), n
            lo, w = cell_at[name]
            assert w == n and lo + n <= 128
            return cells[:, lo:lo + n]

        def col(name, i=None, n=1):
            lo, hi = COLS[name]
            return cols[:, lo:hi] if i is None else cols[:, lo + i:lo + i + n]

        def row(name):
            lo, hi = ROWS[name]
            return rows[:, lo:hi]

        def wait(eng, name, value):
            if not isinstance(value, int) or value >= 1:
                eng.wait_ge(s(name), value)

        used = {name: 0 for name in ("dve_step", "pool_step", "act_step")}

        def chained(eng, name, ins):
            used[name] += 1
            ins.then_inc(S[name], 1)
            eng.wait_ge(S[name], used[name])

        block = ctx.enter_context(nc.Block())

        def broadcast_row(src, n):
            return src.rearrange("(o n) -> o n", o=1).broadcast_to([P, n])

        @block.sync
        def _(sp):
            def load_avec(h):
                wait(sp, "alpha_ready", h)
                sp.dma_start(avec[:], a["gat_a"][bass.ds(h, 1), :].broadcast_to([P, 2 * D])).then_inc(S["avec_in"], 16)

            def load_w1(h, par):
                if not isinstance(h, int) or h >= 2:
                    sp.wait_ge(S["hprod"], h - 1)
                sp.dma_start(ring[:, par, :], a["gat_w1"][bass.ds(h, 1)].rearrange("o p n -> (o p) n")) \
                    .then_inc(S[f"w1_in{par}"], 16)

            def load_w2(h, par):
                if not isinstance(h, int) or h >= 2:
                    sp.wait_ge(S["w2_used"], h - 1)
                sp.dma_start(ring[:, 2 + par, :], a["gat_w2"][bass.ds(h, 1)].rearrange("o p n -> (o p) n")) \
                    .then_inc(S[f"w2_in{par}"], 16)

            def load_step(h, par):
                load_w1(h + 1, 1 - par)
                load_avec(h)
                load_w2(h - 1, 1 - par)

            def load_unit(u):
                slot = landed[u][0]
                for name, c0, parts, n in UNITS[u]:
                    sp.dma_start(ring[0:parts, slot, c0:c0 + n], a[name]).then_inc(S[f"slot{slot}_in"], 16)

            sp.dma_start(x[:], a["x"]).then_inc(S["x_in"], 16)
            for n, name in enumerate(("dst", "src")):
                sp.dma_start(idx[:, n, :], a[name]).then_inc(S["graph_in"], 16)
            sp.dma_start(ew[:, 0, :], a["edge_weight"]).then_inc(S["graph_in"], 16)
            w1_0 = a["gat_w1"][0:1].rearrange("o p n -> (o p) n")
            sp.dma_start(ring[:, 0, 0:UNIT // 2], w1_0[:, 0:UNIT // 2]).then_inc(S["w1_first_in"], 16)
            sp.dma_start(ring[:, 0, UNIT // 2:UNIT], w1_0[:, UNIT // 2:UNIT]).then_inc(S["w1_in0"], 16)
            sp.dma_start(cols[:], a["cols"]).then_inc(S["cols_in"], 16)
            load_avec(0)
            load_w1(1, 1)
            load_step(1, 1)
            load_step(2, 0)
            with sp.Fori(1, 3) as i:
                load_step(2 * i + 1, 1)
                load_step(2 * i + 2, 0)
            load_avec(7)
            load_w2(6, 0)
            load_w2(7, 1)
            load_avec(8)

            sp.wait_ge(s("edges_summed"), 1)
            for u in range(len(UNITS)):
                if u == 4:
                    sp.wait_ge(S["hprod"], 7)
                if u == 5:
                    sp.wait_ge(S["hprod"], 8)
                if u == 6:
                    sp.wait_ge(S["w2_used"], 7)
                if u == 7:
                    sp.wait_ge(S["hprod"], 9)
                if u >= SLOTS:
                    sp.wait_ge(s(released[u - SLOTS][0]), released[u - SLOTS][1])
                if u - SLOTS == U_L2:
                    sp.wait_ge(s("w_quantised"), 1)
                load_unit(u)
            for n, (lo, hi) in enumerate(HALVES):
                sp.wait_ge(s("result_ready"), n + 1)
                sp.dma_start(out[:, lo:hi], xb[:, lo:hi]).then_inc(S["out_done"], 16)
            sp.wait_ge(S["out_done"], 32)

        @block.gpsimd
        def _(pool):
            def link(ins):
                chained(pool, "pool_step", ins)

            def inverse_root(k):
                pool.wait_ge(s("var_ready"), k)
                pool.tensor_tensor(rstd[:], var[:], mhalf[:], ALU.pow).then_inc(s("rstd_ready"), 1)

            link(pool.memset(mhalf[:], -0.5))
            pool.memset(shiftm[:], 0.0).then_inc(S["pool_step"], 1)
            used["pool_step"] += 1
            pool.wait_ge(S["pool_step"], used["pool_step"])
            pool.affine_select(out=shiftm[:], in_=shiftm[:], compare_op=ALU.not_equal, fill=1.0, base=P,
                               pattern=[[-1, 3 * P]], channel_multiplier=1).then_inc(s("constants"), 1)
            inverse_root(1)
            pool.wait_ge(s("constants"), 1)
            pool.tensor_copy(identb[:], ident).then_inc(s("constants"), 1)
            link(pool.iota(iotai, [[1, P]], base=0, channel_multiplier=0))
            pool.tensor_copy(iotab, iotai).then_inc(s("constants"), 1)
            pool.memset(ones[:], 1.0).then_inc(s("constants"), 1)
            pool.memset(zrow[:], 0.0).then_inc(s("constants"), 1)
            pool.memset(zT[:], 1.0).then_inc(s("constants"), 1)
            steps8 = tk[:, 0, 0:E1N].bitcast(I32)
            link(pool.iota(steps8, [[-1, E1N]], base=E1N, channel_multiplier=0))
            pool.tensor_copy(desc[:], steps8).then_inc(s("constants"), 1)
            pool.wait_ge(S["graph_in"], 48)
            link(pool.tensor_copy(ewb[:, 0, :], ew[:, 0, :]))
            link(pool.tensor_tensor(ew[:, 1, :], ew[:, 0, :], ewb[:, 0, :], ALU.subtract))
            link(pool.tensor_copy(ewb[:, 1, :], ew[:, 1, :]))
            link(pool.tensor_tensor(ew[:, 0, :], ew[:, 1, :], ewb[:, 1, :], ALU.subtract))
            pool.tensor_copy(ewb[:, 2, :], ew[:, 0, :]).then_inc(s("ew_parts"), 1)
            pool.wait_ge(s("ew_parts"), 1)
            pool.wait_ge(s("onehots"), 2)
            for k in range(3):
                pool.tensor_tensor(oh_src[:, 1 + k], oh_src[:, 0], ewb[:, k, :].unsqueeze(2).broadcast_to([P, EC, P]),
                                   ALU.mult).then_inc(s("ew_rows"), 1)

            def residual_bias(k, bias):
                pool.wait_ge(s("residual"), k)
                pool.tensor_tensor(xb[:], x[:], bias, ALU.add).then_inc(s("xb_ready"), 1)

            def load_row(dst, name, n=D):
                pool.dma_start(dst, broadcast_row(a[name], n)).then_inc(s("in_" + name), 16)

            pool.wait_ge(S["small_in"], SMALL)
            pool.wait_ge(S["x_in"], 16)
            pool.tensor_tensor(xb[:], x[:], row0[:], ALU.add).then_inc(s("xb_ready"), 1)
            def inverse_degree_root(n):
                pool.wait_ge(s("degree"), n + 1)
                pool.tensor_tensor(cell("deg_root", 2)[:, n:n + 1], cell("degree", 2)[:, n:n + 1], mhalf[:], ALU.pow) \
                    .then_inc(s("deg_root"), 1)

            inverse_degree_root(0)

            pool.wait_ge(S["elu_ready"], 8)
            link(pool.memset(g1[0:11, :], 1.0))
            pool.dma_start(g1[8:11, :], a["bk_scale"].rearrange("(o n) -> o n", o=1).broadcast_to([3, D])) \
                .then_inc(s("spec_in"), 16)
            pool.dma_start(g2[0:11, :], a["l0_tail"]).then_inc(s("spec_in"), 16)
            pool.wait_ge(S["hprod"], 9)
            link(pool.memset(state, 0.0))
            for d in range(2):
                m = state[:, 16 * d:16 * d + 16]
                pool.memset(m[:, 1:3], -1.0).then_inc(s("bk_const"), 1)
                pool.memset(m[:, 7:8], -1.0).then_inc(s("bk_const"), 1)
                pool.memset(m[:, 4:5], 1.0).then_inc(s("bk_const"), 1)
                pool.memset(m[:, 8:14:5], 1.0).then_inc(s("bk_const"), 1)
            pool.memset(comb[:, 10:11], 1.0).then_inc(s("bk_const"), 1)
            inverse_degree_root(1)
            inverse_root(2)
            pool.wait_ge(s("spec_in"), 32)
            pool.wait_ge(S["alpha_ready"], 9)
            pool.tensor_tensor(g3[0:11, :], g2[0:11, :], g1[0:11, :], ALU.mult).then_inc(s("tail_ready"), 1)
            load_row(avec[:], "l1_b1", 2 * D)
            pool.wait_ge(s("tail_ready"), 1)
            pool.dma_start(g1[0:G1N * E1N, :], a["l1_b2"]).then_inc(s("in_b2"), 16)

            inverse_root(3)
            residual_bias(2, row1[:])
            load_row(row0[:], "g_in")
            pool.dma_start(g4[0:BIT, :], a["l2_wout"]).then_inc(s("in_wout"), 16)
            pool.wait_ge(S["xb_ready"], 2)
            load_row(row1[:], "l2_b2")
            inverse_root(4)

            inverse_root(5)
            pool.wait_ge(s("in_l2_b2"), 16)
            residual_bias(4, row1[:])
            pool.wait_ge(s("hid1_ready"), 4)
            load_row(avec[:, 0:D], "l3_b1")
            load_row(avec[:, D:2 * D], "bv")
            pool.wait_ge(S["xb_ready"], 3)
            load_row(row1[:], "l3_b2")
            for k in (6, 7, 8):
                inverse_root(k)

            inverse_root(9)
            pool.wait_ge(s("in_l3_b2"), 16)
            residual_bias(6, row1[:])
            pool.dma_start(row0[0:MLP + 1, :], a["fc2"]).then_inc(s("in_fc2"), 16)
            for k in (10, 11):
                inverse_root(k)
            load_row(avec[:, 0:D], "bo")
            inverse_root(12)
            pool.wait_ge(s("out_rows"), 2)
            pool.tensor_tensor(xb[:], x[:], g3[:], ALU.add).then_inc(s("xb_ready"), 1)

        @block.scalar
        def _(act):
            def copy(dst, src):
                return nc.scalar.activation(dst, src, ACT.Copy)

            def link(ins):
                chained(act, "act_step", ins)

            def half_T(k):
                act.wait_ge(s("T_ps"), 2 * k - 1)
                copy(xT[:, 0:4, :], bank(4).rearrange("p (c n) -> p c n", n=P)).then_inc(s("T_first_ready"), 1)

            def affine_T(name, value, dst, chunks, vectors, signal):
                act.wait_ge(s(name), value)
                for c in chunks:
                    last = nc.scalar.activation(dst[:, c * P:(c + 1) * P], ps[:, 4 * WIN + c * P:4 * WIN + (c + 1) * P],
                                                ACT.Identity, bias=col(vectors + "_b", c), scale=col(vectors + "_g", c))
                last.then_inc(s(signal), 1)

            def head_rows(h, par):
                wait(act, "hprod", h + 1)
                if not isinstance(h, int) or h >= 2:
                    wait(act, "agg_ready", h - 1)
                    wait(act, "alpha_ready", h - 1)
                copy(h1[:, par * D:(par + 1) * D], head_psum(par)).then_inc(S["h_rows"], 1)

            def head_exp(h):
                wait(act, "negmax", h + 1)
                nc.scalar.activation(att[:, 0, :], att[:, 1, :], ACT.Exp, bias=soft[:, 1:2]) \
                    .then_inc(S["exped"], 1)

            def head_attnT(h, par):
                wait(act, "attnT_ps", h + 1)
                copy(attnT[:, par, :], bank(7, P, 384)).then_inc(S["attnT_ready"], 1)

            def head_elu(h):
                wait(act, "z_neg", h + 1)
                nc.scalar.activation(g2[:], g2[:], ACT.Exp).then_inc(S["z_exp"], 1)

            def step(h, par, last=False):
                head_exp(h)
                head_attnT(h, par)
                if not last:
                    head_rows(h + 1, 1 - par)
                head_elu(h)

            act.wait_ge(s("constants"), 1)
            nc.scalar.activation(cell("scrap"), mhalf[:], ACT.Exp)

            half_T(1)
            head_rows(0, 0)
            step(0, 0)
            step(1, 1)
            act.dma_start(row0[:], broadcast_row(a["gat_b2"], D)).then_inc(S["small_in"], 16)
            act.dma_start(row1[:], broadcast_row(a["l1_b"], D)).then_inc(S["small_in"], 16)
            act.dma_start(rows[:], broadcast_row(a["rows"], NROWS)).then_inc(S["small_in"], 16)
            act.dma_start(gatew[:], a["gatew"]).then_inc(S["small_in"], 16)
            act.dma_start(gatew1[:], a["gatew1"]).then_inc(S["small_in"], 16)
            act.dma_start(bias1[0:DOWN, 0:1], a["bd"]).then_inc(S["small_in"], 16)
            act.dma_start(bias1[0:MLP, 1:2], a["fc1_b"]).then_inc(S["small_in"], 16)
            step(2, 0)
            with act.Fori(1, 3) as i:
                step(2 * i + 1, 1)
                step(2 * i + 2, 0)
            step(7, 1, last=True)
            act.wait_ge(s("gat2_first"), 1)
            copy(h1[:, 0:WIN], bank(4)).then_inc(s("gat2_rows"), 1)
            head_exp(8)
            head_attnT(8, 0)

            half_T(2)
            act.wait_ge(s("top_shifted"), 1)
            nc.scalar.activation(tk[:, 3, 0:E0], tk[:, 3, 0:E0], ACT.Exp).then_inc(s("top_exped"), 1)
            act.wait_ge(s("hid0_ready"), 1)
            nc.scalar.activation(h1[:, 0:H0], h1[:, 0:H0], ACT.Gelu_apprx_tanh).then_inc(s("gelu0"), 1)
            act.wait_ge(s("hid0_ps"), 1)
            copy(h1[:, H0:2 * H0], ps[:, 4 * WIN:4 * WIN + H0]).then_inc(s("hid0T"), 1)

            half_T(3)
            half_T(4)
            act.wait_ge(s("top_shifted"), 2)
            nc.scalar.activation(tk[:, 3, :], tk[:, 3, :], ACT.Exp).then_inc(s("top_exped"), 1)
            act.wait_ge(s("top_shifted"), 3)
            nc.scalar.activation(tk[:, 3, 0:G1N], tk[:, 3, 0:G1N], ACT.Exp).then_inc(s("top_exped"), 1)

            def hidden_gelu(g):
                act.wait_ge(s("hid1_ready"), g + 1)
                nc.scalar.activation(h1[:, g * H0:(g + 1) * H0], h1[:, g * H0:(g + 1) * H0], ACT.Gelu) \
                    .then_inc(s("gelu1"), 1)

            def hidden_T(g):
                act.wait_ge(s("hid1_ps"), g + 1)
                copy(h2[:, g * H0:(g + 1) * H0], bank(4 + g % 2, H0)).then_inc(s("hid1T"), 1)

            hidden_gelu(0)
            hidden_gelu(1)
            hidden_T(0)
            hidden_gelu(2)
            hidden_T(1)
            hidden_gelu(3)
            hidden_T(2)
            hidden_T(3)

            half_T(5)
            act.wait_ge(s("l2_ps"), 1)
            act.wait_ge(s("constants"), 6)
            nc.scalar.activation(zT[0:DOWN, :], bank(6, P, 0, DOWN), ACT.Relu, bias=bias1[0:DOWN, 0:1]) \
                .then_inc(s("l2_copied"), 1)
            half_T(6)
            act.wait_ge(s("l2_ps"), 5)
            copy(g3[:, 0:HID2], bank(2, HID2)).then_inc(s("l2_copied"), 1)
            nc.scalar.activation(cell("scrap"), mhalf[:], ACT.Exp)
            act.wait_ge(s("bits_ps"), 1)
            copy(bitsT, ps[:, 4 * WIN:4 * WIN + D // 2].bitcast(BF16)).then_inc(s("bitsT_ready"), 1)
            act.wait_ge(s("gated"), 1)
            nc.scalar.activation(g1[:, 2 * BIT:3 * BIT], g1[:, BIT:2 * BIT], ACT.Exp, scale=-1.0).then_inc(s("gate_exp"), 1)

            half_T(7)
            half_T(8)

            affine_T("zhatT_ps", 2, xT[:].rearrange("p c n -> p (c n)"), range(4, C), "r_ln", "xrT_ready")
            affine_T("xrT_ready", 2, g1, range(0, 4), "ln1", "xaT_ready")
            for f in range(4):
                act.wait_ge(s("rin_ps"), f + 1)
                nc.scalar.activation(h1[:, f * P:(f + 1) * P], bank(f % 2, P), ACT.Gelu, bias=col("r_in_b", f)) \
                    .then_inc(s("eT_ready"), 1)
            act.wait_ge(s("ro1_bias"), 1)
            for f in range(4):
                act.wait_ge(s("ro1_ps"), f + 1)
                nc.scalar.activation(h1[:, 512 + f * P:512 + (f + 1) * P], bank(6 + f % 2, P), ACT.Gelu,
                                     bias=cell("ro1_bias", 4)[:, f:f + 1]).then_inc(s("h1T_ready"), 1)
            for f in range(2):
                act.wait_ge(s("ro2_ps"), f + 1)
                nc.scalar.activation(h1[:, 1024 + f * P:1024 + (f + 1) * P], bank(f % 2, P), ACT.Gelu,
                                     bias=col("r_o2_b", f)).then_inc(s("h2T_ready"), 1)
            for h in range(AH):
                if h % 4 == 0:
                    act.wait_ge(s("smax"), h // 4 + 1)
                if h == 0:
                    act.wait_ge(s("ro3_ps"), 1)
                nc.scalar.activation(h1[:, h * P:(h + 1) * P], score_ps(h), ACT.Exp,
                                     bias=cell("s_negmax", AH)[:, h:h + 1], scale=AD ** -0.5,
                                     accum_out=cell("s_sum", AH)[:, h:h + 1]).then_inc(s("sexp"), 1)
            for g in range(3):
                act.wait_ge(s("pT_ps"), g + 1)
                copy(h2[:, g * 512:(g + 1) * 512], bank((4, 5, 3)[g])).then_inc(s("pT_ready"), 1)
            o_ps = ps[:, 0:AH * P].rearrange("p (c b n) -> p c b n", b=2, n=P)
            for n, (lo, hi) in enumerate(((0, 4), (4, C))):
                act.wait_ge(s("oT_ps"), n + 1)
                copy(xT[0:AD, lo:hi, :], o_ps[0:AD, lo:hi, 0, :]).then_inc(s("o_even_ready"), 1)
            affine_T("hhatT_ps", 1, g2, range(0, 4), "ln2", "xfT_ready")
            act.wait_ge(s("fc1_ps"), 1)
            nc.scalar.activation(zT[0:MLP, :], bank(6, P, 0, MLP), ACT.Gelu, bias=bias1[0:MLP, 1:2]) \
                .then_inc(s("fc1_ready"), 1)
            half_T(9)
            half_T(10)

        @block.vector
        def _(dve):
            def link(ins):
                chained(dve, "dve_step", ins)

            def statistics(n, src):
                lo, hi = HALVES[n]
                nc.vector.bn_stats(stats[:, n, :], src[:, lo:hi]).then_inc(S["dve_step"], 1)
                used["dve_step"] += 1
                if n == 1:
                    dve.wait_ge(S["dve_step"], used["dve_step"])

            def whiten(k):
                link(nc.vector.bn_aggr(mv[:], stats[:].rearrange("p a b -> p (a b)")))
                nc.vector.tensor_scalar(var[:], mv[:, 1:2], LN_EPS, None, ALU.add).then_inc(s("var_ready"), 1)
                dve.wait_ge(s("rstd_ready"), k)

            def normalise(k, dst, src, signal):
                whiten(k)
                for lo, hi in ((0, D // 2), (D // 2, D)):
                    nc.vector.tensor_scalar(dst[:, lo:hi], src[:, lo:hi], mv[:, 0:1], rstd[:], ALU.subtract, ALU.mult) \
                        .then_inc(s(signal), 1)

            def affine_T(name, value, dst, chunks, vectors, signal):
                dve.wait_ge(s(name), value)
                for c in chunks:
                    last = nc.vector.tensor_scalar(dst[:, c * P:(c + 1) * P], ps[:, 4 * WIN + c * P:4 * WIN + (c + 1) * P],
                                                   col(vectors + "_g", c), col(vectors + "_b", c), ALU.mult, ALU.add)
                last.then_inc(s(signal), 1)

            def half_T(k):
                dve.wait_ge(s("T_ps"), 2 * k)
                nc.vector.tensor_copy(xT[:, 4:6, :], bank(5, 2 * P).rearrange("p (c n) -> p c n", n=P)) \
                    .then_inc(s("T_ready"), 1)

            dve.wait_ge(S["x_in"], 16)
            for n in range(2):
                statistics(n, x)
            normalise(1, xn, x, "xn_ready")
            dve.wait_ge(S["graph_in"], 48)
            link(nc.vector.tensor_copy(idxb[:], idx[:]))
            dve.wait_ge(s("constants"), 3)
            iota_rows = iotab.unsqueeze(1).broadcast_to([P, EC, P])
            half_T(1)
            for n, dst in ((0, oh_dst), (1, oh_src[:, 0])):
                nc.vector.tensor_tensor(dst, iota_rows, idxb[:, n, :].unsqueeze(2).broadcast_to([P, EC, P]),
                                        ALU.is_equal).then_inc(s("onehots"), 1)
            def head_alphas(h, par):
                wait(dve, "h_rows", h + 1)
                dve.wait_ge(S["avec_in"], 16 * h + 16)
                wait(dve, "alpha_ready", h)
                hp = h1[:, par * D:(par + 1) * D]
                nc.vector.tensor_tensor_reduce(g3[:], hp, avec[:, 0:D], 1.0, 0.0, ALU.mult, ALU.add,
                                               alpha[:, par, 0:1]).then_inc(S["alpha_rows"], 1)
                wait(dve, "alpha_rows", h + 1)
                nc.vector.tensor_tensor_reduce(g4[:], hp, avec[:, D:2 * D], 1.0, 0.0, ALU.mult, ALU.add,
                                               alpha[:, par, 1:2]).then_inc(S["alpha_ready"], 1)

            def head_softmax(h, par):
                wait(dve, "score_row_ps", h + 1)
                wait(dve, "attn_ready", h)
                if not isinstance(h, int) or h >= 1:
                    wait(dve, "attnT_ps", h)
                nc.vector.scalar_tensor_tensor(out=att[:, 0, :], in0=bank(7, P, 256), scalar=alpha[:, par, 1:2],
                                               in1=absent[:], op0=ALU.add, op1=ALU.add).then_inc(S["score_sum"], 1)
                wait(dve, "score_sum", h + 1)
                nc.vector.scalar_tensor_tensor(out=att[:, 1, :], in0=att[:, 0, :], scalar=LEAK, in1=att[:, 0, :],
                                               op0=ALU.mult, op1=ALU.max).then_inc(S["score_leaky"], 1)
                wait(dve, "score_leaky", h + 1)
                nc.vector.tensor_reduce(soft[:, 1:2], att[:, 1, :], AX.X, ALU.max, negate=True).then_inc(S["negmax"], 1)
                wait(dve, "exped", h + 1)
                nc.vector.tensor_tensor_reduce(att[:, 1, :], att[:, 0, :], count[:], 1.0, SEG_EPS, ALU.mult, ALU.add,
                                               soft[:, 2:3]).then_inc(S["weighed"], 1)
                wait(dve, "weighed", h + 1)
                nc.vector.reciprocal(soft[:, 3:4], soft[:, 2:3]).then_inc(S["denom_ready"], 1)
                wait(dve, "denom_ready", h + 1)
                nc.vector.tensor_scalar(att[:, 1, :], att[:, 1, :], soft[:, 3:4], None, ALU.mult) \
                    .then_inc(S["attn_ready"], 1)

            def head_elu(h, par):
                wait(dve, "agg_ready", h + 1)
                wait(dve, "elu_ready", h)
                if isinstance(h, int):
                    b1 = cols[:, C * h:C * h + C]
                else:
                    b1 = cols[:, bass.ds(h * C, C)]
                nc.vector.tensor_tensor(g1[:].rearrange("p (c n) -> p c n", n=P),
                                        ps[:, 6 * WIN:6 * WIN + D].rearrange("p (c n) -> p c n", n=P),
                                        b1.unsqueeze(2).broadcast_to([P, C, P]), ALU.add).then_inc(S["z_ready"], 1)
                wait(dve, "z_ready", h + 1)
                nc.vector.tensor_scalar(g2[:], g1[:], 0.0, None, ALU.min).then_inc(S["z_neg"], 1)
                wait(dve, "z_exp", h + 1)
                if not isinstance(h, int) or h >= 2:
                    wait(dve, "w2_used", h - 1)
                nc.vector.scalar_tensor_tensor(out=h2[:, par * D:(par + 1) * D], in0=g2[:], scalar=-1.0, in1=g1[:],
                                               op0=ALU.add, op1=ALU.max).then_inc(S["elu_ready"], 1)

            def step(h, par, last=False):
                head_softmax(h, par)
                if not last:
                    head_alphas(h + 1, 1 - par)
                head_elu(h, par)

            deg, root = cell("degree", 2), cell("deg_root", 2)

            def half_adjacency(n, adjT):
                nc.vector.tensor_reduce(deg[:, n:n + 1], adjT[:], AX.X, ALU.add).then_inc(s("degree"), 1)
                dve.wait_ge(s("deg_root"), n + 1)
                nc.vector.tensor_scalar(adjT[:], adjT[:], root[:, n:n + 1], None, ALU.mult).then_inc(s("adj_half"), 1)

            def whole_adjacency(n, adjT):
                dve.wait_ge(s("adj_ps"), n + 1)
                nc.vector.tensor_scalar(adjT[:], bank(3, P), root[:, n:n + 1], None, ALU.mult).then_inc(s("adj_ready"), 1)

            dve.wait_ge(s("onehots"), 2)
            head_alphas(0, 0)
            dve.wait_ge(s("counted"), 1)
            link(nc.vector.tensor_copy(count[:], bank(3, P)))
            link(nc.vector.tensor_scalar(absent[:], count[:], 1.0, None, ALU.min))
            link(nc.vector.tensor_scalar(absent[:], absent[:], BIG, -BIG, ALU.mult, ALU.add))
            dve.wait_ge(S["cols_in"], 16)
            step(0, 0)
            step(1, 1)
            step(2, 0)
            missing = cell("missing", 14)
            for lv in range(7):
                for d, off in enumerate((P + 2 ** lv, P - 2 ** lv)):
                    last = nc.vector.tensor_reduce(missing[:, 2 * lv + d:2 * lv + d + 1], shiftm[:, off:off + P], AX.X, ALU.add)
            link(last)
            link(nc.vector.tensor_scalar(missing, missing, -1.0, 1.0, ALU.mult, ALU.add))
            link(nc.vector.tensor_tensor(adj1T[:], count[:], ident, ALU.add))
            half_adjacency(0, adj1T)
            whole_adjacency(0, adj1T)
            with dve.Fori(1, 3) as i:
                step(2 * i + 1, 1)
                step(2 * i + 2, 0)
            step(7, 1, last=True)

            dve.wait_ge(S["hprod"], 9)
            nc.vector.tensor_copy(h1[:, WIN:D], bank(5, D - WIN)).then_inc(S["h_rows"], 1)
            dve.wait_ge(s("gat2_rows"), 1)
            head_alphas(8, 0)
            head_softmax(8, 0)

            dve.wait_ge(s("edges_summed"), 1)
            link(nc.vector.tensor_tensor(adj2T[:], bank(3, P, P), ident, ALU.add))
            link(nc.vector.tensor_tensor(adj2T[:], adj2T[:], bank(3, P, 2 * P), ALU.add))
            link(nc.vector.tensor_tensor(adj2T[:], adj2T[:], bank(3, P, 3 * P), ALU.add))
            half_adjacency(1, adj2T)

            def add_residual(k, at, base, worth_each=None):
                for n, (lo, hi) in enumerate(HALVES):
                    dve.wait_ge(s("rows_ps"), 2 * k - 1 + n)
                    part = ps[:, at + lo:at + hi]
                    if worth_each is None:
                        ins = nc.vector.tensor_tensor(x[:, lo:hi], part, base[:, lo:hi], ALU.add)
                    else:
                        ins = nc.vector.scalar_tensor_tensor(out=x[:, lo:hi], in0=part, scalar=worth_each, in1=base[:, lo:hi],
                                                             op0=ALU.mult, op1=ALU.add)
                    if n == 0:
                        link(ins)
                    else:
                        ins.then_inc(s("residual"), 1)
                        dve.wait_ge(s("residual"), k)
                    statistics(n, x)

            dve.wait_ge(S["xb_ready"], 1)
            add_residual(1, 0, xb)

            normalise(2, xn, x, "xn_ready")
            half_T(2)
            whole_adjacency(1, adj2T)

            def grouped(v, groups, n):
                return v.rearrange("p (g n) -> p g n", n=n)

            def wide(v, groups, n):
                return v.unsqueeze(2).broadcast_to([P, groups, n])

            def pick(src, dst, groups, n, shifted=None):
                top, order = tks[:, 1, 0:groups], desc[:, 0:n].unsqueeze(1).broadcast_to([P, groups, n])
                t = grouped(tk[:, 0, 0:groups * n], groups, n)
                link(nc.vector.tensor_reduce(top, src, AX.X, ALU.max))
                if shifted is not None:
                    link(nc.vector.tensor_tensor(shifted, src, wide(top, groups, n), ALU.subtract))
                link(nc.vector.tensor_tensor(t, src, wide(top, groups, n), ALU.is_equal))
                link(nc.vector.tensor_tensor(t, t, order, ALU.mult))
                link(nc.vector.tensor_reduce(top, t, AX.X, ALU.max))
                return nc.vector.tensor_tensor(dst, t, wide(top, groups, n), ALU.is_equal)

            def pick_first(k, logits, groups, n):
                w = groups * n
                pick(grouped(logits, groups, n), grouped(tk[:, 2, 0:w], groups, n), groups, n,
                     grouped(tk[:, 3, 0:w], groups, n)).then_inc(s("top_shifted"), 1)
                dve.wait_ge(s("top_shifted"), k)

            def pick_second(logits, groups, n):
                w = groups * n
                link(nc.vector.scalar_tensor_tensor(out=tk[:, 1, 0:w], in0=tk[:, 2, 0:w], scalar=-BIG, in1=logits,
                                                    op0=ALU.mult, op1=ALU.add))
                link(pick(grouped(tk[:, 1, 0:w], groups, n), grouped(tk[:, 4, 0:w], groups, n), groups, n))
                link(nc.vector.tensor_tensor(tk[:, 2, 0:w], tk[:, 2, 0:w], tk[:, 4, 0:w], ALU.add))

            def top_shares(k, dst, groups, n):
                w = groups * n
                e, top = tk[:, 3, 0:w], tks[:, 1, 0:groups]
                dve.wait_ge(s("top_exped"), k)
                link(nc.vector.tensor_tensor(e, e, tk[:, 2, 0:w], ALU.mult))
                link(nc.vector.tensor_reduce(top, grouped(e, groups, n), AX.X, ALU.add))
                link(nc.vector.reciprocal(top, top))
                link(nc.vector.tensor_tensor(grouped(dst, groups, n), grouped(e, groups, n), wide(top, groups, n), ALU.mult))

            directions = state.rearrange("p (d m) -> p d m", m=16)

            def green_level(lv):
                dve.wait_ge(s("green_state"), lv + 1)
                nc.vector.tensor_tensor(prod.rearrange("p (d m k) -> p d m k", d=2, k=5)[:, :, :, 4], directions,
                                        missing[:, 2 * lv:2 * lv + 2].unsqueeze(2).broadcast_to([P, 2, 16]), ALU.mult) \
                    .then_inc(S["dve_step"], 1)
                used["dve_step"] += 1
                dve.wait_ge(s("shifted"), lv + 1)
                for d in range(2):
                    own = state[:, 16 * d:16 * d + 16].rearrange("p (a k) -> p a k", k=4)
                    far = bank(7, 16, 16 * d).rearrange("p (k b) -> p b k", b=4)
                    nc.vector.tensor_tensor(prod[:, 80 * d:80 * d + 80].rearrange("p (a b k) -> p a b k", a=4, k=5)[:, :, :, 0:4],
                                            own.unsqueeze(2).broadcast_to([P, 4, 4, 4]),
                                            far.unsqueeze(1).broadcast_to([P, 4, 4, 4]), ALU.mult) \
                        .then_inc(S["dve_step"], 1)
                used["dve_step"] += 2
                dve.wait_ge(S["dve_step"], used["dve_step"])
                last = nc.vector.tensor_reduce(state, prod.rearrange("p (m k) -> p m k", k=5), AX.X, ALU.add)
                if lv == 4:
                    largest = cell("largest", 2)
                    link(last)
                    link(nc.vector.tensor_reduce(largest, directions, AX.X, ALU.max, apply_absolute_value=True))
                    link(nc.vector.reciprocal(largest, largest))
                    last = nc.vector.tensor_tensor(directions, directions, largest.unsqueeze(2).broadcast_to([P, 2, 16]),
                                                   ALU.mult)
                last.then_inc(s("green_state"), 1)

            dve.wait_ge(s("gate_ps"), 1)
            level = cell("level")
            link(nc.vector.tensor_tensor(lin[:, 0:E0 + 1], bank(6, E0 + 1), row("l0_gate"), ALU.add))
            link(nc.vector.tensor_scalar(level, lin[:, E0:E0 + 1], 3.0, -3.0, ALU.min, ALU.max))
            link(nc.vector.tensor_scalar(level, level, -2.0, None, ALU.add))
            dve.wait_ge(s("bk_const"), 9)
            nc.vector.tensor_copy(directions[:, :, 0:6:5], level.unsqueeze(2).broadcast_to([P, 2, 2])) \
                .then_inc(s("green_state"), 1)
            dve.wait_ge(s("constants"), 7)
            pick_first(1, lin[:, 0:E0], 1, E0)
            green_level(0)
            pick_second(lin[:, 0:E0], 1, E0)
            green_level(1)
            top_shares(1, comb[:, 0:E0], 1, E0)
            green_level(2)
            dve.wait_ge(s("hid0_mm"), 1)
            nc.vector.tensor_tensor(h1[:, 0:H0], bank(0, H0), row("l0_b1"), ALU.add).then_inc(s("hid0_ready"), 1)
            green_level(3)
            dve.wait_ge(s("gelu0"), 1)
            nc.vector.tensor_tensor(grouped(h1[:, 0:H0], E0, F0), grouped(h1[:, 0:H0], E0, F0),
                                    wide(comb[:, 0:E0], E0, F0), ALU.mult).then_inc(s("hid0_scaled"), 1)
            for lv in range(4, 7):
                green_level(lv)
            dve.wait_ge(s("green_state"), 8)
            pq = state[:, 0:16].rearrange("p (m r) -> p m r", r=8)[:, :, 0:2]
            w_blk = state[:, 24:32].rearrange("p (r c) -> p c r", c=4)[:, 0:2, :]
            q_blk = state[:, 8:16].rearrange("p (r c) -> p c r", c=4)[:, 0:2, :]
            r_vec = state[:, 16:18]
            terms, sums, half = cell("terms", 12), cell("sums", 6), cell("half", 2)
            for m in range(2):
                nc.vector.tensor_tensor(terms[:, 4 * m:4 * m + 4].rearrange("p (c r) -> p c r", c=2),
                                        pq[:, m, :].unsqueeze(1).broadcast_to([P, 2, 2]), w_blk, ALU.mult) \
                    .then_inc(S["dve_step"], 1)
            used["dve_step"] += 2
            link(nc.vector.tensor_tensor(terms[:, 8:12].rearrange("p (c r) -> p c r", c=2),
                                         r_vec.unsqueeze(1).broadcast_to([P, 2, 2]), q_blk, ALU.mult))
            link(nc.vector.tensor_reduce(sums, terms.rearrange("p (m r) -> p m r", r=2), AX.X, ALU.add))
            qw, den = sums[:, 2:4], cell("den", 2)
            link(nc.vector.tensor_tensor(half, sums[:, 0:2], sums[:, 4:6], ALU.add))
            link(nc.vector.scalar_tensor_tensor(out=den, in0=qw, scalar=level, in1=half, op0=ALU.mult, op1=ALU.subtract))
            link(nc.vector.tensor_tensor(den[:, 0:1], den[:, 0:1], qw[:, 1:2], ALU.add))
            link(nc.vector.tensor_tensor(den[:, 1:2], den[:, 1:2], qw[:, 0:1], ALU.subtract))
            norm, dot, cross, gre = cell("norm"), cell("dot"), cell("cross"), cell("green", 2)
            link(nc.vector.tensor_tensor_reduce(terms[:, 0:2], den, den, 1.0, 0.0, ALU.mult, ALU.add, norm))
            link(nc.vector.tensor_tensor_reduce(terms[:, 2:4], qw, den, 1.0, 0.0, ALU.mult, ALU.add, dot))
            link(nc.vector.reciprocal(norm, norm))
            link(nc.vector.tensor_tensor(cross, qw[:, 1:2], den[:, 0:1], ALU.mult))
            link(nc.vector.tensor_scalar(gre[:, 0:1], dot, -1.0, None, ALU.mult))
            link(nc.vector.scalar_tensor_tensor(out=gre[:, 1:2], in0=qw[:, 0:1], scalar=den[:, 1:2], in1=cross,
                                                op0=ALU.mult, op1=ALU.subtract))
            link(nc.vector.tensor_scalar(gre, gre, norm, 10.0, ALU.mult, ALU.min))
            nc.vector.tensor_scalar(comb[:, 8:10], gre, -10.0, None, ALU.max).then_inc(s("comb_ready"), 1)
            dve.wait_ge(s("combT_ps"), 1)
            nc.vector.tensor_copy(combT[0:11, :], bank(7, P, 0, 11)).then_inc(s("combT_ready"), 1)
            add_residual(2, 2 * WIN, x)

            normalise(3, xn, x, "xn_ready")
            half_T(3)
            dve.wait_ge(S["xb_ready"], 2)
            add_residual(3, 0, xb)

            normalise(4, xn, x, "xn_ready")
            half_T(4)
            NG = G1N * E1N
            dve.wait_ge(s("gate_ps"), 2)
            link(nc.vector.tensor_tensor(lin[:, 0:G1N + NG], bank(6, G1N + NG), row("l1_gate"), ALU.add))
            pick_first(2, lin[:, G1N:G1N + NG], G1N, E1N)
            pick_second(lin[:, G1N:G1N + NG], G1N, E1N)
            top_shares(2, comb[:, 0:NG], G1N, E1N)
            pick_first(3, lin[:, 0:G1N], 1, G1N)
            pick_second(lin[:, 0:G1N], 1, G1N)
            top_shares(3, comb[:, 32:36], 1, G1N)
            nc.vector.tensor_tensor(grouped(comb[:, 0:NG], G1N, E1N), grouped(comb[:, 0:NG], G1N, E1N),
                                    wide(comb[:, 32:36], G1N, E1N), ALU.mult).then_inc(s("comb_ready"), 1)
            dve.wait_ge(s("comb_ready"), 2)
            dve.wait_ge(s("in_l1_b1"), 16)

            def hidden_bias(g):
                dve.wait_ge(s("hid1_mm"), g + 1)
                nc.vector.tensor_tensor(h1[:, g * H0:(g + 1) * H0], bank(g, H0), avec[:, g * H0:(g + 1) * H0], ALU.add) \
                    .then_inc(s("hid1_ready"), 1)

            def hidden_scale(g):
                dve.wait_ge(s("gelu1"), g + 1)
                v = grouped(h1[:, g * H0:(g + 1) * H0], E0, F0)
                nc.vector.tensor_tensor(v, v, wide(comb[:, E0 * g:E0 * g + E0], E0, F0), ALU.mult) \
                    .then_inc(s("hid1_scaled"), 1)

            hidden_bias(0)
            dve.wait_ge(s("combT_ps"), 2)
            nc.vector.tensor_copy(combT[:], bank(7, P, 0, 32)).then_inc(s("combT_ready"), 1)
            hidden_bias(1)
            hidden_scale(0)
            hidden_bias(2)
            hidden_scale(1)
            hidden_bias(3)
            hidden_scale(2)
            hidden_scale(3)

            dve.wait_ge(s("in_wout"), 16)
            wait_unit(dve, U_L2)
            w_in = unit(U_L2, "l2_win")
            wabs, worth, winv = cell("w_abs", 2), cell("w_worth", 2), cell("w_inverse", 2)
            nc.vector.tensor_reduce(wabs[:, 0:1], w_in, AX.X, ALU.add, apply_absolute_value=True).then_inc(s("wsum_ready"), 1)
            nc.vector.tensor_reduce(wabs[0:BIT, 1:2], g4[0:BIT, :], AX.X, ALU.add, apply_absolute_value=True) \
                .then_inc(s("wsum_ready"), 1)
            dve.wait_ge(s("wsum_ps"), 1)
            for n, size in enumerate((2 * BIT * D, BIT * D)):
                link(nc.vector.tensor_scalar(worth[:, n:n + 1], bank(7, 1, P + n), 1.0 / size, QUANT_EPS, ALU.mult, ALU.max))
            link(nc.vector.reciprocal(winv, worth))
            link(nc.vector.tensor_scalar(g1[:, 0:384], w_in, winv[:, 0:1], ROUND, ALU.mult, ALU.add))
            link(nc.vector.tensor_scalar(g1[:, 0:384], g1[:, 0:384], ROUND, 1.0, ALU.subtract, ALU.min))
            nc.vector.tensor_scalar(w_in_q, g1[:, 0:384], -1.0, None, ALU.max).then_inc(s("w_quantised"), 1)
            dve.wait_ge(s("w_quantised"), 1)
            link(nc.vector.tensor_scalar(g1[0:BIT, :], g4[0:BIT, :], winv[0:BIT, 1:2], ROUND, ALU.mult, ALU.add))
            link(nc.vector.tensor_scalar(g1[0:BIT, :], g1[0:BIT, :], ROUND, 1.0, ALU.subtract, ALU.min))
            nc.vector.tensor_scalar(w_out_q, g1[0:BIT, :], -1.0, None, ALU.max).then_inc(s("w_quantised"), 1)
            dve.wait_ge(s("w_quantised"), 2)
            add_residual(4, 0, x)

            normalise(5, xn, x, "xn_ready")
            half_T(5)
            for n, (lo, hi) in enumerate(HALVES):
                dve.wait_ge(s("l2_ps"), n + 2)
                nc.vector.tensor_tensor(g1[:, lo:hi], ps[:, lo:hi], xn[:, lo:hi], ALU.add).then_inc(s("node_rows"), 1)
            half_T(6)
            dve.wait_ge(s("l2_ps"), 4)
            link(nc.vector.tensor_tensor(g2[:, 0:HID2], bank(6, HID2), row("l2_b1"), ALU.add))
            nc.vector.tensor_scalar(g2[:, 0:HID2], g2[:, 0:HID2], 0.0, None, ALU.max).then_inc(s("node_rows"), 1)
            dve.wait_ge(S["xb_ready"], 3)
            add_residual(5, 0, xb)

            largest, scale, square, root2 = cell("act_max"), cell("act_scale"), cell("square"), cell("root2", 2)
            link(nc.vector.bn_aggr(mv[:], stats[:].rearrange("p a b -> p (a b)")))
            nc.vector.tensor_scalar(var[:], mv[:, 1:2], LN_EPS, None, ALU.add).then_inc(s("var_ready"), 1)
            dve.wait_ge(s("in_g_in"), 16)
            nc.vector.scalar_tensor_tensor(out=g1[:], in0=x[:], scalar=mv[:, 0:1], in1=row0[:], op0=ALU.subtract,
                                           op1=ALU.mult).then_inc(S["dve_step"], 1)
            used["dve_step"] += 1
            dve.wait_ge(s("rstd_ready"), 6)
            link(nc.vector.tensor_copy(root2[:, 0:1], rstd[:]))
            link(nc.vector.scalar_tensor_tensor(out=square, in0=rstd[:], scalar=root2[:, 0:1], in1=mv[:, 1:2],
                                                op0=ALU.mult, op1=ALU.mult))
            nc.vector.tensor_scalar(var[:], square, RMS_EPS, None, ALU.add).then_inc(s("var_ready"), 1)
            link(nc.vector.tensor_reduce(largest, g1[:], AX.X, ALU.max, apply_absolute_value=True))
            dve.wait_ge(s("rstd_ready"), 7)
            link(nc.vector.tensor_tensor(root2[:, 1:2], root2[:, 0:1], rstd[:], ALU.mult))

            def integers(dst, tmp, n, parts):
                link(nc.vector.tensor_scalar(largest, largest, root2[:, 1:2], QUANT_EPS, ALU.mult, ALU.max))
                link(nc.vector.reciprocal(scale, largest))
                link(nc.vector.tensor_scalar(scale, scale, 127.0, root2[:, 1:2], ALU.mult, ALU.mult))
                cuts = [(k * n // parts, (k + 1) * n // parts) for k in range(parts)]
                for first, op0, second, op1 in ((scale, ALU.mult, ROUND, ALU.add), (ROUND, ALU.subtract, 127.0, ALU.min)):
                    base = used["dve_step"]
                    for k, (lo, hi) in enumerate(cuts):
                        if op0 == ALU.subtract:
                            dve.wait_ge(S["dve_step"], base - parts + k + 1)
                        nc.vector.tensor_scalar(tmp[:, lo:hi], tmp[:, lo:hi], first, second, op0, op1) \
                            .then_inc(S["dve_step"], 1)
                        used["dve_step"] += 1
                for k, (lo, hi) in enumerate(cuts):
                    dve.wait_ge(S["dve_step"], used["dve_step"] - parts + k + 1)
                    nc.vector.tensor_scalar(dst[:, lo:hi], tmp[:, lo:hi], -128.0, None, ALU.max).then_inc(s("bits_ready"), 1)

            def quantise(k, dst, src, gain, n, tmp):
                link(nc.vector.tensor_tensor_reduce(tmp, src, src, 1.0, 0.0, ALU.mult, ALU.add, square))
                nc.vector.tensor_scalar(var[:], square, 1.0 / n, RMS_EPS, ALU.mult, ALU.add).then_inc(s("var_ready"), 1)
                link(nc.vector.tensor_tensor(tmp, src, gain, ALU.mult))
                link(nc.vector.tensor_reduce(largest, tmp, AX.X, ALU.max, apply_absolute_value=True))
                dve.wait_ge(s("rstd_ready"), k)
                link(nc.vector.tensor_copy(root2[:, 1:2], rstd[:]))
                integers(dst, tmp, n, 1)

            def worth_of(n, dst):
                link(nc.vector.scalar_tensor_tensor(out=dst, in0=largest, scalar=1.0 / 127.0, in1=worth[:, n:n + 1],
                                                    op0=ALU.mult, op1=ALU.mult))

            integers(bits, g1[:], D, 2)
            worth_of(0, cell("unit_in"))
            dve.wait_ge(s("bit_ps"), 1)
            nc.vector.tensor_scalar(g1[:, 0:2 * BIT], bank(6, 2 * BIT), cell("unit_in"), None, ALU.mult).then_inc(s("gated"), 1)
            expd, y = g1[:, 2 * BIT:3 * BIT], g1[:, 3 * BIT:4 * BIT]
            dve.wait_ge(s("gated"), 1)
            link(nc.vector.tensor_tensor(y, g1[:, 0:BIT], g1[:, BIT:2 * BIT], ALU.mult))
            dve.wait_ge(s("gate_exp"), 1)
            link(nc.vector.tensor_scalar(expd, expd, 1.0, None, ALU.add))
            link(nc.vector.reciprocal(expd, expd))
            link(nc.vector.tensor_tensor(y, y, expd, ALU.mult))
            bits_y = h2[:, 0:BIT // 2].bitcast(BF16)
            quantise(8, bits_y, y, row("g_out"), BIT, g1[:, 4 * BIT:5 * BIT])
            worth_of(1, cell("unit_out"))
            dve.wait_ge(s("bits_ps"), 2)
            nc.vector.tensor_copy(bitsT[0:BIT, 0:P], ps[0:BIT, 4 * WIN:4 * WIN + P // 2].bitcast(BF16)) \
                .then_inc(s("bitsT_ready"), 1)
            add_residual(6, 0, x, cell("unit_out"))

            normalise(9, xn, x, "xn_ready")
            half_T(7)
            dve.wait_ge(s("in_l3_b1"), 16)
            for n, (lo, hi) in enumerate(HALVES):
                dve.wait_ge(s("mid_ps"), n + 1)
                link(nc.vector.tensor_tensor(g1[:, lo:hi], ps[:, lo:hi], avec[:, lo:hi], ALU.add))
                nc.vector.tensor_scalar(g1[:, lo:hi], g1[:, lo:hi], 0.0, None, ALU.max).then_inc(s("node_rows"), 1)
            half_T(8)
            dve.wait_ge(S["xb_ready"], 4)
            add_residual(7, 2 * WIN, xb)

            whiten(10)
            again = cell("again", 2)
            link(nc.vector.tensor_copy(again[:, 0:1], rstd[:]))
            link(nc.vector.scalar_tensor_tensor(out=again[:, 1:2], in0=rstd[:], scalar=again[:, 0:1], in1=mv[:, 1:2],
                                                op0=ALU.mult, op1=ALU.mult))
            nc.vector.tensor_scalar(var[:], again[:, 1:2], LN_EPS, None, ALU.add).then_inc(s("var_ready"), 1)
            nc.vector.tensor_scalar(xn[:], x[:], mv[:, 0:1], again[:, 0:1], ALU.subtract, ALU.mult) \
                .then_inc(S["dve_step"], 1)
            used["dve_step"] += 1
            dve.wait_ge(s("rstd_ready"), 11)
            link(nc.vector.tensor_tensor(again[:, 1:2], again[:, 0:1], rstd[:], ALU.mult))
            for lo, hi in ((0, D // 2), (D // 2, D)):
                nc.vector.tensor_scalar(g1[:, lo:hi], x[:, lo:hi], mv[:, 0:1], again[:, 1:2], ALU.subtract, ALU.mult) \
                    .then_inc(s("zhat_ready"), 1)
            affine_T("zhatT_ps", 1, xT[:].rearrange("p c n -> p (c n)"), range(0, 4), "r_ln", "xrT_ready")
            affine_T("xrT_ready", 2, g1, range(4, C), "ln1", "xaT_ready")

            def biased_T(dst, ps_at, bias):
                return nc.vector.tensor_tensor(dst.rearrange("p (c n) -> p c n", n=P),
                                               ps[:, ps_at:ps_at + D].rearrange("p (c n) -> p c n", n=P),
                                               bias.unsqueeze(2).broadcast_to([P, C, P]), ALU.add)

            dve.wait_ge(s("eT_ready"), 4)
            gmean = cell("router_mean", 4)
            link(nc.vector.tensor_reduce(gmean, h1[:, 0:512].rearrange("p (f n) -> p f n", n=P)[:, :, 1:P], AX.X, ALU.add))
            nc.vector.tensor_scalar(gmean, gmean, 1.0 / (P - 1), None, ALU.mult).then_inc(s("gmean_ready"), 1)
            dve.wait_ge(s("q_ps"), 1)
            biased_T(g2[:], 2 * WIN, col("bq")).then_inc(s("q_ready"), 1)
            dve.wait_ge(s("ro1g_ps"), 1)
            nc.vector.tensor_tensor(cell("ro1_bias", 4), bank(6, 4), col("r_o1_b"), ALU.add).then_inc(s("ro1_bias"), 1)
            dve.wait_ge(s("k_ps"), 1)
            biased_T(g3[:], 4 * WIN, col("bk")).then_inc(s("k_ready"), 1)
            dve.wait_ge(s("ro3_ps"), 1)
            lg, bit, nbit, sel = cell("router_logits", 4), cell("bits", 2), cell("not_bits", 2), cell("selected", 3)
            link(nc.vector.tensor_tensor(lg, bank(5, 4, 256), row("r_o3_b"), ALU.add))
            link(nc.vector.tensor_tensor(bit, lg[:, 1:4:2], lg[:, 0:4:2], ALU.is_gt))
            link(nc.vector.memset(bit[0:1, :], 1.0))
            link(nc.vector.tensor_scalar(nbit, bit, -1.0, 1.0, ALU.mult, ALU.add))
            link(nc.vector.tensor_tensor(sel[:, 0:1], nbit[:, 0:1], nbit[:, 1:2], ALU.mult))
            link(nc.vector.tensor_tensor(sel[:, 1:2], nbit[:, 0:1], bit[:, 1:2], ALU.mult))
            nc.vector.tensor_tensor(sel[:, 2:3], bit[:, 0:1], nbit[:, 1:2], ALU.mult).then_inc(s("router_done"), 1)
            negmax, total = cell("s_negmax", AH), cell("s_sum", AH)
            for g in range(3):
                dve.wait_ge(s("s_ps"), g + 1)
                m = negmax[:, 4 * g:4 * g + 4]
                sc = bank(g).rearrange("p (h n) -> p h n", n=P)
                if g == 2:
                    sc = ps[:, 2 * WIN:4 * WIN].rearrange("p (b h n) -> p b h n", b=2, n=P)[:, :, 0:2, :]
                link(nc.vector.tensor_reduce(m, sc, AX.X, ALU.max, negate=True))
                nc.vector.tensor_scalar(m, m, AD ** -0.5, None, ALU.mult).then_inc(s("smax"), 1)
            for g in range(3):
                dve.wait_ge(s("sexp"), 4 * g + 4)
                link(nc.vector.reciprocal(total[:, 4 * g:4 * g + 4], total[:, 4 * g:4 * g + 4]))
                v = h1[:, 512 * g:512 * g + 512].rearrange("p (h n) -> p h n", n=P)
                nc.vector.tensor_tensor(v, v, total[:, 4 * g:4 * g + 4].unsqueeze(2).broadcast_to([P, 4, P]), ALU.mult) \
                    .then_inc(s("p_ready"), 1)
            dve.wait_ge(s("v_ps"), 1)
            dve.wait_ge(s("in_bv"), 16)
            nc.vector.tensor_tensor(g4[:], ps[:, 6 * WIN:6 * WIN + D], avec[:, D:2 * D], ALU.add).then_inc(s("v_ready"), 1)
            dve.wait_ge(s("in_bo"), 16)
            link(nc.vector.scalar_tensor_tensor(out=g3[:], in0=avec[:, 0:D], scalar=bit[:, 0:1], in1=xn[:], op0=ALU.mult,
                                                op1=ALU.add))
            o_ps = ps[:, 0:AH * P].rearrange("p (c b n) -> p c b n", b=2, n=P)
            for n, (lo, hi) in enumerate(((0, 4), (4, C))):
                dve.wait_ge(s("oT_ps"), n + 1)
                nc.vector.tensor_copy(xT[AD:P, lo:hi, :], o_ps[AD:P, lo:hi, 1, :]).then_inc(s("o_odd_ready"), 1)
            for n, (lo, hi) in enumerate(HALVES):
                dve.wait_ge(s("wo_ps"), n + 1)
                link(nc.vector.scalar_tensor_tensor(out=g1[:, lo:hi], in0=ps[:, 4 * WIN + lo:4 * WIN + hi],
                                                    scalar=bit[:, 0:1], in1=g3[:, lo:hi], op0=ALU.mult, op1=ALU.add))
                statistics(n, g1)
            normalise(12, g4, g1, "hhat_ready")
            affine_T("hhatT_ps", 2, g2, range(4, C), "ln2", "xfT_ready")
            for n, (lo, hi) in enumerate(HALVES):
                dve.wait_ge(s("fc2_ps"), n + 1)
                nc.vector.scalar_tensor_tensor(out=g3[:, lo:hi], in0=ps[:, lo:hi], scalar=bit[:, 1:2], in1=g1[:, lo:hi],
                                               op0=ALU.mult, op1=ALU.add).then_inc(s("out_rows"), 1)
            half_T(9)
            for k in range(3):
                if k != 1:
                    dve.wait_ge(s("rank_ps"), 1 + k // 2)
                last = nc.vector.tensor_scalar(g4[:, 256 * k:256 * k + 256], ps[:, 2 * WIN + 256 * k:2 * WIN + 256 * k + 256],
                                               sel[:, k:k + 1], None, ALU.mult)
                last.then_inc(s("rank_rows"), 1)
            half_T(10)
            dve.wait_ge(S["xb_ready"], 5)
            for n, (lo, hi) in enumerate(HALVES):
                dve.wait_ge(s("final_ps"), n + 1)
                nc.vector.tensor_tensor(xb[:, lo:hi], ps[:, lo:hi], xb[:, lo:hi], ALU.add).then_inc(s("result_ready"), 1)

        @block.tensor
        def _(pe):
            mm, tr = nc.tensor.matmul, nc.tensor.transpose

            def transpose_rows(src, signal, name, before):
                for c in range(C):
                    if c in before:
                        pe.wait_ge(s(name), before[c])
                    last = tr(ps[:, 4 * WIN + c * P:4 * WIN + (c + 1) * P], src[:, c * P:(c + 1) * P], ident)
                    if c in (3, 5):
                        last.then_inc(s(signal), 1)

            def aggregate(src, adjT, name, before):
                for c in range(C):
                    if c in before:
                        pe.wait_ge(s(name), before[c])
                    last = mm(ps[:, 4 * WIN + c * P:4 * WIN + (c + 1) * P], src[:, c * P:(c + 1) * P], adjT[:],
                              start=True, stop=True)
                    if c in (3, 5):
                        last.then_inc(s("T_ps"), 1)

            def in_halves(k):
                return {0: 2 * k - 1, 3: 2 * k}

            def wait_T(k, c):
                if c == 0:
                    pe.wait_ge(s("T_first_ready"), k)
                if c == 4:
                    pe.wait_ge(s("T_ready"), k)

            def product(k, u, name, at, signal):
                wait_unit(pe, u)
                w = unit(u, name, "p (c n) -> p c n", c=C)
                for lo, hi in HALVES:
                    for c in range(C):
                        if lo == 0:
                            wait_T(k, c)
                        last = mm(ps[:, at + lo:at + hi], xT[:, c, :], w[:, c, lo:hi], start=(c == 0), stop=(c == C - 1))
                    last.then_inc(s(signal), 1)

            def head_product(n, par, in_value, after_first=None, halfway=None):
                pe.wait_ge(S[f"w1_in{par}"], in_value)
                if not isinstance(n, int) or n >= 2:
                    pe.wait_ge(S["h_rows"], n - 1)
                w = ring[:, par, :].rearrange("p (c n) -> p c n", c=C)
                at = 0 if par == 0 else WIN + 256
                parts = ((0, WIN), (WIN, D)) if par == 0 else ((256, D), (0, 256))
                for lo, hi in parts:
                    if lo != parts[0][0]:
                        if after_first is not None:
                            after_first()
                        wait(pe, "h_rows", n)
                    for c in range(C):
                        if c == 3 and lo == parts[0][0] and halfway is not None:
                            halfway()
                        last = mm(ps[:, at + lo:at + hi], xT[:, c, :], w[:, c, lo:hi], start=(c == 0), stop=(c == C - 1))
                return last

            def score_row(h, par):
                wait(pe, "alpha_ready", h + 1)
                wait(pe, "score_sum", h)
                wait(pe, "z_ready", h)
                mm(bank(7, P, 256), alpha[:, par, 0:1].broadcast_to([P, P]), ident, start=True, stop=True) \
                    .then_inc(s("score_row_ps"), 1)

            def turn_attention(h):
                wait(pe, "attn_ready", h + 1)
                wait(pe, "attnT_ready", h)
                tr(bank(7, P, 384), att[:, 1, :], ident).then_inc(S["attnT_ps"], 1)

            def aggregate_head(h, par):
                wait(pe, "attnT_ready", h + 1)
                wait(pe, "h_rows", h + 1)
                wait(pe, "z_ready", h)
                for c in range(C):
                    last = mm(ps[:, 6 * WIN + c * P:6 * WIN + (c + 1) * P], h1[:, par * D + c * P:par * D + (c + 1) * P],
                              attnT[:, par, :], start=True, stop=True)
                last.then_inc(S["agg_ready"], 1)

            def head_second(n, par, in_value, chunks=range(C)):
                if 0 in chunks:
                    pe.wait_ge(S[f"w2_in{par}"], in_value)
                    wait(pe, "elu_ready", n + 1)
                w = ring[:, 2 + par, :].rearrange("p (c n) -> p c n", c=C)
                for c in chunks:
                    for lo, hi in HALVES:
                        last = mm(ps[:, 4 * WIN + lo:4 * WIN + hi], h2[:, par * D + c * P:par * D + (c + 1) * P],
                                  w[:, c, lo:hi], start=False, stop=False)
                return last

            def sum_edges(es):
                for e in es:
                    last = mm(bank(3, 3 * P, P), oh_dst[:, e, :], oh_src[:, 1:4, e, :], start=(e == 0), stop=(e == EC - 1))
                return last

            def turn_adjacency(n, adjT):
                pe.wait_ge(s("adj_half"), n + 1)
                tr(bank(3, P), adjT[:], ident).then_inc(s("adj_ps"), 1)

            def step(h, par, w1_value, w2_value):
                score_row(h, par)
                head_product(h + 1, 1 - par, w1_value, lambda: turn_attention(h)).then_inc(S["hprod"], 1)
                aggregate_head(h, par)
                head_second(h - 1, 1 - par, w2_value).then_inc(S["w2_used"], 1)

            pe.wait_ge(s("constants"), 1)
            transpose_rows(xn, "T_ps", "xn_ready", in_halves(1))
            w = ring[:, 0, :].rearrange("p (c n) -> p c n", c=C)
            pe.wait_ge(S["w1_first_in"], 16)
            for c in range(C):
                wait_T(1, c)
                if c == C // 2:
                    pe.wait_ge(S["w1_in0"], 16)
                for lo, hi in HALVES:
                    last = mm(ps[:, lo:hi], xT[:, c, :], w[:, c, lo:hi], start=(c == 0), stop=(c == C - 1))
            last.then_inc(S["hprod"], 1)
            pe.wait_ge(s("constants"), 5)
            for lo, hi in HALVES:
                mm(ps[:, 4 * WIN + lo:4 * WIN + hi], zrow[:], zrow[:, 0:1].broadcast_to([1, hi - lo]), start=True, stop=False)
            pe.wait_ge(s("onehots"), 2)
            for e in range(EC):
                last = mm(bank(3, P), oh_dst[:, e, :], oh_src[:, 0, e, :], start=(e == 0), stop=(e == EC - 1))
            last.then_inc(s("counted"), 1)
            score_row(0, 0)
            head_product(1, 1, 16, lambda: turn_attention(0)).then_inc(S["hprod"], 1)
            aggregate_head(0, 0)
            head_product(2, 0, 32, lambda: turn_attention(1), lambda: score_row(1, 1)).then_inc(S["hprod"], 1)
            aggregate_head(1, 1)
            head_second(0, 0, 16).then_inc(S["w2_used"], 1)
            step(2, 0, 32, 16)
            turn_adjacency(0, adj1T)
            with pe.Fori(1, 3) as i:
                step(2 * i + 1, 1, 16 * i + 32, 16 * i + 16)
                step(2 * i + 2, 0, 16 * i + 32, 16 * i + 16)
            score_row(7, 1)
            head_second(6, 0, 64, range(0, 3))
            turn_attention(7)
            head_second(6, 0, 64, range(3, 4))
            aggregate_head(7, 1)
            head_second(6, 0, 64, range(4, C)).then_inc(S["w2_used"], 1)
            pe.wait_ge(s("ew_rows"), 3)
            sum_edges(range(0, 10))
            pe.wait_ge(S["w2_in1"], 64)
            wait(pe, "elu_ready", 8)
            w = ring[:, 3, :].rearrange("p (c n) -> p c n", c=C)
            for (lo, hi), signal in zip(HALVES, ("gat2_first", "hprod")):
                for c in range(C):
                    last = mm(ps[:, 4 * WIN + lo:4 * WIN + hi], h2[:, D + c * P:D + (c + 1) * P], w[:, c, lo:hi],
                              start=False, stop=(c == C - 1))
                last.then_inc(s(signal), 1)
            sum_edges(range(10, EC)).then_inc(s("edges_summed"), 1)
            score_row(8, 0)
            turn_attention(8)
            wait(pe, "attnT_ready", 9)
            wait(pe, "h_rows", 9)
            for lo, hi in HALVES:
                mm(ps[:, lo:hi], attnT[:, 0, :], h1[:, lo:hi], start=True, stop=True).then_inc(s("rows_ps"), 1)
            transpose_rows(xn, "T_ps", "xn_ready", in_halves(2))
            for c in range(C):
                wait_T(2, c)
                last = mm(bank(6, E0 + 1), xT[:, c, :], gatew[:, c * (E0 + 1):(c + 1) * (E0 + 1)],
                          start=(c == 0), stop=(c == C - 1))
            last.then_inc(s("gate_ps"), 1)
            turn_adjacency(1, adj2T)

            def shift_green(lv):
                pe.wait_ge(s("green_state"), lv + 1)
                for d, off in enumerate((P - 2 ** lv, P + 2 ** lv)):
                    last = mm(bank(7, 16, 16 * d), shiftm[:, off:off + P], state[:, 16 * d:16 * d + 16], start=True, stop=True)
                last.then_inc(s("shifted"), 1)

            wait_unit(pe, U_L0)
            w = unit(U_L0, "l0_w1", "p (c n) -> p c n", c=C)
            for c in range(C):
                last = mm(bank(0, H0), xT[:, c, :], w[:, c, :], start=(c == 0), stop=(c == C - 1))
                if c == C - 1:
                    last.then_inc(s("hid0_mm"), 1)
                if c in (0, 2, 4):
                    shift_green(c // 2)
            shift_green(3)
            pe.wait_ge(s("hid0_scaled"), 1)
            for c in range(3):
                last = tr(ps[:, 4 * WIN + c * P:4 * WIN + (c + 1) * P], h1[:, c * P:(c + 1) * P], ident)
            last.then_inc(s("hid0_ps"), 1)
            shift_green(4)
            pe.wait_ge(s("adj_ready"), 2)
            pe.wait_ge(s("hid0T"), 1)
            w = unit(U_L0, "l0_w2", "p (c n) -> p c n", c=3)
            for c in range(3):
                for lo, hi in HALVES:
                    last = mm(ps[:, 2 * WIN + lo:2 * WIN + hi], h1[:, H0 + c * P:H0 + (c + 1) * P], w[:, c, lo:hi],
                              start=(c == 0), stop=False)
                    if lo == 0 and c < 2:
                        shift_green(5 + c)
            last.then_inc(s("l0_weights_used"), 1)
            pe.wait_ge(s("comb_ready"), 1)
            tr(bank(7, P, 0, 11), comb[:, 0:11], ident).then_inc(s("combT_ps"), 1)
            pe.wait_ge(s("combT_ready"), 1)
            pe.wait_ge(s("tail_ready"), 1)
            for lo, hi in HALVES:
                mm(ps[:, 2 * WIN + lo:2 * WIN + hi], combT[0:11, :], g3[0:11, lo:hi], start=False, stop=True) \
                    .then_inc(s("rows_ps"), 1)

            pe.wait_ge(s("adj_ready"), 2)
            aggregate(xn, adj1T, "xn_ready", in_halves(3))
            product(3, U_L1, "l1_w", 0, "rows_ps")

            transpose_rows(xn, "T_ps", "xn_ready", in_halves(4))
            n36 = G1N + G1N * E1N
            for c in range(C):
                wait_T(4, c)
                last = mm(bank(6, n36), xT[:, c, :], gatew1[:, c * n36:(c + 1) * n36], start=(c == 0), stop=(c == C - 1))
            last.then_inc(s("gate_ps"), 1)

            def hidden(g):
                u, name = ((U_L1W1A, "l1f_w1a"), (U_L1W1B, "l1f_w1b"))[g // 2]
                wait_unit(pe, u)
                weights = unit(u, name, "p (c n) -> p c n", c=C)
                lo = (g % 2) * H0
                for c in range(C):
                    last_ = mm(bank(g, H0), xT[:, c, :], weights[:, c, lo:lo + H0], start=(c == 0), stop=(c == C - 1))
                last_.then_inc(s("hid1_mm"), 1)

            def turn_hidden(g):
                pe.wait_ge(s("hid1_scaled"), g + 1)
                if g >= 2:
                    pe.wait_ge(s("hid1T"), g - 1)
                for c in range(3):
                    last_ = tr(bank(4 + g % 2, P, c * P), h1[:, g * H0 + c * P:g * H0 + (c + 1) * P], ident)
                last_.then_inc(s("hid1_ps"), 1)

            def hidden_out(g):
                u, name = ((U_L1W2A, "l1f_w2a"), (U_L1W2B, "l1f_w2b"))[g // 2]
                wait_unit(pe, u)
                pe.wait_ge(s("hid1T"), g + 1)
                weights = unit(u, name, "p (c n) -> p c n", c=C)
                for lo, hi in HALVES:
                    for c in range(3):
                        last_ = mm(ps[:, lo:hi], h2[:, g * H0 + c * P:g * H0 + (c + 1) * P],
                                   weights[:, 3 * (g % 2) + c, lo:hi], start=False, stop=(g == 3 and c == 2))
                    if g == 3:
                        last_.then_inc(s("rows_ps"), 1)
                return last_

            hidden(0)
            hidden(1)
            pe.wait_ge(s("comb_ready"), 2)
            tr(bank(7, P, 0, 32), comb[:, 0:32], ident).then_inc(s("combT_ps"), 1)
            hidden(2)
            turn_hidden(0)
            hidden(3)
            turn_hidden(1)
            pe.wait_ge(s("combT_ready"), 2)
            pe.wait_ge(s("in_b2"), 16)
            for lo, hi in HALVES:
                mm(ps[:, lo:hi], combT[:], g1[0:32, lo:hi], start=True, stop=False)
            hidden_out(0)
            turn_hidden(2)
            hidden_out(1).then_inc(s("w2a_used"), 1)
            turn_hidden(3)
            hidden_out(2)
            pe.wait_ge(s("wsum_ready"), 2)
            pe.wait_ge(s("constants"), 4)
            mm(bank(7, 1, P), ones[:], cell("w_abs", 2)[:, 0:1], start=True, stop=True)
            mm(bank(7, 1, P + 1), ones[0:BIT, :], cell("w_abs", 2)[0:BIT, 1:2], start=True, stop=True) \
                .then_inc(s("wsum_ps"), 1)
            hidden_out(3)

            transpose_rows(xn, "T_ps", "xn_ready", in_halves(5))
            wait_unit(pe, U_L2)
            w = unit(U_L2, "l2_wd", "p (c n) -> p c n", c=C)
            for c in range(C):
                wait_T(5, c)
                last = mm(bank(6, P, 0, DOWN), w[:, c, :], xT[:, c, :], start=(c == 0), stop=(c == C - 1))
            last.then_inc(s("l2_ps"), 1)
            pe.wait_ge(s("l2_copied"), 1)
            w = unit(U_L2, "l2_wu")
            for lo, hi in HALVES:
                mm(ps[:, lo:hi], zT[0:DOWN + 1, :], w[:, lo:hi], start=True, stop=True).then_inc(s("l2_ps"), 1)
            aggregate(g1, adj2T, "node_rows", {0: 1, 4: 2})
            w = unit(U_L2, "l2_w1", "p (c n) -> p c n", c=C)
            for c in range(C):
                wait_T(6, c)
                last = mm(bank(6, HID2), xT[:, c, :], w[:, c, :], start=(c == 0), stop=(c == C - 1))
            last.then_inc(s("l2_ps"), 1)
            pe.wait_ge(s("node_rows"), 3)
            for c in range(2):
                last = mm(bank(2, P, c * P), g2[:, c * P:(c + 1) * P], adj2T[:], start=True, stop=True)
            last.then_inc(s("l2_ps"), 1)
            pe.wait_ge(s("l2_copied"), 2)
            w = unit(U_L2, "l2_w2", "p (c n) -> p c n", c=2)
            for lo, hi in HALVES:
                for c in range(2):
                    last = mm(ps[:, lo:hi], g3[:, c * P:(c + 1) * P], w[:, c, lo:hi], start=(c == 0), stop=(c == 1))
                last.then_inc(s("rows_ps"), 1)

            pe.wait_ge(s("constants"), 2)
            for c in range(C):
                if c % 3 == 0:
                    pe.wait_ge(s("bits_ready"), 1 + c // 3)
                last = tr(ps[:, 4 * WIN + c * P // 2:4 * WIN + (c + 1) * P // 2].bitcast(BF16), bits[:, c * P:(c + 1) * P],
                          identb[:])
            last.then_inc(s("bits_ps"), 1)
            pe.wait_ge(s("bitsT_ready"), 1)
            for c in range(C):
                last = mm(bank(6, 2 * BIT), bitsT[:, c * P:(c + 1) * P], w_in_q[:, c * 2 * BIT:(c + 1) * 2 * BIT],
                          start=(c == 0), stop=(c == C - 1))
            last.then_inc(s("bit_ps"), 1)
            pe.wait_ge(s("bits_ready"), 3)
            tr(ps[0:BIT, 4 * WIN:4 * WIN + P // 2].bitcast(BF16), h2[:, 0:BIT // 2].bitcast(BF16), identb[:]) \
                .then_inc(s("bits_ps"), 1)
            pe.wait_ge(s("bitsT_ready"), 2)
            for lo, hi in HALVES:
                mm(ps[:, lo:hi], bitsT[0:BIT, 0:P], w_out_q[:, lo:hi], start=True, stop=True).then_inc(s("rows_ps"), 1)

            aggregate(xn, adj1T, "xn_ready", in_halves(6))
            product(7, U_L3A, "l3_w1", 0, "mid_ps")
            aggregate(g1, adj1T, "node_rows", {0: 4, 4: 5})
            product(8, U_L3B, "l3_w2", 2 * WIN, "rows_ps")

            def product_T(weights, first_bank, outs, operand, signal, emptied=None):
                chunks = weights.shape[1]
                for o in range(outs):
                    if emptied is not None and o >= 2:
                        pe.wait_ge(s(emptied), o - 1)
                    to = ps[:, first_bank * WIN + o * P:first_bank * WIN + (o + 1) * P]
                    if emptied is not None:
                        to = bank(first_bank + o % 2, P)
                    for c in range(chunks):
                        last_ = mm(to, weights[:, c, o * P:(o + 1) * P], operand(c), start=(c == 0), stop=(c == chunks - 1))
                    if emptied is not None or o == outs - 1:
                        last_.then_inc(s(signal), 1)

            transpose_rows(g1, "zhatT_ps", "zhat_ready", in_halves(1))
            wait_unit(pe, U_RIN)
            pe.wait_ge(s("xrT_ready"), 2)
            product_T(unit(U_RIN, "r_in", "p (c n) -> p c n", c=C), 0, 4, lambda c: xT[:, c, :], "rin_ps", emptied="eT_ready")
            wait_unit(pe, U_Q)
            pe.wait_ge(s("xaT_ready"), 2)
            product_T(unit(U_Q, "wq", "p (c n) -> p c n", c=C), 2, C, lambda c: g1[:, c * P:(c + 1) * P], "q_ps")
            wait_unit(pe, U_RO1)
            pe.wait_ge(s("gmean_ready"), 1)
            w = unit(U_RO1, "r_o1", "p (c n) -> p c n", c=8)
            for f in range(4):
                for c in range(4):
                    last = mm(bank(6, 1, f), w[:, 4 + c, f * P:(f + 1) * P], cell("router_mean", 4)[:, c:c + 1],
                              start=(c == 0), stop=(c == 3))
            last.then_inc(s("ro1g_ps"), 1)
            pe.wait_ge(s("ro1_bias"), 1)
            product_T(w[:, 0:4, :], 6, 4, lambda c: h1[:, c * P:(c + 1) * P], "ro1_ps", emptied="h1T_ready")
            wait_unit(pe, U_K)
            product_T(unit(U_K, "wk", "p (c n) -> p c n", c=C), 4, C, lambda c: g1[:, c * P:(c + 1) * P], "k_ps")
            pe.wait_ge(s("h1T_ready"), 4)
            product_T(unit(U_RIN, "r_o2", "p (c n) -> p c n", c=4), 0, 2,
                      lambda c: h1[:, 512 + c * P:512 + (c + 1) * P], "ro2_ps", emptied="h2T_ready")
            def scores():
                pe.wait_ge(s("h2T_ready"), 2)
                w3 = unit(U_RIN, "r_o3", "p (c n) -> p c n", c=2)
                for c in range(2):
                    last = mm(bank(5, 4, 256), h1[:, 1024 + c * P:1024 + (c + 1) * P], w3[:, c, :], start=(c == 0), stop=(c == 1))
                last.then_inc(s("ro3_ps"), 1)
                pe.wait_ge(s("q_ready"), 1)
                for h in range(AH):
                    r0, c = (h % 2) * AD, h // 2
                    last = mm(score_ps(POSITION[h]), g2[r0:r0 + AD, c * P:(c + 1) * P], g3[r0:r0 + AD, c * P:(c + 1) * P],
                              start=True, stop=True)
                    if h in (6, 7, 11):
                        last.then_inc(s("s_ps"), 1)

            wait_unit(pe, U_V)
            pe.wait_ge(s("k_ready"), 1)
            w = unit(U_V, "wv", "p (c n) -> p c n", c=C)
            for lo, hi in HALVES:
                for c in range(C):
                    last = mm(ps[:, 6 * WIN + lo:6 * WIN + hi], g1[:, c * P:(c + 1) * P], w[:, c, lo:hi],
                              start=(c == 0), stop=(c == C - 1))
                    if lo == 0 and c == 0:
                        scores()
            last.then_inc(s("v_ps"), 1)
            pT_banks = (4, 5, 3)
            for g in range(3):
                pe.wait_ge(s("p_ready"), g + 1)
                for h in range(4):
                    last = tr(bank(pT_banks[g], P, h * P), h1[:, (4 * g + h) * P:(4 * g + h + 1) * P], ident)
                last.then_inc(s("pT_ps"), 1)
            pe.wait_ge(s("v_ready"), 1)
            for at in range(AH):
                h = POSITION.index(at)
                if at % 4 == 0:
                    pe.wait_ge(s("pT_ready"), at // 4 + 1)
                last = mm(ps[:, h * P:(h + 1) * P], g4[:, (h // 2) * P:(h // 2 + 1) * P], h2[:, at * P:(at + 1) * P],
                          start=True, stop=True)
                if at in (7, 11):
                    last.then_inc(s("oT_ps"), 1)
            wait_unit(pe, U_O)
            w = unit(U_O, "wo", "p (c n) -> p c n", c=C)
            for lo, hi in HALVES:
                for c in range(C):
                    if lo == 0 and c in (0, 4):
                        pe.wait_ge(s("o_even_ready"), 1 + c // 4)
                        pe.wait_ge(s("o_odd_ready"), 1 + c // 4)
                    last = mm(ps[:, 4 * WIN + lo:4 * WIN + hi], xT[:, c, :], w[:, c, lo:hi], start=(c == 0), stop=(c == C - 1))
                last.then_inc(s("wo_ps"), 1)
            transpose_rows(g4, "hhatT_ps", "hhat_ready", in_halves(1))
            pe.wait_ge(s("xfT_ready"), 2)
            w = unit(U_RO1, "fc1", "p (c n) -> p c n", c=C)
            for c in range(C):
                last = mm(bank(6, P, 0, MLP), w[:, c, :], g2[:, c * P:(c + 1) * P], start=(c == 0), stop=(c == C - 1))
            last.then_inc(s("fc1_ps"), 1)
            pe.wait_ge(s("fc1_ready"), 1)
            pe.wait_ge(s("in_fc2"), 16)
            for lo, hi in HALVES:
                mm(ps[:, lo:hi], zT[0:MLP + 1, :], row0[0:MLP + 1, lo:hi], start=True, stop=True).then_inc(s("fc2_ps"), 1)
            transpose_rows(g3, "T_ps", "out_rows", {0: 1, 4: 2})
            product(9, U_DOWN, "down", 2 * WIN, "rank_ps")
            transpose_rows(g4, "T_ps", "rank_rows", {0: 1, 2: 2, 4: 3})
            product(10, U_UP, "up", 0, "final_ps")


def chunked(np, w):
    k, n = w.shape
    return np.ascontiguousarray(w.reshape(k // P, P, n).transpose(1, 0, 2).reshape(P, k // P * n))


def lay_out(np, i):
    a = {"x": i["x"], "edge_weight": i["edge_weight"].reshape(P, EC)}
    a["src"], a["dst"] = i["src"].reshape(P, EC), i["dst"].reshape(P, EC)
    a["gat_w1"] = i["L0_gnn_W1"].reshape(C, P, HEADS1, D).transpose(2, 1, 0, 3).reshape(HEADS1, P, UNIT)
    a["gat_w2"] = i["L0_gnn_W2"].reshape(HEADS1, C, P, D).transpose(0, 2, 1, 3).reshape(HEADS1, P, UNIT)
    a["gat_a"] = np.concatenate([np.concatenate([i["L0_gnn_a_src1"], i["L0_gnn_a_src2"]]),
                                 np.concatenate([i["L0_gnn_a_dst1"], i["L0_gnn_a_dst2"]])], axis=1)
    a["gat_b2"] = i["L0_gnn_b2"]
    a["gatew"] = chunked(np, np.concatenate([i["L0_ffn_gate_w"], i["L0_ffn_v_w"][:, None]], axis=1))
    a["l0_w1"] = chunked(np, i["L0_ffn_w1"].transpose(1, 0, 2).reshape(D, H0))
    a["l0_w2"] = chunked(np, i["L0_ffn_w2"].reshape(H0, D))
    a["l0_tail"] = np.concatenate([i["L0_ffn_b2"], i["L0_ffn_out_w"], i["L0_ffn_out_b"][None]])
    a["bk_scale"] = i["L0_ffn_bk_scale"]
    a["l1_w"] = chunked(np, i["L1_gnn_W"])
    a["l1_b"] = i["L1_gnn_b"]
    a["gatew1"] = chunked(np, np.concatenate([i["L1_ffn_Wg"], i["L1_ffn_Wge"].transpose(1, 0, 2).reshape(D, G1N * E1N)],
                                             axis=1))
    w1 = i["L1_ffn_W1"].transpose(1, 0, 2).reshape(D, H1N)
    a["l1f_w1a"], a["l1f_w1b"] = chunked(np, w1[:, :D]), chunked(np, w1[:, D:])
    w2 = i["L1_ffn_W2"].reshape(H1N, D)
    a["l1f_w2a"], a["l1f_w2b"] = chunked(np, w2[:D]), chunked(np, w2[D:])
    a["l1_b1"] = i["L1_ffn_b1"].reshape(H1N)
    a["l1_b2"] = i["L1_ffn_b2"]
    a["l2_w1"], a["l2_w2"] = chunked(np, i["L2_gnn_W1"]), chunked(np, i["L2_gnn_W2"])
    a["l2_wd"] = chunked(np, i["L2_gnn_Wd"])
    a["l2_wu"] = np.concatenate([i["L2_gnn_Wu"], i["L2_gnn_bu"][None]])
    a["l2_b2"] = i["L2_gnn_b2"]
    a["l2_win"] = chunked(np, i["L2_ffn_w_in"].T)
    a["l2_wout"] = i["L2_ffn_w_out"].T
    a["g_in"] = i["L2_ffn_g_in"]
    a["l3_w1"], a["l3_w2"] = chunked(np, i["L3_gnn_W1"]), chunked(np, i["L3_gnn_W2"])
    a["l3_b1"], a["l3_b2"] = i["L3_gnn_b1"], i["L3_gnn_b2"]
    for name in ("wq", "wk", "wv", "wo"):
        a[name] = chunked(np, i["L3_ffn_" + name].T)
    a["bv"], a["bo"] = i["L3_ffn_bv"], i["L3_ffn_bo"]
    a["r_in"], a["r_o1"] = chunked(np, i["L3_ffn_r_in_w"].T), chunked(np, i["L3_ffn_r_o1_w"].T)
    a["r_o2"], a["r_o3"] = chunked(np, i["L3_ffn_r_o2_w"].T), chunked(np, i["L3_ffn_r_o3_w"].T)
    a["fc1"] = chunked(np, i["L3_ffn_fc1_w"].T)
    a["fc2"] = np.concatenate([i["L3_ffn_fc2_w"].T, i["L3_ffn_fc2_b"][None]])
    a["down"] = chunked(np, i["L3_ffn_lra_down"].reshape(D, D).T)
    a["up"] = chunked(np, i["L3_ffn_lra_up"].transpose(0, 2, 1).reshape(D, D))
    a["bd"], a["fc1_b"] = i["L2_gnn_bd"].reshape(DOWN, 1), i["L3_ffn_fc1_b"].reshape(MLP, 1)
    vectors = [i["L0_gnn_b1"]] + [i["L3_ffn_" + n] for n in ("bq", "bk", "ln1_g", "ln1_b", "r_ln_g", "r_ln_b", "ln2_g",
                                                           "ln2_b", "r_in_b", "r_o1_b", "r_o2_b")]
    a["cols"] = np.concatenate(vectors).reshape(NCOLS, P).T
    a["rows"] = np.concatenate([i["L0_ffn_b1"].reshape(-1), i["L2_gnn_b1"], i["L0_ffn_gate_b"], i["L0_ffn_v_b"].reshape(1),
                                i["L1_ffn_bg"], i["L1_ffn_bge"].reshape(-1), i["L2_ffn_g_out"], i["L3_ffn_r_o3_b"]])
    return {n: np.ascontiguousarray(v) for n, v in a.items()}


def kernel(**inputs):
    import numpy as np
    import concourse.bacc as bacc
    from concourse.bass_utils import run_bass_kernel_spmd

    arrays = lay_out(np, {n: np.asarray(v) for n, v in inputs.items()})
    nc = bacc.Bacc("TRN2", target_bir_lowering=False, num_devices=1)
    a = {n: nc.dram_tensor("in_" + n, v.shape, mybir.dt.from_np(v.dtype), kind="ExternalInput").ap()
         for n, v in arrays.items()}
    out = nc.dram_tensor("out_x", (P, D), F32, kind="ExternalOutput").ap()
    build(nc, a, out)
    r = run_bass_kernel_spmd(nc, [{"in_" + n: v for n, v in arrays.items()}], core_ids=[0])
    return r.results[0]["out_x"]
```

```python
import concourse.bass as bass
from concourse import mybir
from contextlib import ExitStack

F32 = mybir.dt.float32
BF16 = mybir.dt.bfloat16
I32 = mybir.dt.int32
ALU = mybir.AluOpType
ACT = mybir.ActivationFunctionType
AX = mybir.AxisListType

P = 128
D = 768
C = D // P
UNIT = C * D
SLOTS = 8
EDGES = 4224
EC = EDGES // P
HEADS1 = 8
WIN = 512
BIG = 1.0e30
LEAK = 0.2
SEG_EPS = 1e-16
LN_EPS = 1e-5
RMS_EPS = 1e-6
QUANT_EPS = 1e-5
ROUND = 12582912.0
E0, F0 = 8, 48
G1N, E1N = 4, 8
H0 = E0 * F0
H1N = G1N * E1N * F0
DOWN = 24
HID2 = 256
BIT = 32
RHD = 512
AH, AD = 12, 64
MLP = 48

HALVES = ((0, WIN), (WIN, D))

POSITION = [0, 4, 1, 5, 2, 6, 3, 7, 8, 10, 9, 11]

COLS = {}
_at = 0
for _name, _n in (("gat_b1", 48), ("bq", 6), ("bk", 6), ("ln1_g", 6), ("ln1_b", 6), ("r_ln_g", 6),
                  ("r_ln_b", 6), ("ln2_g", 6), ("ln2_b", 6), ("r_in_b", 4), ("r_o1_b", 4), ("r_o2_b", 2)):
    COLS[_name] = (_at, _at + _n)
    _at += _n
NCOLS = _at

ROWS = {}
_at = 0
for _name, _n in (("l0_b1", H0), ("l2_b1", HID2), ("l0_gate", E0 + 1), ("l1_gate", G1N + G1N * E1N),
                  ("g_out", BIT), ("r_o3_b", 4)):
    ROWS[_name] = (_at, _at + _n)
    _at += _n
NROWS = _at

UNITS = [
    [("l0_w1", 0, P, C * H0), ("l0_w2", C * H0, P, 3 * D)],
    [("l1_w", 0, P, UNIT)],
    [("l1f_w1a", 0, P, UNIT)],
    [("l1f_w1b", 0, P, UNIT)],
    [("l1f_w2a", 0, P, UNIT)],
    [("l1f_w2b", 0, P, UNIT)],
    [("l2_w1", 0, P, C * HID2), ("l2_w2", 1536, P, 2 * D), ("l2_win", 3072, P, C * 2 * BIT),
     ("l2_wd", 3456, P, C * DOWN), ("l2_wu", 3600, DOWN + 1, D)],
    [("l3_w1", 0, P, UNIT)],
    [("l3_w2", 0, P, UNIT)],
    [("r_in", 0, P, C * RHD), ("r_o2", 3072, P, 4 * RHD // 2), ("r_o3", 4096, P, 8)],
    [("wq", 0, P, UNIT)],
    [("r_o1", 0, P, 8 * RHD), ("fc1", 8 * RHD, P, C * MLP)],
    [("wk", 0, P, UNIT)],
    [("wv", 0, P, UNIT)],
    [("wo", 0, P, UNIT)],
    [("down", 0, P, UNIT)],
    [("up", 0, P, UNIT)],
]
FIRST_SLOT = 4
(U_L0, U_L1, U_L1W1A, U_L1W1B, U_L1W2A, U_L1W2B, U_L2, U_L3A, U_L3B, U_RIN, U_Q, U_RO1, U_K, U_V,
 U_O, U_DOWN, U_UP) = range(len(UNITS))


def build(nc, a, out):
    ctx = ExitStack()
    with ctx:
        def sb(name, shape, dt=F32):
            return ctx.enter_context(nc.sbuf_tensor(name, shape, dt))

        def sem(name):
            return ctx.enter_context(nc.semaphore(name))

        ring = sb("ring", [P, SLOTS, UNIT])
        x = sb("x", [P, D])
        xb = sb("xb", [P, D])
        xn = sb("xn", [P, D])
        xT = sb("xT", [P, C, P])
        g1 = sb("g1", [P, D])
        g2 = sb("g2", [P, D])
        g3 = sb("g3", [P, D])
        g4 = sb("g4", [P, D])
        h1 = sb("h1", [P, 2 * D])
        h2 = sb("h2", [P, 2 * D])
        avec = sb("avec", [P, 2 * D])
        row0 = sb("row0", [P, D])
        row1 = sb("row1", [P, D])
        rows = sb("rows", [P, NROWS])
        cols = sb("cols", [P, NCOLS])
        shiftm = sb("shiftm", [P, 3 * P])
        count = sb("count", [P, P])
        absent = sb("absent", [P, P])
        adj1T = sb("adj1T", [P, P])
        adj2T = sb("adj2T", [P, P])
        att = sb("att", [P, 2, P])
        attnT = sb("attnT", [P, 2, P])
        alpha = sb("alpha", [P, 2, 2])
        soft = sb("soft", [P, 4])
        stats = sb("stats", [P, 2, 6])
        mv = sb("mv", [P, 2])
        var = sb("var", [P, 1])
        rstd = sb("rstd", [P, 1])
        mhalf = sb("mhalf", [P, 1])
        ones = sb("ones", [P, P])
        zrow = sb("zrow", [1, P])
        gatew = sb("gatew", [P, C * (E0 + 1)])
        gatew1 = sb("gatew1", [P, C * (G1N + G1N * E1N)])
        lin = sb("lin", [P, 40])
        tk = sb("tk", [P, 5, 32])
        tks = sb("tks", [P, 2, 4])
        desc = sb("desc", [P, E1N])
        comb = sb("comb", [P, 44])
        identb = sb("identb", [P, P], BF16)
        combT = sb("combT", [32, P])
        cells = sb("cells", [P, 128])
        bias1 = sb("bias1", [P, 2])
        zT = sb("zT", [64, P])
        idx = sb("idx", [P, 2, EC], I32)
        idxb = sb("idxb", [P, 2, EC], BF16)
        ew = sb("ew", [P, 2, EC])
        ewb = sb("ewb", [P, 3, EC], BF16)

        ps = ctx.enter_context(nc.psum_tensor("ps", [P, 8 * WIN], F32))

        def bank(n, w=WIN, off=0, rows_=P):
            return ps[0:rows_, n * WIN + off:n * WIN + off + w]

        def head_psum(par):
            return ps[:, 0:D] if par == 0 else ps[:, WIN + 256:WIN + 256 + D]

        def score_ps(at):
            return ps[:, at * P:(at + 1) * P] if at < 10 else ps[:, (at + 2) * P:(at + 3) * P]

        def hat_at(c):
            return bank(4 + c // 2, P, c % 2 * P) if c < 5 else bank(7, P)

        ident = shiftm[:, P:2 * P]

        scratch = ring[:, 4:8, :].rearrange("p s n -> p (s n)").bitcast(BF16)
        n1h = EC * P
        oh_dst = scratch[:, 0:n1h].rearrange("p (e n) -> p e n", n=P)
        oh_src = scratch[:, n1h:5 * n1h].rearrange("p (k e n) -> p k e n", k=4, n=P)
        iotab = scratch[:, 5 * n1h:5 * n1h + P]
        iotai = ring[:, 7, UNIT - P:UNIT].bitcast(I32)

        state = h2[:, 384:416]
        prod = h2[:, 512:672]
        w_in_q = g2[:, 256:448].bitcast(BF16)
        w_out_q = g3[0:BIT, 256:640].bitcast(BF16)
        bits = h2[:, 0:384].bitcast(BF16)
        bitsT = h2[:, 384:768].bitcast(BF16)
        SMALL = 16 * 7

        S = {}

        def s(name):
            if name not in S:
                S[name] = sem(name)
            return S[name]

        for name in ("x_in w1_first_in cols_in graph_in small_in avec_in w1_in0 w1_in1 w2_in0 w2_in1 w2_used hprod "
                     "h_rows alpha_ready alpha_rows score_sum score_leaky negmax exped weighed "
                     "denom_ready attn_ready attnT_ps attnT_ready agg_ready z_ready z_neg z_exp elu_ready "
                     "dve_step pool_step act_step out_done").split():
            s(name)
        for n in range(SLOTS):
            s(f"slot{n}_in")

        landed, filled = [], [0] * SLOTS
        for u, parts in enumerate(UNITS):
            slot = (FIRST_SLOT + u) % SLOTS
            filled[slot] += 16 * len(parts)
            landed.append((slot, filled[slot]))

        released = [("l0_weights_used", 1), ("rows_ps", 6), ("hid1_mm", 2), ("hid1_mm", 4), ("w2a_used", 1),
                    ("rows_ps", 8), ("rows_ps", 10), ("mid_ps", 2), ("rows_ps", 14)]

        def unit(u, name, rearr=None, **kw):
            slot = landed[u][0]
            for part, c0, parts, n in UNITS[u]:
                if part == name:
                    v = ring[0:parts, slot, c0:c0 + n]
                    return v.rearrange(rearr, **kw) if rearr else v
            raise KeyError(name)

        def wait_unit(eng, u):
            slot, value = landed[u]
            eng.wait_ge(S[f"slot{slot}_in"], value)

        cell_at = {}

        def cell(name, n=1):
            if name not in cell_at:
                cell_at[name] = sum(w for _, w in cell_at.values()), n
            lo, w = cell_at[name]
            assert w == n and lo + n <= 128
            return cells[:, lo:lo + n]

        again, twice = cell("again"), cell("twice")

        def col(name, i=None, n=1):
            lo, hi = COLS[name]
            return cols[:, lo:hi] if i is None else cols[:, lo + i:lo + i + n]

        def row(name):
            lo, hi = ROWS[name]
            return rows[:, lo:hi]

        def wait(eng, name, value):
            if not isinstance(value, int) or value >= 1:
                eng.wait_ge(s(name), value)

        used = {name: 0 for name in ("dve_step", "pool_step", "act_step")}

        def chained(eng, name, ins):
            used[name] += 1
            ins.then_inc(S[name], 1)
            eng.wait_ge(S[name], used[name])

        block = ctx.enter_context(nc.Block())

        def broadcast_row(src, n):
            return src.rearrange("(o n) -> o n", o=1).broadcast_to([P, n])

        @block.sync
        def _(sp):
            def load_avec(h):
                wait(sp, "alpha_ready", h)
                sp.dma_start(avec[:], a["gat_a"][bass.ds(h, 1), :].broadcast_to([P, 2 * D])).then_inc(S["avec_in"], 16)

            def load_w1(h, par):
                if not isinstance(h, int) or h >= 2:
                    sp.wait_ge(S["hprod"], h - 1)
                sp.dma_start(ring[:, par, :], a["gat_w1"][bass.ds(h, 1)].rearrange("o p n -> (o p) n")) \
                    .then_inc(S[f"w1_in{par}"], 16)

            def load_w2(h, par):
                if not isinstance(h, int) or h >= 2:
                    sp.wait_ge(S["w2_used"], h - 1)
                sp.dma_start(ring[:, 2 + par, :], a["gat_w2"][bass.ds(h, 1)].rearrange("o p n -> (o p) n")) \
                    .then_inc(S[f"w2_in{par}"], 16)

            def load_step(h, par):
                load_w1(h + 1, 1 - par)
                load_avec(h)
                load_w2(h - 1, 1 - par)

            def load_unit(u):
                slot = landed[u][0]
                for name, c0, parts, n in UNITS[u]:
                    sp.dma_start(ring[0:parts, slot, c0:c0 + n], a[name]).then_inc(S[f"slot{slot}_in"], 16)

            sp.dma_start(x[:], a["x"]).then_inc(S["x_in"], 16)
            for n, name in enumerate(("dst", "src")):
                sp.dma_start(idx[:, n, :], a[name]).then_inc(S["graph_in"], 16)
            sp.dma_start(ew[:, 0, :], a["edge_weight"]).then_inc(S["graph_in"], 16)
            w1_0 = a["gat_w1"][0:1].rearrange("o p n -> (o p) n")
            sp.dma_start(ring[:, 0, 0:UNIT // 2], w1_0[:, 0:UNIT // 2]).then_inc(S["w1_first_in"], 16)
            sp.dma_start(ring[:, 0, UNIT // 2:UNIT], w1_0[:, UNIT // 2:UNIT]).then_inc(S["w1_in0"], 16)
            sp.dma_start(cols[:], a["cols"]).then_inc(S["cols_in"], 16)
            load_avec(0)
            load_w1(1, 1)
            load_step(1, 1)
            load_step(2, 0)
            with sp.Fori(1, 3) as i:
                load_step(2 * i + 1, 1)
                load_step(2 * i + 2, 0)
            load_avec(7)
            load_w2(6, 0)
            load_w2(7, 1)
            load_avec(8)

            sp.wait_ge(s("edges_summed"), 1)
            for u in range(len(UNITS)):
                if u == 4:
                    sp.wait_ge(S["hprod"], 7)
                if u == 5:
                    sp.wait_ge(S["hprod"], 8)
                if u == 6:
                    sp.wait_ge(S["w2_used"], 7)
                if u == 7:
                    sp.wait_ge(S["hprod"], 9)
                if u >= SLOTS:
                    sp.wait_ge(s(released[u - SLOTS][0]), released[u - SLOTS][1])
                if u - SLOTS == U_L2:
                    sp.wait_ge(s("w_quantised"), 1)
                load_unit(u)
            for n, (lo, hi) in enumerate(HALVES):
                sp.wait_ge(s("result_ready"), n + 1)
                sp.dma_start(out[:, lo:hi], xb[:, lo:hi]).then_inc(S["out_done"], 16)
            sp.wait_ge(S["out_done"], 32)

        @block.gpsimd
        def _(pool):
            def link(ins):
                chained(pool, "pool_step", ins)

            roots = [0]

            def inverse_root(k):
                roots[0] += 1
                pool.wait_ge(s("var_ready"), k)
                pool.tensor_tensor(rstd[:], var[:], mhalf[:], ALU.pow).then_inc(s("rstd_ready"), 1)

            def inverse_root_twice(k, eps):
                inverse_root(k)
                pool.wait_ge(s("rstd_ready"), roots[0])
                link(pool.tensor_tensor(again[:, 0:1], rstd[:], rstd[:], ALU.mult))
                link(pool.tensor_tensor(again[:, 0:1], again[:, 0:1], mv[:, 1:2], ALU.mult))
                link(pool.tensor_scalar(again[:, 0:1], again[:, 0:1], eps, None, ALU.add))
                link(pool.tensor_tensor(again[:, 0:1], again[:, 0:1], mhalf[:], ALU.pow))
                pool.tensor_tensor(twice, again[:, 0:1], rstd[:], ALU.mult).then_inc(s("rstd_ready"), 1)
                roots[0] += 1

            link(pool.memset(mhalf[:], -0.5))
            pool.memset(shiftm[:], 0.0).then_inc(S["pool_step"], 1)
            used["pool_step"] += 1
            pool.wait_ge(S["pool_step"], used["pool_step"])
            pool.affine_select(out=shiftm[:], in_=shiftm[:], compare_op=ALU.not_equal, fill=1.0, base=P,
                               pattern=[[-1, 3 * P]], channel_multiplier=1).then_inc(s("constants"), 1)
            inverse_root(1)
            pool.wait_ge(s("constants"), 1)
            pool.tensor_copy(identb[:], ident).then_inc(s("constants"), 1)
            link(pool.iota(iotai, [[1, P]], base=0, channel_multiplier=0))
            pool.tensor_copy(iotab, iotai).then_inc(s("constants"), 1)
            pool.memset(ones[:], 1.0).then_inc(s("constants"), 1)
            pool.memset(zrow[:], 0.0).then_inc(s("constants"), 1)
            pool.memset(zT[:], 1.0).then_inc(s("constants"), 1)
            steps8 = tk[:, 0, 0:E1N].bitcast(I32)
            link(pool.iota(steps8, [[-1, E1N]], base=E1N, channel_multiplier=0))
            pool.tensor_copy(desc[:], steps8).then_inc(s("constants"), 1)
            pool.wait_ge(S["graph_in"], 48)
            link(pool.tensor_copy(ewb[:, 0, :], ew[:, 0, :]))
            link(pool.tensor_tensor(ew[:, 1, :], ew[:, 0, :], ewb[:, 0, :], ALU.subtract))
            link(pool.tensor_copy(ewb[:, 1, :], ew[:, 1, :]))
            link(pool.tensor_tensor(ew[:, 0, :], ew[:, 1, :], ewb[:, 1, :], ALU.subtract))
            pool.tensor_copy(ewb[:, 2, :], ew[:, 0, :]).then_inc(s("ew_parts"), 1)
            pool.wait_ge(s("ew_parts"), 1)
            pool.wait_ge(s("onehots"), 2)
            for k in range(3):
                pool.tensor_tensor(oh_src[:, 1 + k], oh_src[:, 0], ewb[:, k, :].unsqueeze(2).broadcast_to([P, EC, P]),
                                   ALU.mult).then_inc(s("ew_rows"), 1)

            def residual_bias(k, bias):
                pool.wait_ge(s("residual"), k)
                pool.tensor_tensor(xb[:], x[:], bias, ALU.add).then_inc(s("xb_ready"), 1)

            def load_row(dst, name, n=D):
                pool.dma_start(dst, broadcast_row(a[name], n)).then_inc(s("in_" + name), 16)

            def inverse_degree_root(n):
                pool.wait_ge(s("degree"), n + 1)
                pool.tensor_tensor(cell("deg_root", 2)[:, n:n + 1], cell("degree", 2)[:, n:n + 1], mhalf[:], ALU.pow) \
                    .then_inc(s("deg_root"), 1)

            inverse_degree_root(0)
            pool.wait_ge(S["small_in"], SMALL)
            pool.wait_ge(S["x_in"], 16)
            pool.tensor_tensor(xb[:], x[:], row0[:], ALU.add).then_inc(s("xb_ready"), 1)

            pool.wait_ge(S["elu_ready"], 8)
            link(pool.memset(g1[0:11, :], 1.0))
            pool.dma_start(g1[8:11, :], a["bk_scale"].rearrange("(o n) -> o n", o=1).broadcast_to([3, D])) \
                .then_inc(s("spec_in"), 16)
            pool.dma_start(g2[0:11, :], a["l0_tail"]).then_inc(s("spec_in"), 16)
            pool.wait_ge(S["hprod"], 9)
            link(pool.memset(state, 0.0))
            for d in range(2):
                m = state[:, 16 * d:16 * d + 16]
                pool.memset(m[:, 1:3], -1.0).then_inc(s("bk_const"), 1)
                pool.memset(m[:, 7:8], -1.0).then_inc(s("bk_const"), 1)
                pool.memset(m[:, 4:5], 1.0).then_inc(s("bk_const"), 1)
                pool.memset(m[:, 8:14:5], 1.0).then_inc(s("bk_const"), 1)
            pool.memset(comb[:, 10:11], 1.0).then_inc(s("bk_const"), 1)
            inverse_degree_root(1)
            inverse_root(2)
            pool.wait_ge(s("spec_in"), 32)
            pool.wait_ge(S["alpha_ready"], 9)
            pool.tensor_tensor(g3[0:11, :], g2[0:11, :], g1[0:11, :], ALU.mult).then_inc(s("tail_ready"), 1)
            load_row(avec[:], "l1_b1", 2 * D)
            pool.wait_ge(s("tail_ready"), 1)
            pool.dma_start(g1[0:G1N * E1N, :], a["l1_b2"]).then_inc(s("in_b2"), 16)

            inverse_root(3)
            residual_bias(2, row1[:])
            load_row(row0[:], "g_in")
            pool.dma_start(g4[0:BIT, :], a["l2_wout"]).then_inc(s("in_wout"), 16)
            pool.wait_ge(S["xb_ready"], 2)
            load_row(row1[:], "l2_b2")
            inverse_root(4)

            inverse_root(5)
            pool.wait_ge(s("in_l2_b2"), 16)
            residual_bias(4, row1[:])
            pool.wait_ge(s("hid1_ready"), 4)
            load_row(avec[:, 0:D], "l3_b1")
            load_row(avec[:, D:2 * D], "bv")
            pool.wait_ge(S["xb_ready"], 3)
            load_row(row1[:], "l3_b2")
            inverse_root_twice(6, RMS_EPS)
            inverse_root(7)

            inverse_root(8)
            pool.wait_ge(s("in_l3_b2"), 16)
            residual_bias(6, row1[:])
            pool.dma_start(row0[0:MLP + 1, :], a["fc2"]).then_inc(s("in_fc2"), 16)
            inverse_root_twice(9, LN_EPS)
            load_row(avec[:, 0:D], "bo")
            inverse_root(10)
            pool.wait_ge(s("out_rows"), 2)
            pool.tensor_tensor(xb[:], x[:], g3[:], ALU.add).then_inc(s("xb_ready"), 1)

        @block.scalar
        def _(act):
            def copy(dst, src):
                return nc.scalar.activation(dst, src, ACT.Copy)

            def link(ins):
                chained(act, "act_step", ins)

            def part_T(k):
                for n in (0, 2):
                    act.wait_ge(s("T_ps"), 3 * k - 2 + n)
                    copy(xT[:, 2 * n:2 * n + 2, :], bank(4 + n, 2 * P).rearrange("p (c n) -> p c n", n=P)) \
                        .then_inc(s("T_outer_ready"), 1)

            def affine_T(name, dst, vectors, signal):
                for value, chunks in ((1, (0, 1)), (3, (4,))):
                    act.wait_ge(s(name), value)
                    for c in chunks:
                        last = nc.scalar.activation(dst[:, c * P:(c + 1) * P], hat_at(c), ACT.Identity,
                                                    bias=col(vectors + "_b", c), scale=col(vectors + "_g", c))
                last.then_inc(s(signal), 1)

            def head_rows(h, par):
                wait(act, "hprod", h + 1)
                if not isinstance(h, int) or h >= 2:
                    wait(act, "agg_ready", h - 1)
                    wait(act, "alpha_ready", h - 1)
                copy(h1[:, par * D:(par + 1) * D], head_psum(par)).then_inc(S["h_rows"], 1)

            def head_exp(h):
                wait(act, "negmax", h + 1)
                nc.scalar.activation(att[:, 0, :], att[:, 1, :], ACT.Exp, bias=soft[:, 1:2]) \
                    .then_inc(S["exped"], 1)

            def head_attnT(h, par):
                wait(act, "attnT_ps", h + 1)
                copy(attnT[:, par, :], bank(7, P, 384)).then_inc(S["attnT_ready"], 1)

            def head_elu(h):
                wait(act, "z_neg", h + 1)
                nc.scalar.activation(g2[:], g2[:], ACT.Exp).then_inc(S["z_exp"], 1)

            def step(h, par, last=False):
                head_exp(h)
                head_attnT(h, par)
                if not last:
                    head_rows(h + 1, 1 - par)
                head_elu(h)

            act.wait_ge(s("constants"), 1)
            nc.scalar.activation(cell("scrap"), mhalf[:], ACT.Exp)

            part_T(1)
            head_rows(0, 0)
            step(0, 0)
            step(1, 1)
            act.dma_start(row0[:], broadcast_row(a["gat_b2"], D)).then_inc(S["small_in"], 16)
            act.dma_start(row1[:], broadcast_row(a["l1_b"], D)).then_inc(S["small_in"], 16)
            act.dma_start(rows[:], broadcast_row(a["rows"], NROWS)).then_inc(S["small_in"], 16)
            act.dma_start(gatew[:], a["gatew"]).then_inc(S["small_in"], 16)
            act.dma_start(gatew1[:], a["gatew1"]).then_inc(S["small_in"], 16)
            act.dma_start(bias1[0:DOWN, 0:1], a["bd"]).then_inc(S["small_in"], 16)
            act.dma_start(bias1[0:MLP, 1:2], a["fc1_b"]).then_inc(S["small_in"], 16)
            step(2, 0)
            with act.Fori(1, 3) as i:
                step(2 * i + 1, 1)
                step(2 * i + 2, 0)
            step(7, 1, last=True)
            act.wait_ge(s("gat2_first"), 1)
            copy(h1[:, 0:WIN], bank(4)).then_inc(s("gat2_rows"), 1)
            head_exp(8)
            head_attnT(8, 0)

            part_T(2)
            act.wait_ge(s("top_shifted"), 1)
            nc.scalar.activation(tk[:, 3, 0:E0], tk[:, 3, 0:E0], ACT.Exp).then_inc(s("top_exped"), 1)
            act.wait_ge(s("hid0_ready"), 1)
            nc.scalar.activation(h1[:, 0:H0], h1[:, 0:H0], ACT.Gelu_apprx_tanh).then_inc(s("gelu0"), 1)
            act.wait_ge(s("hid0_ps"), 1)
            copy(h1[:, H0:2 * H0], ps[:, 4 * WIN:4 * WIN + H0]).then_inc(s("hid0T"), 1)

            part_T(3)
            part_T(4)
            act.wait_ge(s("top_shifted"), 2)
            nc.scalar.activation(tk[:, 3, :], tk[:, 3, :], ACT.Exp).then_inc(s("top_exped"), 1)
            act.wait_ge(s("top_shifted"), 3)
            nc.scalar.activation(tk[:, 3, 0:G1N], tk[:, 3, 0:G1N], ACT.Exp).then_inc(s("top_exped"), 1)

            def hidden_gelu(g):
                act.wait_ge(s("hid1_ready"), g + 1)
                nc.scalar.activation(h1[:, g * H0:(g + 1) * H0], h1[:, g * H0:(g + 1) * H0], ACT.Gelu) \
                    .then_inc(s("gelu1"), 1)

            def hidden_T(g):
                act.wait_ge(s("hid1_ps"), g + 1)
                copy(h2[:, g * H0:(g + 1) * H0], bank(4 + g % 2, H0)).then_inc(s("hid1T"), 1)

            hidden_gelu(0)
            hidden_gelu(1)
            hidden_T(0)
            hidden_gelu(2)
            hidden_T(1)
            hidden_gelu(3)
            hidden_T(2)
            hidden_T(3)

            part_T(5)
            act.wait_ge(s("l2_ps"), 1)
            act.wait_ge(s("constants"), 6)
            nc.scalar.activation(zT[0:DOWN, :], bank(7, P, 0, DOWN), ACT.Relu, bias=bias1[0:DOWN, 0:1]) \
                .then_inc(s("l2_copied"), 1)
            part_T(6)
            act.wait_ge(s("l2_ps"), 5)
            copy(g3[:, 0:HID2], bank(2, HID2)).then_inc(s("l2_copied"), 1)
            nc.scalar.activation(cell("scrap"), mhalf[:], ACT.Exp)
            act.wait_ge(s("bits_ps"), 1)
            copy(bitsT[:, 0:D // 2], bank(4, D // 4).bitcast(BF16)).then_inc(s("bitsT_ready"), 1)
            act.wait_ge(s("gated"), 1)
            nc.scalar.activation(g1[:, 2 * BIT:3 * BIT], g1[:, BIT:2 * BIT], ACT.Exp, scale=-1.0).then_inc(s("gate_exp"), 1)

            part_T(7)
            part_T(8)

            nc.scalar.activation(cell("scrap"), mhalf[:], ACT.Gelu)
            affine_T("zhatT_ps", xT[:].rearrange("p c n -> p (c n)"), "r_ln", "xrT_ready")
            affine_T("zhatT_ps", g1, "ln1", "xaT_ready")
            for f in range(4):
                act.wait_ge(s("rin_ps"), f + 1)
                nc.scalar.activation(h1[:, f * P:(f + 1) * P], bank(f % 2, P), ACT.Gelu, bias=col("r_in_b", f)) \
                    .then_inc(s("eT_ready"), 1)
            act.wait_ge(s("ro1_bias"), 1)
            for f in range(4):
                act.wait_ge(s("ro1_ps"), f + 1)
                nc.scalar.activation(h1[:, 512 + f * P:512 + (f + 1) * P], bank(6 + f % 2, P), ACT.Gelu,
                                     bias=cell("ro1_bias", 4)[:, f:f + 1]).then_inc(s("h1T_ready"), 1)
            for f in range(2):
                act.wait_ge(s("ro2_ps"), f + 1)
                nc.scalar.activation(h1[:, 1024 + f * P:1024 + (f + 1) * P], bank(f % 2, P), ACT.Gelu,
                                     bias=col("r_o2_b", f)).then_inc(s("h2T_ready"), 1)
            for h in range(AH):
                if h % 4 == 0:
                    act.wait_ge(s("smax"), h // 4 + 1)
                if h == 0:
                    act.wait_ge(s("ro3_ps"), 1)
                nc.scalar.activation(h1[:, h * P:(h + 1) * P], score_ps(h), ACT.Exp,
                                     bias=cell("s_negmax", AH)[:, h:h + 1], scale=AD ** -0.5,
                                     accum_out=cell("s_sum", AH)[:, h:h + 1]).then_inc(s("sexp"), 1)
            for g in range(3):
                act.wait_ge(s("pT_ps"), g + 1)
                copy(h2[:, g * 512:(g + 1) * 512], bank((4, 5, 3)[g])).then_inc(s("pT_ready"), 1)
            o_ps = ps[:, 0:AH * P].rearrange("p (c b n) -> p c b n", b=2, n=P)
            for n, (lo, hi) in enumerate(((0, 4), (4, C))):
                act.wait_ge(s("oT_ps"), n + 1)
                copy(xT[0:AD, lo:hi, :], o_ps[0:AD, lo:hi, 0, :]).then_inc(s("o_even_ready"), 1)
            affine_T("hhatT_ps", g2, "ln2", "xfT_ready")
            act.wait_ge(s("fc1_ps"), 1)
            nc.scalar.activation(zT[0:MLP, :], bank(3, P, 0, MLP), ACT.Gelu, bias=bias1[0:MLP, 1:2]) \
                .then_inc(s("fc1_ready"), 1)
            part_T(9)
            part_T(10)

        @block.vector
        def _(dve):
            def link(ins):
                chained(dve, "dve_step", ins)

            def statistics(n, src):
                lo, hi = HALVES[n]
                nc.vector.bn_stats(stats[:, n, :], src[:, lo:hi]).then_inc(S["dve_step"], 1)
                used["dve_step"] += 1
                if n == 1:
                    dve.wait_ge(S["dve_step"], used["dve_step"])

            def whiten(k):
                link(nc.vector.bn_aggr(mv[:], stats[:].rearrange("p a b -> p (a b)")))
                nc.vector.tensor_scalar(var[:], mv[:, 1:2], LN_EPS, None, ALU.add).then_inc(s("var_ready"), 1)
                dve.wait_ge(s("rstd_ready"), k)

            def normalise(k, dst, src, signal):
                whiten(k)
                for lo, hi in ((0, D // 2), (D // 2, D)):
                    nc.vector.tensor_scalar(dst[:, lo:hi], src[:, lo:hi], mv[:, 0:1], rstd[:], ALU.subtract, ALU.mult) \
                        .then_inc(s(signal), 1)

            def centre(k):
                link(nc.vector.bn_aggr(mv[:], stats[:].rearrange("p a b -> p (a b)")))
                nc.vector.tensor_scalar(var[:], mv[:, 1:2], LN_EPS, None, ALU.add).then_inc(s("var_ready"), 1)
                for lo, hi in ((0, D // 2), (D // 2, D)):
                    nc.vector.tensor_scalar(xn[:, lo:hi], x[:, lo:hi], mv[:, 0:1], None, ALU.subtract) \
                        .then_inc(s("xn_ready"), 1)

            def scaled(dst, product, bias):
                return nc.vector.scalar_tensor_tensor(out=dst, in0=product, scalar=rstd[:], in1=bias, op0=ALU.mult,
                                                      op1=ALU.add)

            def affine_T(name, dst, vectors, signal):
                for value, chunks in ((2, (2, 3)), (4, (5,))):
                    dve.wait_ge(s(name), value)
                    for c in chunks:
                        last = nc.vector.tensor_scalar(dst[:, c * P:(c + 1) * P], hat_at(c), col(vectors + "_g", c),
                                                       col(vectors + "_b", c), ALU.mult, ALU.add)
                last.then_inc(s(signal), 1)

            def part_T(k):
                dve.wait_ge(s("T_ps"), 3 * k - 1)
                nc.vector.tensor_copy(xT[:, 2:4, :], bank(5, 2 * P).rearrange("p (c n) -> p c n", n=P)) \
                    .then_inc(s("T_inner_ready"), 1)

            dve.wait_ge(S["x_in"], 16)
            for n in range(2):
                statistics(n, x)
            normalise(1, xn, x, "xn_ready")
            dve.wait_ge(S["graph_in"], 48)
            link(nc.vector.tensor_copy(idxb[:], idx[:]))
            dve.wait_ge(s("constants"), 3)
            iota_rows = iotab.unsqueeze(1).broadcast_to([P, EC, P])
            part_T(1)
            for n, dst in ((0, oh_dst), (1, oh_src[:, 0])):
                nc.vector.tensor_tensor(dst, iota_rows, idxb[:, n, :].unsqueeze(2).broadcast_to([P, EC, P]),
                                        ALU.is_equal).then_inc(s("onehots"), 1)
            def head_alphas(h, par):
                wait(dve, "h_rows", h + 1)
                dve.wait_ge(S["avec_in"], 16 * h + 16)
                wait(dve, "alpha_ready", h)
                hp = h1[:, par * D:(par + 1) * D]
                nc.vector.tensor_tensor_reduce(g3[:], hp, avec[:, 0:D], 1.0, 0.0, ALU.mult, ALU.add,
                                               alpha[:, par, 0:1]).then_inc(S["alpha_rows"], 1)
                wait(dve, "alpha_rows", h + 1)
                nc.vector.tensor_tensor_reduce(g4[:], hp, avec[:, D:2 * D], 1.0, 0.0, ALU.mult, ALU.add,
                                               alpha[:, par, 1:2]).then_inc(S["alpha_ready"], 1)

            def head_softmax(h, par):
                wait(dve, "score_row_ps", h + 1)
                wait(dve, "attn_ready", h)
                if not isinstance(h, int) or h >= 1:
                    wait(dve, "attnT_ps", h)
                nc.vector.scalar_tensor_tensor(out=att[:, 0, :], in0=bank(7, P, 256), scalar=alpha[:, par, 1:2],
                                               in1=absent[:], op0=ALU.add, op1=ALU.add).then_inc(S["score_sum"], 1)
                wait(dve, "score_sum", h + 1)
                nc.vector.scalar_tensor_tensor(out=att[:, 1, :], in0=att[:, 0, :], scalar=LEAK, in1=att[:, 0, :],
                                               op0=ALU.mult, op1=ALU.max).then_inc(S["score_leaky"], 1)
                wait(dve, "score_leaky", h + 1)
                nc.vector.tensor_reduce(soft[:, 1:2], att[:, 1, :], AX.X, ALU.max, negate=True).then_inc(S["negmax"], 1)
                wait(dve, "exped", h + 1)
                nc.vector.tensor_tensor_reduce(att[:, 1, :], att[:, 0, :], count[:], 1.0, SEG_EPS, ALU.mult, ALU.add,
                                               soft[:, 2:3]).then_inc(S["weighed"], 1)
                wait(dve, "weighed", h + 1)
                nc.vector.reciprocal(soft[:, 3:4], soft[:, 2:3]).then_inc(S["denom_ready"], 1)
                wait(dve, "denom_ready", h + 1)
                nc.vector.tensor_scalar(att[:, 1, :], att[:, 1, :], soft[:, 3:4], None, ALU.mult) \
                    .then_inc(S["attn_ready"], 1)

            def head_z(h):
                wait(dve, "agg_ready", h + 1)
                wait(dve, "elu_ready", h)
                if isinstance(h, int):
                    b1 = cols[:, C * h:C * h + C]
                else:
                    b1 = cols[:, bass.ds(h * C, C)]
                nc.vector.tensor_tensor(g1[:].rearrange("p (c n) -> p c n", n=P),
                                        ps[:, 6 * WIN:6 * WIN + D].rearrange("p (c n) -> p c n", n=P),
                                        b1.unsqueeze(2).broadcast_to([P, C, P]), ALU.add).then_inc(S["z_ready"], 1)
                wait(dve, "z_ready", h + 1)
                nc.vector.tensor_scalar(g2[:], g1[:], 0.0, None, ALU.min).then_inc(S["z_neg"], 1)

            def head_elu(h, par):
                wait(dve, "z_exp", h + 1)
                if not isinstance(h, int) or h >= 2:
                    wait(dve, "w2_used", h - 1)
                nc.vector.scalar_tensor_tensor(out=h2[:, par * D:(par + 1) * D], in0=g2[:], scalar=-1.0, in1=g1[:],
                                               op0=ALU.add, op1=ALU.max).then_inc(S["elu_ready"], 1)

            def step(h, par, last=False):
                head_softmax(h, par)
                if not last:
                    head_alphas(h + 1, 1 - par)
                head_z(h)
                head_elu(h, par)

            deg, root = cell("degree", 2), cell("deg_root", 2)

            def half_adjacency(n, adjT):
                nc.vector.tensor_reduce(deg[:, n:n + 1], adjT[:], AX.X, ALU.add).then_inc(s("degree"), 1)
                dve.wait_ge(s("deg_root"), n + 1)
                nc.vector.tensor_scalar(adjT[:], adjT[:], root[:, n:n + 1], None, ALU.mult).then_inc(s("adj_half"), 1)

            def whole_adjacency(n, adjT):
                dve.wait_ge(s("adj_ps"), n + 1)
                nc.vector.tensor_scalar(adjT[:], bank(3, P), root[:, n:n + 1], None, ALU.mult).then_inc(s("adj_ready"), 1)

            dve.wait_ge(s("onehots"), 2)
            head_alphas(0, 0)
            dve.wait_ge(s("counted"), 1)
            link(nc.vector.tensor_copy(count[:], bank(3, P)))
            link(nc.vector.tensor_scalar(absent[:], count[:], 1.0, None, ALU.min))
            link(nc.vector.tensor_scalar(absent[:], absent[:], BIG, -BIG, ALU.mult, ALU.add))
            dve.wait_ge(S["cols_in"], 16)
            head_softmax(0, 0)
            head_alphas(1, 1)
            head_z(0)
            head_softmax(1, 1)
            head_elu(0, 0)
            head_alphas(2, 0)
            head_z(1)
            head_elu(1, 1)
            link(nc.vector.tensor_tensor(adj1T[:], count[:], ident, ALU.add))
            half_adjacency(0, adj1T)
            step(2, 0)
            whole_adjacency(0, adj1T)
            with dve.Fori(1, 3) as i:
                step(2 * i + 1, 1)
                step(2 * i + 2, 0)
            step(7, 1, last=True)

            missing = cell("missing", 14)
            for lv in range(7):
                for d, off in enumerate((P + 2 ** lv, P - 2 ** lv)):
                    last = nc.vector.tensor_reduce(missing[:, 2 * lv + d:2 * lv + d + 1], shiftm[:, off:off + P], AX.X, ALU.add)
            link(last)
            link(nc.vector.tensor_scalar(missing, missing, -1.0, 1.0, ALU.mult, ALU.add))
            dve.wait_ge(S["hprod"], 9)
            nc.vector.tensor_copy(h1[:, WIN:D], bank(5, D - WIN)).then_inc(S["h_rows"], 1)
            dve.wait_ge(s("gat2_rows"), 1)
            head_alphas(8, 0)
            head_softmax(8, 0)

            dve.wait_ge(s("edges_summed"), 1)
            link(nc.vector.tensor_tensor(adj2T[:], bank(3, P, P), ident, ALU.add))
            link(nc.vector.tensor_tensor(adj2T[:], adj2T[:], bank(3, P, 2 * P), ALU.add))
            link(nc.vector.tensor_tensor(adj2T[:], adj2T[:], bank(3, P, 3 * P), ALU.add))
            half_adjacency(1, adj2T)

            def add_residual(k, at, base, worth_each=None):
                for n, (lo, hi) in enumerate(HALVES):
                    dve.wait_ge(s("rows_ps"), 2 * k - 1 + n)
                    part = ps[:, at + lo:at + hi]
                    if worth_each is None:
                        ins = nc.vector.tensor_tensor(x[:, lo:hi], part, base[:, lo:hi], ALU.add)
                    else:
                        ins = nc.vector.scalar_tensor_tensor(out=x[:, lo:hi], in0=part, scalar=worth_each, in1=base[:, lo:hi],
                                                             op0=ALU.mult, op1=ALU.add)
                    if n == 0:
                        link(ins)
                    else:
                        ins.then_inc(s("residual"), 1)
                        dve.wait_ge(s("residual"), k)
                    statistics(n, x)

            dve.wait_ge(S["xb_ready"], 1)
            add_residual(1, 0, xb)

            centre(2)
            part_T(2)

            def grouped(v, groups, n):
                return v.rearrange("p (g n) -> p g n", n=n)

            def wide(v, groups, n):
                return v.unsqueeze(2).broadcast_to([P, groups, n])

            def pick(src, dst, groups, n, shifted=None):
                top, order = tks[:, 1, 0:groups], desc[:, 0:n].unsqueeze(1).broadcast_to([P, groups, n])
                t = grouped(tk[:, 0, 0:groups * n], groups, n)
                link(nc.vector.tensor_reduce(top, src, AX.X, ALU.max))
                if shifted is not None:
                    link(nc.vector.tensor_tensor(shifted, src, wide(top, groups, n), ALU.subtract))
                link(nc.vector.tensor_tensor(t, src, wide(top, groups, n), ALU.is_equal))
                link(nc.vector.tensor_tensor(t, t, order, ALU.mult))
                link(nc.vector.tensor_reduce(top, t, AX.X, ALU.max))
                return nc.vector.tensor_tensor(dst, t, wide(top, groups, n), ALU.is_equal)

            def pick_first(k, logits, groups, n):
                w = groups * n
                pick(grouped(logits, groups, n), grouped(tk[:, 2, 0:w], groups, n), groups, n,
                     grouped(tk[:, 3, 0:w], groups, n)).then_inc(s("top_shifted"), 1)
                dve.wait_ge(s("top_shifted"), k)

            def pick_second(logits, groups, n):
                w = groups * n
                link(nc.vector.scalar_tensor_tensor(out=tk[:, 1, 0:w], in0=tk[:, 2, 0:w], scalar=-BIG, in1=logits,
                                                    op0=ALU.mult, op1=ALU.add))
                link(pick(grouped(tk[:, 1, 0:w], groups, n), grouped(tk[:, 4, 0:w], groups, n), groups, n))
                link(nc.vector.tensor_tensor(tk[:, 2, 0:w], tk[:, 2, 0:w], tk[:, 4, 0:w], ALU.add))

            def top_shares(k, dst, groups, n):
                w = groups * n
                e, top = tk[:, 3, 0:w], tks[:, 1, 0:groups]
                dve.wait_ge(s("top_exped"), k)
                link(nc.vector.tensor_tensor(e, e, tk[:, 2, 0:w], ALU.mult))
                link(nc.vector.tensor_reduce(top, grouped(e, groups, n), AX.X, ALU.add))
                link(nc.vector.reciprocal(top, top))
                link(nc.vector.tensor_tensor(grouped(dst, groups, n), grouped(e, groups, n), wide(top, groups, n), ALU.mult))

            directions = state.rearrange("p (d m) -> p d m", m=16)

            def green_level(lv):
                dve.wait_ge(s("green_state"), lv + 1)
                nc.vector.tensor_tensor(prod.rearrange("p (d m k) -> p d m k", d=2, k=5)[:, :, :, 4], directions,
                                        missing[:, 2 * lv:2 * lv + 2].unsqueeze(2).broadcast_to([P, 2, 16]), ALU.mult) \
                    .then_inc(S["dve_step"], 1)
                used["dve_step"] += 1
                dve.wait_ge(s("shifted"), lv + 1)
                for d in range(2):
                    own = state[:, 16 * d:16 * d + 16].rearrange("p (a k) -> p a k", k=4)
                    far = bank(7, 16, 16 * d).rearrange("p (k b) -> p b k", b=4)
                    nc.vector.tensor_tensor(prod[:, 80 * d:80 * d + 80].rearrange("p (a b k) -> p a b k", a=4, k=5)[:, :, :, 0:4],
                                            own.unsqueeze(2).broadcast_to([P, 4, 4, 4]),
                                            far.unsqueeze(1).broadcast_to([P, 4, 4, 4]), ALU.mult) \
                        .then_inc(S["dve_step"], 1)
                used["dve_step"] += 2
                dve.wait_ge(S["dve_step"], used["dve_step"])
                last = nc.vector.tensor_reduce(state, prod.rearrange("p (m k) -> p m k", k=5), AX.X, ALU.add)
                if lv == 4:
                    largest = cell("largest", 2)
                    link(last)
                    link(nc.vector.tensor_reduce(largest, directions, AX.X, ALU.max, apply_absolute_value=True))
                    link(nc.vector.reciprocal(largest, largest))
                    last = nc.vector.tensor_tensor(directions, directions, largest.unsqueeze(2).broadcast_to([P, 2, 16]),
                                                   ALU.mult)
                last.then_inc(s("green_state"), 1)

            dve.wait_ge(s("gate_ps"), 1)
            level = cell("level")
            dve.wait_ge(s("rstd_ready"), 2)
            link(scaled(lin[:, 0:E0 + 1], bank(7, E0 + 1), row("l0_gate")))
            link(nc.vector.tensor_scalar(level, lin[:, E0:E0 + 1], 3.0, -3.0, ALU.min, ALU.max))
            link(nc.vector.tensor_scalar(level, level, -2.0, None, ALU.add))
            dve.wait_ge(s("bk_const"), 9)
            nc.vector.tensor_copy(directions[:, :, 0:6:5], level.unsqueeze(2).broadcast_to([P, 2, 2])) \
                .then_inc(s("green_state"), 1)
            dve.wait_ge(s("constants"), 7)
            pick_first(1, lin[:, 0:E0], 1, E0)
            green_level(0)
            whole_adjacency(1, adj2T)
            pick_second(lin[:, 0:E0], 1, E0)
            green_level(1)
            top_shares(1, comb[:, 0:E0], 1, E0)
            green_level(2)
            dve.wait_ge(s("hid0_mm"), 1)
            scaled(h1[:, 0:H0], bank(0, H0), row("l0_b1")).then_inc(s("hid0_ready"), 1)
            green_level(3)
            dve.wait_ge(s("gelu0"), 1)
            nc.vector.tensor_tensor(grouped(h1[:, 0:H0], E0, F0), grouped(h1[:, 0:H0], E0, F0),
                                    wide(comb[:, 0:E0], E0, F0), ALU.mult).then_inc(s("hid0_scaled"), 1)
            for lv in range(4, 7):
                green_level(lv)
            dve.wait_ge(s("green_state"), 8)
            pq = state[:, 0:16].rearrange("p (m r) -> p m r", r=8)[:, :, 0:2]
            w_blk = state[:, 24:32].rearrange("p (r c) -> p c r", c=4)[:, 0:2, :]
            q_blk = state[:, 8:16].rearrange("p (r c) -> p c r", c=4)[:, 0:2, :]
            r_vec = state[:, 16:18]
            terms, both, qw = cell("terms", 12), cell("pw_rq", 2), cell("qw", 2)
            for m, (vector, block_, at) in enumerate(((pq[:, 0, :], w_blk, 0), (r_vec, q_blk, 2))):
                nc.vector.tensor_tensor(terms[:, 0:8].rearrange("p (c r) -> p c r", c=2)[:, :, at:at + 2],
                                        vector.unsqueeze(1).broadcast_to([P, 2, 2]), block_, ALU.mult) \
                    .then_inc(S["dve_step"], 1)
            used["dve_step"] += 2
            link(nc.vector.tensor_tensor(terms[:, 8:12].rearrange("p (c r) -> p c r", c=2),
                                         pq[:, 1, :].unsqueeze(1).broadcast_to([P, 2, 2]), w_blk, ALU.mult))
            nc.vector.tensor_reduce(both, terms[:, 0:8].rearrange("p (c r) -> p c r", c=2), AX.X, ALU.add) \
                .then_inc(S["dve_step"], 1)
            used["dve_step"] += 1
            link(nc.vector.tensor_reduce(qw, terms[:, 8:12].rearrange("p (c r) -> p c r", c=2), AX.X, ALU.add))
            den = cell("den", 2)
            link(nc.vector.scalar_tensor_tensor(out=den, in0=qw, scalar=level, in1=both, op0=ALU.mult, op1=ALU.subtract))
            nc.vector.tensor_tensor(den[:, 0:1], den[:, 0:1], qw[:, 1:2], ALU.add).then_inc(S["dve_step"], 1)
            used["dve_step"] += 1
            link(nc.vector.tensor_tensor(den[:, 1:2], den[:, 1:2], qw[:, 0:1], ALU.subtract))
            norm, cross, gre = cell("norm"), cell("cross"), cell("green", 2)
            nc.vector.tensor_tensor_reduce(terms[:, 0:2], den, den, 1.0, 0.0, ALU.mult, ALU.add, norm).then_inc(S["dve_step"], 1)
            nc.vector.tensor_tensor_reduce(terms[:, 2:4], qw, den, -1.0, 0.0, ALU.mult, ALU.add, gre[:, 0:1]) \
                .then_inc(S["dve_step"], 1)
            used["dve_step"] += 2
            link(nc.vector.tensor_tensor(cross, qw[:, 1:2], den[:, 0:1], ALU.mult))
            nc.vector.reciprocal(norm, norm).then_inc(S["dve_step"], 1)
            used["dve_step"] += 1
            link(nc.vector.scalar_tensor_tensor(out=gre[:, 1:2], in0=qw[:, 0:1], scalar=den[:, 1:2], in1=cross,
                                                op0=ALU.mult, op1=ALU.subtract))
            link(nc.vector.tensor_scalar(gre, gre, norm, 10.0, ALU.mult, ALU.min))
            nc.vector.tensor_scalar(comb[:, 8:10], gre, -10.0, None, ALU.max).then_inc(s("comb_ready"), 1)
            dve.wait_ge(s("combT_ps"), 1)
            nc.vector.tensor_copy(combT[0:11, :], bank(7, P, 0, 11)).then_inc(s("combT_ready"), 1)
            add_residual(2, 2 * WIN, x)

            normalise(3, xn, x, "xn_ready")
            part_T(3)
            dve.wait_ge(S["xb_ready"], 2)
            add_residual(3, 0, xb)

            centre(4)
            part_T(4)
            NG = G1N * E1N
            dve.wait_ge(s("gate_ps"), 2)
            dve.wait_ge(s("rstd_ready"), 4)
            link(scaled(lin[:, 0:G1N + NG], bank(7, G1N + NG), row("l1_gate")))
            pick_first(2, lin[:, G1N:G1N + NG], G1N, E1N)
            pick_second(lin[:, G1N:G1N + NG], G1N, E1N)
            top_shares(2, comb[:, 0:NG], G1N, E1N)
            pick_first(3, lin[:, 0:G1N], 1, G1N)
            pick_second(lin[:, 0:G1N], 1, G1N)
            top_shares(3, comb[:, 32:36], 1, G1N)
            nc.vector.tensor_tensor(grouped(comb[:, 0:NG], G1N, E1N), grouped(comb[:, 0:NG], G1N, E1N),
                                    wide(comb[:, 32:36], G1N, E1N), ALU.mult).then_inc(s("comb_ready"), 1)
            dve.wait_ge(s("comb_ready"), 2)
            dve.wait_ge(s("in_l1_b1"), 16)

            def hidden_bias(g):
                dve.wait_ge(s("hid1_mm"), g + 1)
                scaled(h1[:, g * H0:(g + 1) * H0], bank(g, H0), avec[:, g * H0:(g + 1) * H0]).then_inc(s("hid1_ready"), 1)

            def hidden_scale(g):
                dve.wait_ge(s("gelu1"), g + 1)
                v = grouped(h1[:, g * H0:(g + 1) * H0], E0, F0)
                nc.vector.tensor_tensor(v, v, wide(comb[:, E0 * g:E0 * g + E0], E0, F0), ALU.mult) \
                    .then_inc(s("hid1_scaled"), 1)

            hidden_bias(0)
            dve.wait_ge(s("combT_ps"), 2)
            nc.vector.tensor_copy(combT[:], bank(7, P, 0, 32)).then_inc(s("combT_ready"), 1)
            hidden_bias(1)
            hidden_scale(0)
            hidden_bias(2)
            hidden_scale(1)
            hidden_bias(3)
            hidden_scale(2)
            hidden_scale(3)

            dve.wait_ge(s("in_wout"), 16)
            wait_unit(dve, U_L2)
            w_in = unit(U_L2, "l2_win")
            wabs, worth, winv = cell("w_abs", 2), cell("w_worth", 2), cell("w_inverse", 2)
            nc.vector.tensor_reduce(wabs[:, 0:1], w_in, AX.X, ALU.add, apply_absolute_value=True).then_inc(s("wsum_ready"), 1)
            nc.vector.tensor_reduce(wabs[0:BIT, 1:2], g4[0:BIT, :], AX.X, ALU.add, apply_absolute_value=True) \
                .then_inc(s("wsum_ready"), 1)
            dve.wait_ge(s("wsum_ps"), 1)
            for n, size in enumerate((2 * BIT * D, BIT * D)):
                link(nc.vector.tensor_scalar(worth[:, n:n + 1], bank(7, 1, P + n), 1.0 / size, QUANT_EPS, ALU.mult, ALU.max))
            link(nc.vector.reciprocal(winv, worth))
            link(nc.vector.tensor_scalar(g1[:, 0:384], w_in, winv[:, 0:1], ROUND, ALU.mult, ALU.add))
            link(nc.vector.tensor_scalar(g1[:, 0:384], g1[:, 0:384], ROUND, 1.0, ALU.subtract, ALU.min))
            nc.vector.tensor_scalar(w_in_q, g1[:, 0:384], -1.0, None, ALU.max).then_inc(s("w_quantised"), 1)
            dve.wait_ge(s("w_quantised"), 1)
            link(nc.vector.tensor_scalar(g1[0:BIT, :], g4[0:BIT, :], winv[0:BIT, 1:2], ROUND, ALU.mult, ALU.add))
            link(nc.vector.tensor_scalar(g1[0:BIT, :], g1[0:BIT, :], ROUND, 1.0, ALU.subtract, ALU.min))
            nc.vector.tensor_scalar(w_out_q, g1[0:BIT, :], -1.0, None, ALU.max).then_inc(s("w_quantised"), 1)
            dve.wait_ge(s("w_quantised"), 2)
            add_residual(4, 0, x)

            normalise(5, xn, x, "xn_ready")
            part_T(5)
            for n, (lo, hi) in enumerate(HALVES):
                dve.wait_ge(s("l2_ps"), n + 2)
                nc.vector.tensor_tensor(g1[:, lo:hi], ps[:, lo:hi], xn[:, lo:hi], ALU.add).then_inc(s("node_rows"), 1)
            part_T(6)
            dve.wait_ge(s("l2_ps"), 4)
            nc.vector.tensor_scalar(g2[:, 0:HID2], bank(7, HID2), 0.0, None, ALU.max).then_inc(s("node_rows"), 1)
            dve.wait_ge(S["xb_ready"], 3)
            add_residual(5, 0, xb)

            largest, scale, square = cell("act_max"), cell("act_scale"), cell("square")
            link(nc.vector.bn_aggr(mv[:], stats[:].rearrange("p a b -> p (a b)")))
            nc.vector.tensor_scalar(var[:], mv[:, 1:2], LN_EPS, None, ALU.add).then_inc(s("var_ready"), 1)
            dve.wait_ge(s("in_g_in"), 16)
            link(nc.vector.scalar_tensor_tensor(out=g1[:], in0=x[:], scalar=mv[:, 0:1], in1=row0[:], op0=ALU.subtract,
                                                op1=ALU.mult))
            link(nc.vector.tensor_reduce(largest, g1[:], AX.X, ALU.max, apply_absolute_value=True))
            dve.wait_ge(s("rstd_ready"), 7)

            def integers(dst, tmp, root, n, parts):
                link(nc.vector.tensor_scalar(largest, largest, root, QUANT_EPS, ALU.mult, ALU.max))
                link(nc.vector.reciprocal(scale, largest))
                link(nc.vector.tensor_scalar(scale, scale, 127.0, root, ALU.mult, ALU.mult))
                cuts = [(k * n // parts, (k + 1) * n // parts) for k in range(parts)]
                for first, op0, second, op1 in ((scale, ALU.mult, ROUND, ALU.add), (ROUND, ALU.subtract, 127.0, ALU.min)):
                    base = used["dve_step"]
                    for k, (lo, hi) in enumerate(cuts):
                        if op0 == ALU.subtract:
                            dve.wait_ge(S["dve_step"], base - parts + k + 1)
                        nc.vector.tensor_scalar(tmp[:, lo:hi], tmp[:, lo:hi], first, second, op0, op1) \
                            .then_inc(S["dve_step"], 1)
                        used["dve_step"] += 1
                for k, (lo, hi) in enumerate(cuts):
                    dve.wait_ge(S["dve_step"], used["dve_step"] - parts + k + 1)
                    nc.vector.tensor_scalar(dst[:, lo:hi], tmp[:, lo:hi], -128.0, None, ALU.max).then_inc(s("bits_ready"), 1)

            def quantise(k, dst, src, gain, n, tmp):
                link(nc.vector.tensor_tensor_reduce(tmp, src, src, 1.0, 0.0, ALU.mult, ALU.add, square))
                nc.vector.tensor_scalar(var[:], square, 1.0 / n, RMS_EPS, ALU.mult, ALU.add).then_inc(s("var_ready"), 1)
                link(nc.vector.tensor_tensor(tmp, src, gain, ALU.mult))
                link(nc.vector.tensor_reduce(largest, tmp, AX.X, ALU.max, apply_absolute_value=True))
                dve.wait_ge(s("rstd_ready"), k)
                integers(dst, tmp, rstd[:], n, 1)

            def worth_of(n, dst):
                link(nc.vector.scalar_tensor_tensor(out=dst, in0=largest, scalar=1.0 / 127.0, in1=worth[:, n:n + 1],
                                                    op0=ALU.mult, op1=ALU.mult))

            integers(bits, g1[:], twice, D, 2)
            dve.wait_ge(s("bits_ps"), 2)
            nc.vector.tensor_copy(bitsT[:, D // 2:D], bank(5, D // 4).bitcast(BF16)).then_inc(s("bitsT_ready"), 1)
            worth_of(0, cell("unit_in"))
            dve.wait_ge(s("bit_ps"), 1)
            nc.vector.tensor_scalar(g1[:, 0:2 * BIT], bank(6, 2 * BIT), cell("unit_in"), None, ALU.mult).then_inc(s("gated"), 1)
            expd, y = g1[:, 2 * BIT:3 * BIT], g1[:, 3 * BIT:4 * BIT]
            dve.wait_ge(s("gated"), 1)
            link(nc.vector.tensor_tensor(y, g1[:, 0:BIT], g1[:, BIT:2 * BIT], ALU.mult))
            dve.wait_ge(s("gate_exp"), 1)
            link(nc.vector.tensor_scalar(expd, expd, 1.0, None, ALU.add))
            link(nc.vector.reciprocal(expd, expd))
            link(nc.vector.tensor_tensor(y, y, expd, ALU.mult))
            bits_y = h2[:, 0:BIT // 2].bitcast(BF16)
            quantise(8, bits_y, y, row("g_out"), BIT, g1[:, 4 * BIT:5 * BIT])
            worth_of(1, cell("unit_out"))
            dve.wait_ge(s("bits_ps"), 3)
            nc.vector.tensor_copy(bitsT[0:BIT, 0:P], ps[0:BIT, 4 * WIN:4 * WIN + P // 2].bitcast(BF16)) \
                .then_inc(s("bitsT_ready"), 1)
            add_residual(6, 0, x, cell("unit_out"))

            normalise(9, xn, x, "xn_ready")
            part_T(7)
            for n, (lo, hi) in enumerate(HALVES):
                dve.wait_ge(s("mid_ps"), n + 1)
                nc.vector.tensor_scalar(g1[:, lo:hi], ps[:, 2 * WIN + lo:2 * WIN + hi], 0.0, None, ALU.max).then_inc(s("node_rows"), 1)
            part_T(8)
            dve.wait_ge(S["xb_ready"], 4)
            add_residual(7, 0, xb)

            whiten(10)
            nc.vector.tensor_scalar(xn[:], x[:], mv[:, 0:1], rstd[:], ALU.subtract, ALU.mult).then_inc(S["dve_step"], 1)
            used["dve_step"] += 1
            dve.wait_ge(s("rstd_ready"), 11)
            for lo, hi in ((0, D // 2), (D // 2, D)):
                nc.vector.tensor_scalar(g1[:, lo:hi], x[:, lo:hi], mv[:, 0:1], twice, ALU.subtract, ALU.mult) \
                    .then_inc(s("zhat_ready"), 1)
            affine_T("zhatT_ps", xT[:].rearrange("p c n -> p (c n)"), "r_ln", "xrT_ready")
            affine_T("zhatT_ps", g1, "ln1", "xaT_ready")

            def biased_T(dst, ps_at, bias):
                return nc.vector.tensor_tensor(dst.rearrange("p (c n) -> p c n", n=P),
                                               ps[:, ps_at:ps_at + D].rearrange("p (c n) -> p c n", n=P),
                                               bias.unsqueeze(2).broadcast_to([P, C, P]), ALU.add)

            dve.wait_ge(s("eT_ready"), 4)
            gmean = cell("router_mean", 4)
            link(nc.vector.tensor_reduce(gmean, h1[:, 0:512].rearrange("p (f n) -> p f n", n=P)[:, :, 1:P], AX.X, ALU.add))
            nc.vector.tensor_scalar(gmean, gmean, 1.0 / (P - 1), None, ALU.mult).then_inc(s("gmean_ready"), 1)
            dve.wait_ge(s("q_ps"), 1)
            biased_T(g2[:], 2 * WIN, col("bq")).then_inc(s("q_ready"), 1)
            dve.wait_ge(s("ro1g_ps"), 1)
            nc.vector.tensor_tensor(cell("ro1_bias", 4), bank(6, 4), col("r_o1_b"), ALU.add).then_inc(s("ro1_bias"), 1)
            dve.wait_ge(s("k_ps"), 1)
            biased_T(g3[:], 4 * WIN, col("bk")).then_inc(s("k_ready"), 1)
            dve.wait_ge(s("ro3_ps"), 1)
            lg, bit, nbit, sel = cell("router_logits", 4), cell("bits", 2), cell("not_bits", 2), cell("selected", 3)
            link(nc.vector.tensor_tensor(lg, bank(5, 4, 256), row("r_o3_b"), ALU.add))
            link(nc.vector.tensor_tensor(bit, lg[:, 1:4:2], lg[:, 0:4:2], ALU.is_gt))
            link(nc.vector.memset(bit[0:1, :], 1.0))
            link(nc.vector.tensor_scalar(nbit, bit, -1.0, 1.0, ALU.mult, ALU.add))
            link(nc.vector.tensor_tensor(sel[:, 0:1], nbit[:, 0:1], nbit[:, 1:2], ALU.mult))
            link(nc.vector.tensor_tensor(sel[:, 1:2], nbit[:, 0:1], bit[:, 1:2], ALU.mult))
            nc.vector.tensor_tensor(sel[:, 2:3], bit[:, 0:1], nbit[:, 1:2], ALU.mult).then_inc(s("router_done"), 1)
            negmax, total = cell("s_negmax", AH), cell("s_sum", AH)
            for g in range(3):
                dve.wait_ge(s("s_ps"), g + 1)
                m = negmax[:, 4 * g:4 * g + 4]
                sc = bank(g).rearrange("p (h n) -> p h n", n=P)
                if g == 2:
                    sc = ps[:, 2 * WIN:4 * WIN].rearrange("p (b h n) -> p b h n", b=2, n=P)[:, :, 0:2, :]
                link(nc.vector.tensor_reduce(m, sc, AX.X, ALU.max, negate=True))
                nc.vector.tensor_scalar(m, m, AD ** -0.5, None, ALU.mult).then_inc(s("smax"), 1)
            for g in range(3):
                dve.wait_ge(s("sexp"), 4 * g + 4)
                link(nc.vector.reciprocal(total[:, 4 * g:4 * g + 4], total[:, 4 * g:4 * g + 4]))
                v = h1[:, 512 * g:512 * g + 512].rearrange("p (h n) -> p h n", n=P)
                nc.vector.tensor_tensor(v, v, total[:, 4 * g:4 * g + 4].unsqueeze(2).broadcast_to([P, 4, P]), ALU.mult) \
                    .then_inc(s("p_ready"), 1)
            dve.wait_ge(s("v_ps"), 1)
            dve.wait_ge(s("in_bv"), 16)
            nc.vector.tensor_tensor(g4[:], ps[:, 6 * WIN:6 * WIN + D], avec[:, D:2 * D], ALU.add).then_inc(s("v_ready"), 1)
            dve.wait_ge(s("in_bo"), 16)
            link(nc.vector.scalar_tensor_tensor(out=g3[:], in0=avec[:, 0:D], scalar=bit[:, 0:1], in1=xn[:], op0=ALU.mult,
                                                op1=ALU.add))
            o_ps = ps[:, 0:AH * P].rearrange("p (c b n) -> p c b n", b=2, n=P)
            for n, (lo, hi) in enumerate(((0, 4), (4, C))):
                dve.wait_ge(s("oT_ps"), n + 1)
                nc.vector.tensor_copy(xT[AD:P, lo:hi, :], o_ps[AD:P, lo:hi, 1, :]).then_inc(s("o_odd_ready"), 1)
            for n, (lo, hi) in enumerate(HALVES):
                dve.wait_ge(s("wo_ps"), n + 1)
                link(nc.vector.scalar_tensor_tensor(out=g1[:, lo:hi], in0=ps[:, 4 * WIN + lo:4 * WIN + hi],
                                                    scalar=bit[:, 0:1], in1=g3[:, lo:hi], op0=ALU.mult, op1=ALU.add))
                statistics(n, g1)
            normalise(12, g4, g1, "hhat_ready")
            affine_T("hhatT_ps", g2, "ln2", "xfT_ready")
            for n, (lo, hi) in enumerate(HALVES):
                dve.wait_ge(s("fc2_ps"), n + 1)
                nc.vector.scalar_tensor_tensor(out=g3[:, lo:hi], in0=ps[:, lo:hi], scalar=bit[:, 1:2], in1=g1[:, lo:hi],
                                               op0=ALU.mult, op1=ALU.add).then_inc(s("out_rows"), 1)
            part_T(9)
            for k in range(3):
                if k != 1:
                    dve.wait_ge(s("rank_ps"), 1 + k // 2)
                last = nc.vector.tensor_scalar(g4[:, 256 * k:256 * k + 256], ps[:, 2 * WIN + 256 * k:2 * WIN + 256 * k + 256],
                                               sel[:, k:k + 1], None, ALU.mult)
                last.then_inc(s("rank_rows"), 1)
            part_T(10)
            dve.wait_ge(S["xb_ready"], 5)
            for n, (lo, hi) in enumerate(HALVES):
                dve.wait_ge(s("final_ps"), n + 1)
                nc.vector.tensor_tensor(xb[:, lo:hi], ps[:, lo:hi], xb[:, lo:hi], ALU.add).then_inc(s("result_ready"), 1)

        @block.tensor
        def _(pe):
            mm, tr = nc.tensor.matmul, nc.tensor.transpose

            def stay_warm(n, spare=7):
                some = shiftm[:].bitcast(BF16)
                for _ in range(n):
                    mm(bank(spare), some[:, 0:P], some[:, 0:WIN], start=True, stop=True)

            def T_at(c):
                return bank(4 + c // 2, P, c % 2 * P)

            def transpose_rows(src, name, before):
                for c in range(C):
                    if c in before:
                        pe.wait_ge(s(name), before[c])
                    last = tr(T_at(c), src[:, c * P:(c + 1) * P], ident)
                    if c % 2:
                        last.then_inc(s("T_ps"), 1)

            def aggregate(src, adjT, name, before):
                for c in range(C):
                    if c in before:
                        pe.wait_ge(s(name), before[c])
                    last = mm(T_at(c), src[:, c * P:(c + 1) * P], adjT[:], start=True, stop=True)
                    if c % 2:
                        last.then_inc(s("T_ps"), 1)

            def transpose_hats(src, name, signal):
                for c in range(C):
                    if c % 3 == 0:
                        pe.wait_ge(s(name), 1 + c // 3)
                    last = tr(hat_at(c), src[:, c * P:(c + 1) * P], ident)
                    if c != 0 and c != 2:
                        last.then_inc(s(signal), 1)

            def in_halves(k):
                return {0: 2 * k - 1, 3: 2 * k}

            def wait_T(k, c):
                if c in (0, 4):
                    pe.wait_ge(s("T_outer_ready"), 2 * k - 1 + c // 4)
                if c == 2:
                    pe.wait_ge(s("T_inner_ready"), k)

            def product(k, u, name, at, signal, biased=False):
                wait_unit(pe, u)
                w = unit(u, name, "p (c n) -> p c n", c=C)
                for lo, hi in HALVES:
                    for c in range(C):
                        if lo == 0:
                            wait_T(k, c)
                        last = mm(ps[:, at + lo:at + hi], xT[:, c, :], w[:, c, lo:hi], start=(c == 0 and not biased),
                                  stop=(c == C - 1))
                    last.then_inc(s(signal), 1)

            def head_product(n, par, in_value, after_first=None, halfway=None):
                pe.wait_ge(S[f"w1_in{par}"], in_value)
                if not isinstance(n, int) or n >= 2:
                    pe.wait_ge(S["h_rows"], n - 1)
                w = ring[:, par, :].rearrange("p (c n) -> p c n", c=C)
                at = 0 if par == 0 else WIN + 256
                parts = ((0, WIN), (WIN, D)) if par == 0 else ((256, D), (0, 256))
                for lo, hi in parts:
                    if lo != parts[0][0]:
                        if after_first is not None:
                            after_first()
                        wait(pe, "h_rows", n)
                    for c in range(C):
                        if c == 3 and lo == parts[0][0] and halfway is not None:
                            halfway()
                        last = mm(ps[:, at + lo:at + hi], xT[:, c, :], w[:, c, lo:hi], start=(c == 0), stop=(c == C - 1))
                return last

            def score_row(h, par):
                wait(pe, "alpha_ready", h + 1)
                wait(pe, "score_sum", h)
                wait(pe, "z_ready", h)
                mm(bank(7, P, 256), alpha[:, par, 0:1].broadcast_to([P, P]), ident, start=True, stop=True) \
                    .then_inc(s("score_row_ps"), 1)

            def turn_attention(h):
                wait(pe, "attn_ready", h + 1)
                wait(pe, "attnT_ready", h)
                tr(bank(7, P, 384), att[:, 1, :], ident).then_inc(S["attnT_ps"], 1)

            def aggregate_head(h, par):
                wait(pe, "attnT_ready", h + 1)
                wait(pe, "h_rows", h + 1)
                wait(pe, "z_ready", h)
                for c in range(C):
                    last = mm(ps[:, 6 * WIN + c * P:6 * WIN + (c + 1) * P], h1[:, par * D + c * P:par * D + (c + 1) * P],
                              attnT[:, par, :], start=True, stop=True)
                last.then_inc(S["agg_ready"], 1)

            def head_second(n, par, in_value, chunks=range(C)):
                if 0 in chunks:
                    pe.wait_ge(S[f"w2_in{par}"], in_value)
                    wait(pe, "elu_ready", n + 1)
                w = ring[:, 2 + par, :].rearrange("p (c n) -> p c n", c=C)
                for c in chunks:
                    for lo, hi in HALVES:
                        last = mm(ps[:, 4 * WIN + lo:4 * WIN + hi], h2[:, par * D + c * P:par * D + (c + 1) * P],
                                  w[:, c, lo:hi], start=False, stop=False)
                return last

            def sum_edges(es):
                for e in es:
                    last = mm(bank(3, 3 * P, P), oh_dst[:, e, :], oh_src[:, 1:4, e, :], start=(e == 0), stop=(e == EC - 1))
                return last

            def turn_adjacency(n, adjT):
                pe.wait_ge(s("adj_half"), n + 1)
                tr(bank(3, P), adjT[:], ident).then_inc(s("adj_ps"), 1)

            def step(h, par, w1_value, w2_value):
                score_row(h, par)
                head_product(h + 1, 1 - par, w1_value, lambda: turn_attention(h)).then_inc(S["hprod"], 1)
                aggregate_head(h, par)
                head_second(h - 1, 1 - par, w2_value).then_inc(S["w2_used"], 1)

            pe.wait_ge(s("constants"), 1)
            stay_warm(7)
            transpose_rows(xn, "xn_ready", in_halves(1))
            w = ring[:, 0, :].rearrange("p (c n) -> p c n", c=C)
            pe.wait_ge(S["w1_first_in"], 16)
            for c in range(C):
                wait_T(1, c)
                if c == C // 2:
                    pe.wait_ge(S["w1_in0"], 16)
                for lo, hi in HALVES:
                    last = mm(ps[:, lo:hi], xT[:, c, :], w[:, c, lo:hi], start=(c == 0), stop=(c == C - 1))
            last.then_inc(S["hprod"], 1)
            pe.wait_ge(s("constants"), 5)
            for lo, hi in HALVES:
                mm(ps[:, 4 * WIN + lo:4 * WIN + hi], zrow[:], zrow[:, 0:1].broadcast_to([1, hi - lo]), start=True, stop=False)
            pe.wait_ge(s("onehots"), 2)
            for e in range(EC):
                last = mm(bank(3, P), oh_dst[:, e, :], oh_src[:, 0, e, :], start=(e == 0), stop=(e == EC - 1))
            last.then_inc(s("counted"), 1)
            score_row(0, 0)
            head_product(1, 1, 16, lambda: turn_attention(0)).then_inc(S["hprod"], 1)
            aggregate_head(0, 0)
            head_product(2, 0, 32, lambda: turn_attention(1), lambda: score_row(1, 1)).then_inc(S["hprod"], 1)
            aggregate_head(1, 1)
            head_second(0, 0, 16).then_inc(S["w2_used"], 1)
            step(2, 0, 32, 16)
            turn_adjacency(0, adj1T)
            with pe.Fori(1, 3) as i:
                step(2 * i + 1, 1, 16 * i + 32, 16 * i + 16)
                step(2 * i + 2, 0, 16 * i + 32, 16 * i + 16)
            score_row(7, 1)
            head_second(6, 0, 64, range(0, 3))
            turn_attention(7)
            head_second(6, 0, 64, range(3, 4))
            aggregate_head(7, 1)
            head_second(6, 0, 64, range(4, C)).then_inc(S["w2_used"], 1)
            pe.wait_ge(s("ew_rows"), 3)
            sum_edges(range(0, 10))
            pe.wait_ge(S["w2_in1"], 64)
            wait(pe, "elu_ready", 8)
            w = ring[:, 3, :].rearrange("p (c n) -> p c n", c=C)
            for (lo, hi), signal in zip(HALVES, ("gat2_first", "hprod")):
                for c in range(C):
                    last = mm(ps[:, 4 * WIN + lo:4 * WIN + hi], h2[:, D + c * P:D + (c + 1) * P], w[:, c, lo:hi],
                              start=False, stop=(c == C - 1))
                last.then_inc(s(signal), 1)
            sum_edges(range(10, 25))
            score_row(8, 0)
            sum_edges(range(25, EC)).then_inc(s("edges_summed"), 1)
            turn_attention(8)
            wait(pe, "attnT_ready", 9)
            wait(pe, "h_rows", 9)
            for lo, hi in HALVES:
                mm(ps[:, lo:hi], attnT[:, 0, :], h1[:, lo:hi], start=True, stop=True).then_inc(s("rows_ps"), 1)
            wait(pe, "attnT_ready", 9)
            stay_warm(15)
            transpose_rows(xn, "xn_ready", in_halves(2))
            for c in range(C):
                wait_T(2, c)
                last = mm(bank(7, E0 + 1), xT[:, c, :], gatew[:, c * (E0 + 1):(c + 1) * (E0 + 1)],
                          start=(c == 0), stop=(c == C - 1))
            last.then_inc(s("gate_ps"), 1)
            turn_adjacency(1, adj2T)

            def shift_green(lv):
                pe.wait_ge(s("green_state"), lv + 1)
                for d, off in enumerate((P - 2 ** lv, P + 2 ** lv)):
                    last = mm(bank(7, 16, 16 * d), shiftm[:, off:off + P], state[:, 16 * d:16 * d + 16], start=True, stop=True)
                last.then_inc(s("shifted"), 1)

            wait_unit(pe, U_L0)
            w = unit(U_L0, "l0_w1", "p (c n) -> p c n", c=C)
            for c in range(C):
                last = mm(bank(0, H0), xT[:, c, :], w[:, c, :], start=(c == 0), stop=(c == C - 1))
                if c == C - 1:
                    last.then_inc(s("hid0_mm"), 1)
                if c in (0, 2, 4):
                    shift_green(c // 2)
            stay_warm(2, 1)
            shift_green(3)
            pe.wait_ge(s("hid0_scaled"), 1)
            for c in range(3):
                last = tr(ps[:, 4 * WIN + c * P:4 * WIN + (c + 1) * P], h1[:, c * P:(c + 1) * P], ident)
            last.then_inc(s("hid0_ps"), 1)
            shift_green(4)
            stay_warm(1, 1)
            pe.wait_ge(s("adj_ready"), 2)
            pe.wait_ge(s("hid0T"), 1)
            w = unit(U_L0, "l0_w2", "p (c n) -> p c n", c=3)
            for c in range(3):
                for lo, hi in HALVES:
                    last = mm(ps[:, 2 * WIN + lo:2 * WIN + hi], h1[:, H0 + c * P:H0 + (c + 1) * P], w[:, c, lo:hi],
                              start=(c == 0), stop=False)
                    if c == 0:
                        shift_green(5 if lo == 0 else 6)
            last.then_inc(s("l0_weights_used"), 1)
            stay_warm(7, 0)
            pe.wait_ge(s("comb_ready"), 1)
            tr(bank(7, P, 0, 11), comb[:, 0:11], ident).then_inc(s("combT_ps"), 1)
            pe.wait_ge(s("combT_ready"), 1)
            pe.wait_ge(s("tail_ready"), 1)
            for lo, hi in HALVES:
                mm(ps[:, 2 * WIN + lo:2 * WIN + hi], combT[0:11, :], g3[0:11, lo:hi], start=False, stop=True) \
                    .then_inc(s("rows_ps"), 1)

            pe.wait_ge(s("adj_ready"), 2)
            stay_warm(11)
            aggregate(xn, adj1T, "xn_ready", in_halves(3))
            product(3, U_L1, "l1_w", 0, "rows_ps")

            stay_warm(8)
            transpose_rows(xn, "xn_ready", in_halves(4))
            n36 = G1N + G1N * E1N
            for c in range(C):
                wait_T(4, c)
                last = mm(bank(7, n36), xT[:, c, :], gatew1[:, c * n36:(c + 1) * n36], start=(c == 0), stop=(c == C - 1))
            last.then_inc(s("gate_ps"), 1)

            def hidden(g):
                u, name = ((U_L1W1A, "l1f_w1a"), (U_L1W1B, "l1f_w1b"))[g // 2]
                wait_unit(pe, u)
                weights = unit(u, name, "p (c n) -> p c n", c=C)
                lo = (g % 2) * H0
                for c in range(C):
                    last_ = mm(bank(g, H0), xT[:, c, :], weights[:, c, lo:lo + H0], start=(c == 0), stop=(c == C - 1))
                last_.then_inc(s("hid1_mm"), 1)

            def turn_hidden(g):
                pe.wait_ge(s("hid1_scaled"), g + 1)
                if g >= 2:
                    pe.wait_ge(s("hid1T"), g - 1)
                for c in range(3):
                    last_ = tr(bank(4 + g % 2, P, c * P), h1[:, g * H0 + c * P:g * H0 + (c + 1) * P], ident)
                last_.then_inc(s("hid1_ps"), 1)

            def hidden_out(g):
                u, name = ((U_L1W2A, "l1f_w2a"), (U_L1W2B, "l1f_w2b"))[g // 2]
                wait_unit(pe, u)
                pe.wait_ge(s("hid1T"), g + 1)
                weights = unit(u, name, "p (c n) -> p c n", c=C)
                for lo, hi in HALVES:
                    for c in range(3):
                        last_ = mm(ps[:, lo:hi], h2[:, g * H0 + c * P:g * H0 + (c + 1) * P],
                                   weights[:, 3 * (g % 2) + c, lo:hi], start=False, stop=(g == 3 and c == 2))
                    if g == 3:
                        last_.then_inc(s("rows_ps"), 1)
                return last_

            hidden(0)
            hidden(1)
            pe.wait_ge(s("comb_ready"), 2)
            tr(bank(7, P, 0, 32), comb[:, 0:32], ident).then_inc(s("combT_ps"), 1)
            hidden(2)
            turn_hidden(0)
            hidden(3)
            turn_hidden(1)
            pe.wait_ge(s("combT_ready"), 2)
            pe.wait_ge(s("in_b2"), 16)
            for lo, hi in HALVES:
                mm(ps[:, lo:hi], combT[:], g1[0:32, lo:hi], start=True, stop=False)
            hidden_out(0)
            turn_hidden(2)
            pe.wait_ge(s("wsum_ready"), 2)
            pe.wait_ge(s("constants"), 4)
            mm(bank(7, 1, P), ones[:], cell("w_abs", 2)[:, 0:1], start=True, stop=True)
            mm(bank(7, 1, P + 1), ones[0:BIT, :], cell("w_abs", 2)[0:BIT, 1:2], start=True, stop=True) \
                .then_inc(s("wsum_ps"), 1)
            hidden_out(1).then_inc(s("w2a_used"), 1)
            turn_hidden(3)
            hidden_out(2)
            hidden_out(3)

            pe.wait_ge(s("w_quantised"), 2)
            stay_warm(11)
            transpose_rows(xn, "xn_ready", in_halves(5))
            wait_unit(pe, U_L2)
            w = unit(U_L2, "l2_wd", "p (c n) -> p c n", c=C)
            for c in range(C):
                wait_T(5, c)
                last = mm(bank(7, P, 0, DOWN), w[:, c, :], xT[:, c, :], start=(c == 0), stop=(c == C - 1))
            last.then_inc(s("l2_ps"), 1)
            pe.wait_ge(s("l2_copied"), 1)
            w = unit(U_L2, "l2_wu")
            for lo, hi in HALVES:
                mm(ps[:, lo:hi], zT[0:DOWN + 1, :], w[:, lo:hi], start=True, stop=True).then_inc(s("l2_ps"), 1)
            mm(bank(7, HID2), ones[0:1, :], row("l2_b1")[0:1, :], start=True, stop=False)
            aggregate(g1, adj2T, "node_rows", {0: 1, 4: 2})
            w = unit(U_L2, "l2_w1", "p (c n) -> p c n", c=C)
            for c in range(C):
                wait_T(6, c)
                last = mm(bank(7, HID2), xT[:, c, :], w[:, c, :], start=False, stop=(c == C - 1))
            last.then_inc(s("l2_ps"), 1)
            pe.wait_ge(s("node_rows"), 3)
            for c in range(2):
                last = mm(bank(2, P, c * P), g2[:, c * P:(c + 1) * P], adj2T[:], start=True, stop=True)
            last.then_inc(s("l2_ps"), 1)
            pe.wait_ge(s("l2_copied"), 2)
            w = unit(U_L2, "l2_w2", "p (c n) -> p c n", c=2)
            for lo, hi in HALVES:
                for c in range(2):
                    last = mm(ps[:, lo:hi], g3[:, c * P:(c + 1) * P], w[:, c, lo:hi], start=(c == 0), stop=(c == 1))
                last.then_inc(s("rows_ps"), 1)

            pe.wait_ge(s("in_l3_b1"), 16)
            for lo, hi in HALVES:
                mm(ps[:, 2 * WIN + lo:2 * WIN + hi], ones[0:1, :], avec[0:1, lo:hi], start=True, stop=False)

            pe.wait_ge(s("constants"), 2)
            for c in range(C):
                if c % 3 == 0:
                    pe.wait_ge(s("bits_ready"), 1 + c // 3)
                last = tr(bank(4 + c // 3, P // 2, c % 3 * P // 2).bitcast(BF16), bits[:, c * P:(c + 1) * P], identb[:])
                if c % 3 == 2:
                    last.then_inc(s("bits_ps"), 1)
            pe.wait_ge(s("bitsT_ready"), 2)
            for c in range(C):
                last = mm(bank(6, 2 * BIT), bitsT[:, c * P:(c + 1) * P], w_in_q[:, c * 2 * BIT:(c + 1) * 2 * BIT],
                          start=(c == 0), stop=(c == C - 1))
            last.then_inc(s("bit_ps"), 1)
            pe.wait_ge(s("bits_ready"), 3)
            tr(ps[0:BIT, 4 * WIN:4 * WIN + P // 2].bitcast(BF16), h2[:, 0:BIT // 2].bitcast(BF16), identb[:]) \
                .then_inc(s("bits_ps"), 1)
            pe.wait_ge(s("bitsT_ready"), 3)
            for lo, hi in HALVES:
                mm(ps[:, lo:hi], bitsT[0:BIT, 0:P], w_out_q[:, lo:hi], start=True, stop=True).then_inc(s("rows_ps"), 1)

            stay_warm(13)
            aggregate(xn, adj1T, "xn_ready", in_halves(6))
            product(7, U_L3A, "l3_w1", 2 * WIN, "mid_ps", biased=True)
            aggregate(g1, adj1T, "node_rows", {0: 4, 4: 5})
            product(8, U_L3B, "l3_w2", 0, "rows_ps")

            def product_T(weights, first_bank, outs, operand, signal, emptied=None):
                chunks = weights.shape[1]
                for o in range(outs):
                    if emptied is not None and o >= 2:
                        pe.wait_ge(s(emptied), o - 1)
                    to = ps[:, first_bank * WIN + o * P:first_bank * WIN + (o + 1) * P]
                    if emptied is not None:
                        to = bank(first_bank + o % 2, P)
                    for c in range(chunks):
                        last_ = mm(to, weights[:, c, o * P:(o + 1) * P], operand(c), start=(c == 0), stop=(c == chunks - 1))
                    if emptied is not None or o == outs - 1:
                        last_.then_inc(s(signal), 1)

            stay_warm(12)
            transpose_hats(g1, "zhat_ready", "zhatT_ps")
            wait_unit(pe, U_RIN)
            pe.wait_ge(s("xrT_ready"), 2)
            product_T(unit(U_RIN, "r_in", "p (c n) -> p c n", c=C), 0, 4, lambda c: xT[:, c, :], "rin_ps", emptied="eT_ready")
            wait_unit(pe, U_Q)
            pe.wait_ge(s("xaT_ready"), 2)
            product_T(unit(U_Q, "wq", "p (c n) -> p c n", c=C), 2, C, lambda c: g1[:, c * P:(c + 1) * P], "q_ps")
            wait_unit(pe, U_RO1)
            pe.wait_ge(s("gmean_ready"), 1)
            w = unit(U_RO1, "r_o1", "p (c n) -> p c n", c=8)
            for f in range(4):
                for c in range(4):
                    last = mm(bank(6, 1, f), w[:, 4 + c, f * P:(f + 1) * P], cell("router_mean", 4)[:, c:c + 1],
                              start=(c == 0), stop=(c == 3))
            last.then_inc(s("ro1g_ps"), 1)
            pe.wait_ge(s("ro1_bias"), 1)
            product_T(w[:, 0:4, :], 6, 4, lambda c: h1[:, c * P:(c + 1) * P], "ro1_ps", emptied="h1T_ready")
            wait_unit(pe, U_K)
            product_T(unit(U_K, "wk", "p (c n) -> p c n", c=C), 4, C, lambda c: g1[:, c * P:(c + 1) * P], "k_ps")
            pe.wait_ge(s("h1T_ready"), 4)
            product_T(unit(U_RIN, "r_o2", "p (c n) -> p c n", c=4), 0, 2,
                      lambda c: h1[:, 512 + c * P:512 + (c + 1) * P], "ro2_ps", emptied="h2T_ready")
            def scores():
                pe.wait_ge(s("h2T_ready"), 2)
                w3 = unit(U_RIN, "r_o3", "p (c n) -> p c n", c=2)
                for c in range(2):
                    last = mm(bank(5, 4, 256), h1[:, 1024 + c * P:1024 + (c + 1) * P], w3[:, c, :], start=(c == 0), stop=(c == 1))
                last.then_inc(s("ro3_ps"), 1)
                pe.wait_ge(s("q_ready"), 1)
                for h in range(AH):
                    r0, c = (h % 2) * AD, h // 2
                    last = mm(score_ps(POSITION[h]), g2[r0:r0 + AD, c * P:(c + 1) * P], g3[r0:r0 + AD, c * P:(c + 1) * P],
                              start=True, stop=True)
                    if h in (6, 7, 11):
                        last.then_inc(s("s_ps"), 1)

            wait_unit(pe, U_V)
            pe.wait_ge(s("k_ready"), 1)
            w = unit(U_V, "wv", "p (c n) -> p c n", c=C)
            for lo, hi in HALVES:
                for c in range(C):
                    last = mm(ps[:, 6 * WIN + lo:6 * WIN + hi], g1[:, c * P:(c + 1) * P], w[:, c, lo:hi],
                              start=(c == 0), stop=(c == C - 1))
                    if lo == 0 and c == 0:
                        scores()
            last.then_inc(s("v_ps"), 1)
            pT_banks = (4, 5, 3)
            for g in range(3):
                pe.wait_ge(s("p_ready"), g + 1)
                for h in range(4):
                    last = tr(bank(pT_banks[g], P, h * P), h1[:, (4 * g + h) * P:(4 * g + h + 1) * P], ident)
                last.then_inc(s("pT_ps"), 1)
            pe.wait_ge(s("v_ready"), 1)
            for at in range(AH):
                h = POSITION.index(at)
                if at % 4 == 0:
                    pe.wait_ge(s("pT_ready"), at // 4 + 1)
                last = mm(ps[:, h * P:(h + 1) * P], g4[:, (h // 2) * P:(h // 2 + 1) * P], h2[:, at * P:(at + 1) * P],
                          start=True, stop=True)
                if at in (7, 11):
                    last.then_inc(s("oT_ps"), 1)
            wait_unit(pe, U_O)
            w = unit(U_O, "wo", "p (c n) -> p c n", c=C)
            for lo, hi in HALVES:
                for c in range(C):
                    if lo == 0 and c in (0, 4):
                        pe.wait_ge(s("o_even_ready"), 1 + c // 4)
                        pe.wait_ge(s("o_odd_ready"), 1 + c // 4)
                    last = mm(ps[:, 4 * WIN + lo:4 * WIN + hi], xT[:, c, :], w[:, c, lo:hi], start=(c == 0), stop=(c == C - 1))
                last.then_inc(s("wo_ps"), 1)
            stay_warm(11)
            transpose_hats(g4, "hhat_ready", "hhatT_ps")
            pe.wait_ge(s("xfT_ready"), 2)
            w = unit(U_RO1, "fc1", "p (c n) -> p c n", c=C)
            for c in range(C):
                last = mm(bank(3, P, 0, MLP), w[:, c, :], g2[:, c * P:(c + 1) * P], start=(c == 0), stop=(c == C - 1))
            last.then_inc(s("fc1_ps"), 1)
            pe.wait_ge(s("fc1_ready"), 1)
            pe.wait_ge(s("in_fc2"), 16)
            for lo, hi in HALVES:
                mm(ps[:, lo:hi], zT[0:MLP + 1, :], row0[0:MLP + 1, lo:hi], start=True, stop=True).then_inc(s("fc2_ps"), 1)
            transpose_rows(g3, "out_rows", {0: 1, 4: 2})
            product(9, U_DOWN, "down", 2 * WIN, "rank_ps")
            transpose_rows(g4, "rank_rows", {0: 1, 2: 2, 4: 3})
            product(10, U_UP, "up", 0, "final_ps")


def chunked(np, w):
    k, n = w.shape
    return np.ascontiguousarray(w.reshape(k // P, P, n).transpose(1, 0, 2).reshape(P, k // P * n))


def lay_out(np, i):
    a = {"x": i["x"], "edge_weight": i["edge_weight"].reshape(P, EC)}
    a["src"], a["dst"] = i["src"].reshape(P, EC), i["dst"].reshape(P, EC)
    a["gat_w1"] = i["L0_gnn_W1"].reshape(C, P, HEADS1, D).transpose(2, 1, 0, 3).reshape(HEADS1, P, UNIT)
    a["gat_w2"] = i["L0_gnn_W2"].reshape(HEADS1, C, P, D).transpose(0, 2, 1, 3).reshape(HEADS1, P, UNIT)
    a["gat_a"] = np.concatenate([np.concatenate([i["L0_gnn_a_src1"], i["L0_gnn_a_src2"]]),
                                 np.concatenate([i["L0_gnn_a_dst1"], i["L0_gnn_a_dst2"]])], axis=1)
    a["gat_b2"] = i["L0_gnn_b2"]
    a["gatew"] = chunked(np, np.concatenate([i["L0_ffn_gate_w"], i["L0_ffn_v_w"][:, None]], axis=1))
    a["l0_w1"] = chunked(np, i["L0_ffn_w1"].transpose(1, 0, 2).reshape(D, H0))
    a["l0_w2"] = chunked(np, i["L0_ffn_w2"].reshape(H0, D))
    a["l0_tail"] = np.concatenate([i["L0_ffn_b2"], i["L0_ffn_out_w"], i["L0_ffn_out_b"][None]])
    a["bk_scale"] = i["L0_ffn_bk_scale"]
    a["l1_w"] = chunked(np, i["L1_gnn_W"])
    a["l1_b"] = i["L1_gnn_b"]
    a["gatew1"] = chunked(np, np.concatenate([i["L1_ffn_Wg"], i["L1_ffn_Wge"].transpose(1, 0, 2).reshape(D, G1N * E1N)],
                                             axis=1))
    w1 = i["L1_ffn_W1"].transpose(1, 0, 2).reshape(D, H1N)
    a["l1f_w1a"], a["l1f_w1b"] = chunked(np, w1[:, :D]), chunked(np, w1[:, D:])
    w2 = i["L1_ffn_W2"].reshape(H1N, D)
    a["l1f_w2a"], a["l1f_w2b"] = chunked(np, w2[:D]), chunked(np, w2[D:])
    a["l1_b1"] = i["L1_ffn_b1"].reshape(H1N)
    a["l1_b2"] = i["L1_ffn_b2"]
    a["l2_w1"], a["l2_w2"] = chunked(np, i["L2_gnn_W1"]), chunked(np, i["L2_gnn_W2"])
    a["l2_wd"] = chunked(np, i["L2_gnn_Wd"])
    a["l2_wu"] = np.concatenate([i["L2_gnn_Wu"], i["L2_gnn_bu"][None]])
    a["l2_b2"] = i["L2_gnn_b2"]
    a["l2_win"] = chunked(np, i["L2_ffn_w_in"].T)
    a["l2_wout"] = i["L2_ffn_w_out"].T
    a["g_in"] = i["L2_ffn_g_in"]
    a["l3_w1"], a["l3_w2"] = chunked(np, i["L3_gnn_W1"]), chunked(np, i["L3_gnn_W2"])
    a["l3_b1"], a["l3_b2"] = i["L3_gnn_b1"], i["L3_gnn_b2"]
    for name in ("wq", "wk", "wv", "wo"):
        a[name] = chunked(np, i["L3_ffn_" + name].T)
    a["bv"], a["bo"] = i["L3_ffn_bv"], i["L3_ffn_bo"]
    a["r_in"], a["r_o1"] = chunked(np, i["L3_ffn_r_in_w"].T), chunked(np, i["L3_ffn_r_o1_w"].T)
    a["r_o2"], a["r_o3"] = chunked(np, i["L3_ffn_r_o2_w"].T), chunked(np, i["L3_ffn_r_o3_w"].T)
    a["fc1"] = chunked(np, i["L3_ffn_fc1_w"].T)
    a["fc2"] = np.concatenate([i["L3_ffn_fc2_w"].T, i["L3_ffn_fc2_b"][None]])
    a["down"] = chunked(np, i["L3_ffn_lra_down"].reshape(D, D).T)
    a["up"] = chunked(np, i["L3_ffn_lra_up"].transpose(0, 2, 1).reshape(D, D))
    a["bd"], a["fc1_b"] = i["L2_gnn_bd"].reshape(DOWN, 1), i["L3_ffn_fc1_b"].reshape(MLP, 1)
    vectors = [i["L0_gnn_b1"]] + [i["L3_ffn_" + n] for n in ("bq", "bk", "ln1_g", "ln1_b", "r_ln_g", "r_ln_b", "ln2_g",
                                                           "ln2_b", "r_in_b", "r_o1_b", "r_o2_b")]
    a["cols"] = np.concatenate(vectors).reshape(NCOLS, P).T
    a["rows"] = np.concatenate([i["L0_ffn_b1"].reshape(-1), i["L2_gnn_b1"], i["L0_ffn_gate_b"], i["L0_ffn_v_b"].reshape(1),
                                i["L1_ffn_bg"], i["L1_ffn_bge"].reshape(-1), i["L2_ffn_g_out"], i["L3_ffn_r_o3_b"]])
    return {n: np.ascontiguousarray(v) for n, v in a.items()}


def kernel(**inputs):
    import numpy as np
    import concourse.bacc as bacc
    from concourse.bass_utils import run_bass_kernel_spmd

    arrays = lay_out(np, {n: np.asarray(v) for n, v in inputs.items()})
    nc = bacc.Bacc("TRN2", target_bir_lowering=False, num_devices=1)
    a = {n: nc.dram_tensor("in_" + n, v.shape, mybir.dt.from_np(v.dtype), kind="ExternalInput").ap()
         for n, v in arrays.items()}
    out = nc.dram_tensor("out_x", (P, D), F32, kind="ExternalOutput").ap()
    build(nc, a, out)
    r = run_bass_kernel_spmd(nc, [{"in_" + n: v for n, v in arrays.items()}], core_ids=[0])
    return r.results[0]["out_x"]
```
